# Optimizing a Trainium2 kernel written in Bass

```python
import numpy as np
import jax
import jax.numpy as jnp

def _softmax(x, axis=-1):
    return jax.nn.softmax(x, axis=axis)

def _gelu(x):
    return jax.nn.gelu(x, approximate=True)

def _silu(x):
    return jax.nn.silu(x)

def _sigmoid(x):
    return jax.nn.sigmoid(x)

def _layernorm(x, axis=-1, eps=1e-05):
    m = jnp.mean(x, axis=axis, keepdims=True)
    v = jnp.var(x, axis=axis, keepdims=True)
    return (x - m) / jnp.sqrt(v + eps)

def _scatter_add(tgt, idx, src, axis=0):
    return tgt.at[idx].add(src)

def _segment_sum(src, seg, n):
    return jax.ops.segment_sum(src, seg, n)
kernel_name = 'mk_decoder_preln_d1_seqx_r4_195fe3'

def setup_inputs(seed: int=0):
    np.random.seed(seed)
    _w = jnp.asarray

    def _rec_inputs():
        import jax
        import jax.numpy as jnp
        _rk = jax.random.key(seed)
        x = -0.000125 + 0.9999 * jax.random.normal(jax.random.fold_in(_rk, 1), (16, 128, 1024), jnp.float32)
        _lenS = 128 - jax.random.randint(jax.random.fold_in(_rk, 7), (16,), 0, max(1, 128 // 4) + 1, jnp.int32)
        _lenS2 = 128 - jax.random.randint(jax.random.fold_in(_rk, 8), (16,), 0, max(1, 128 // 4) + 1, jnp.int32)
        _ctx_4096P = jax.random.normal(jax.random.fold_in(_rk, 11), (16, 16, 1024), jnp.float32)
        _ctx_4096c = jax.random.dirichlet(jax.random.fold_in(_rk, 511), 0.3 * jnp.ones((16,), jnp.float32), (16, 128))
        _ctx_4096t = jnp.einsum('bsk,bkd->bsd', _ctx_4096c, _ctx_4096P)
        _ctx_4096t = _ctx_4096t * jax.lax.rsqrt(jnp.mean(jnp.square(_ctx_4096t)) + 1e-12) * 0.953939
        ctx_4096 = -1.52775e-05 + 0.999936 * (_ctx_4096t + 0.3 * jax.random.normal(jax.random.fold_in(_rk, 611), (16, 128, 1024), jnp.float32))
        return (x, ctx_4096)
    x, ctx_4096 = _rec_inputs()

    def _L0_attn_setup():
        import jax, jax.numpy as jnp
        import numpy as np
        import math
        B, T, D_IN, D_OUT = (2, 512, 1024, 1024)
        N_HEADS, N_KV = (32, 8)
        HEAD_DIM = D_OUT // N_HEADS
        GROUP_SIZE = N_HEADS // N_KV
        ROPE_BASE = 500000.0
        CTX = 512

        def _rope_tables(head_dim, base, seq_len):
            inv_freq = 1.0 / base ** (jnp.arange(0, head_dim, 2, dtype=jnp.float32) / head_dim)
            t = jnp.arange(seq_len, dtype=jnp.float32)
            freqs = jnp.einsum('i,j->ij', t, inv_freq)
            return (jnp.cos(freqs), jnp.sin(freqs))

        def _apply_rope(x, cos, sin):
            x1, x2 = jnp.split(x, 2, axis=-1)
            c = cos[None, None]
            s = sin[None, None]
            return jnp.concatenate([x1 * c - x2 * s, x1 * s + x2 * c], axis=-1)
        key = jax.random.key(seed)
        ks = jax.random.split(key, 5)
        scale = 0.02
        return {'x': jax.random.normal(ks[0], (B, T, D_IN), dtype=jnp.float32), 'Wq': jax.random.normal(ks[1], (D_IN, D_OUT), dtype=jnp.float32) * scale, 'Wk': jax.random.normal(ks[2], (D_IN, N_KV * HEAD_DIM), dtype=jnp.float32) * scale, 'Wv': jax.random.normal(ks[3], (D_IN, N_KV * HEAD_DIM), dtype=jnp.float32) * scale, 'Wo': jax.random.normal(ks[4], (D_OUT, D_OUT), dtype=jnp.float32) * scale}
    _L0_attn_all = _L0_attn_setup()
    _L0_attn_in = {k: v for k, v in _L0_attn_all.items() if k in ('Wq', 'Wk', 'Wv', 'Wo')}
    del _L0_attn_all

    def _L0_xattn_setup():
        import jax, jax.numpy as jnp
        import numpy as np
        H = 8
        C = 2

        def _autocorrelation(Q, K, V):
            B, L, D = Q.shape
            d = D // H
            q = Q.reshape(B, L, H, d).transpose(0, 2, 1, 3)
            k = K.reshape(B, L, H, d).transpose(0, 2, 1, 3)
            v = V.reshape(B, L, H, d).transpose(0, 2, 1, 3)
            qf = jnp.fft.fft(q, axis=2)
            kf = jnp.fft.fft(k, axis=2)
            corr = jnp.fft.ifft(qf * jnp.conj(kf), axis=2).real
            topk = int(C * np.log(L))
            w, idx = jax.lax.top_k(corr.transpose(0, 1, 3, 2), topk)
            w = jax.nn.softmax(w, axis=-1)
            pos = jnp.arange(L)[:, None]
            out = jnp.zeros_like(v)
            for i in range(topk):
                g = jnp.minimum(idx[:, :, None, :, i] + pos, L - 1)
                out = out + w[:, :, None, :, i] * jnp.take_along_axis(v, g, axis=2)
            return out.transpose(0, 2, 1, 3).reshape(B, L, D)
        key = jax.random.key(seed)
        k1, k2, k3 = jax.random.split(key, 3)
        B, L, D = (16, 128, 1024)
        Q = jax.random.normal(k1, (B, L, D), dtype=jnp.float32)
        K = jax.random.normal(k2, (B, L, D), dtype=jnp.float32)
        V = jax.random.normal(k3, (B, L, D), dtype=jnp.float32)
        return {'Q': Q, 'K': K, 'V': V}
    _L0_xattn_all = _L0_xattn_setup()
    _L0_xattn_in = {k: v for k, v in _L0_xattn_all.items() if k in ()}
    del _L0_xattn_all

    def _L0_ffn_setup():
        import jax, jax.numpy as jnp
        import numpy as np
        N_STREAMS = 4
        DIM = 256
        SINKHORN_ITERS = 50
        SINKHORN_TAU = 0.1
        RMS_EPS = 1.1920929e-07

        def sinkhorn_log(logits, num_iters=SINKHORN_ITERS, tau=SINKHORN_TAU):
            Z = logits / tau
            u0 = jnp.zeros(Z.shape[:-1], Z.dtype)
            v0 = jnp.zeros_like(u0)

            def step(carry, _):
                u, v = carry
                u = -jax.nn.logsumexp(Z + v[..., None, :], axis=-1)
                v = -jax.nn.logsumexp(Z + u[..., :, None], axis=-2)
                return ((u, v), None)
            (u, v), _ = jax.lax.scan(step, (u0, v0), None, length=num_iters)
            return jnp.exp(Z + u[..., :, None] + v[..., None, :])
        key = jax.random.key(seed)
        ks = jax.random.split(key, 6)
        B, T = (4, 512)
        n, C = (N_STREAMS, DIM)
        wd = n * C
        x = jax.random.normal(ks[0], (B, T, wd), dtype=jnp.float32)
        W_res = 0.01 * jax.random.normal(ks[1], (n * n, wd), dtype=jnp.float32)
        W_pre = 0.01 * jax.random.normal(ks[2], (n, wd), dtype=jnp.float32)
        W_post = 0.01 * jax.random.normal(ks[3], (n, wd), dtype=jnp.float32)
        H_res_base = jnp.full((n, n), -0.5, dtype=jnp.float32)
        H_res_base = H_res_base.at[jnp.arange(n), jnp.arange(n)].set(0.0)
        H_pre_base = jnp.zeros((n,), dtype=jnp.float32).at[0].set(1.0)
        H_post_base = jnp.zeros((n,), dtype=jnp.float32)
        gate = jnp.array([5.0], dtype=jnp.float32)
        W_branch = 1.0 / np.sqrt(C) * jax.random.normal(ks[4], (C, C), dtype=jnp.float32)
        return {'x': x, 'W_res': W_res, 'W_pre': W_pre, 'W_post': W_post, 'H_res_base': H_res_base, 'H_pre_base': H_pre_base, 'H_post_base': H_post_base, 'gate': gate, 'W_branch': W_branch}
    _L0_ffn_all = _L0_ffn_setup()
    _L0_ffn_in = {k: v for k, v in _L0_ffn_all.items() if k in ('W_res', 'W_pre', 'W_post', 'H_res_base', 'H_pre_base', 'H_post_base', 'gate', 'W_branch')}
    del _L0_ffn_all
    return {'x': x, 'ctx_4096': ctx_4096, 'L0_attn_Wq': _L0_attn_in['Wq'], 'L0_attn_Wk': _L0_attn_in['Wk'], 'L0_attn_Wv': _L0_attn_in['Wv'], 'L0_attn_Wo': _L0_attn_in['Wo'], 'L0_ffn_W_res': _L0_ffn_in['W_res'], 'L0_ffn_W_pre': _L0_ffn_in['W_pre'], 'L0_ffn_W_post': _L0_ffn_in['W_post'], 'L0_ffn_H_res_base': _L0_ffn_in['H_res_base'], 'L0_ffn_H_pre_base': _L0_ffn_in['H_pre_base'], 'L0_ffn_H_post_base': _L0_ffn_in['H_post_base'], 'L0_ffn_gate': _L0_ffn_in['gate'], 'L0_ffn_W_branch': _L0_ffn_in['W_branch']}

def reference(x, ctx_4096, L0_attn_Wq, L0_attn_Wk, L0_attn_Wv, L0_attn_Wo, L0_ffn_W_res, L0_ffn_W_pre, L0_ffn_W_post, L0_ffn_H_res_base, L0_ffn_H_pre_base, L0_ffn_H_post_base, L0_ffn_gate, L0_ffn_W_branch):
    import jax
    import jax.numpy as jnp

    def _L0_attn_ref(x, Wq, Wk, Wv, Wo):
        import jax, jax.numpy as jnp
        import numpy as np
        import math
        B, T, D_IN, D_OUT = (2, 512, 1024, 1024)
        N_HEADS, N_KV = (32, 8)
        HEAD_DIM = D_OUT // N_HEADS
        GROUP_SIZE = N_HEADS // N_KV
        ROPE_BASE = 500000.0
        CTX = 512

        def _rope_tables(head_dim, base, seq_len):
            inv_freq = 1.0 / base ** (jnp.arange(0, head_dim, 2, dtype=jnp.float32) / head_dim)
            t = jnp.arange(seq_len, dtype=jnp.float32)
            freqs = jnp.einsum('i,j->ij', t, inv_freq)
            return (jnp.cos(freqs), jnp.sin(freqs))

        def _apply_rope(x, cos, sin):
            x1, x2 = jnp.split(x, 2, axis=-1)
            c = cos[None, None]
            s = sin[None, None]
            return jnp.concatenate([x1 * c - x2 * s, x1 * s + x2 * c], axis=-1)
        b, t, _ = x.shape
        cos, sin = _rope_tables(HEAD_DIM, ROPE_BASE, t)
        q = (x @ Wq).reshape(b, t, N_HEADS, HEAD_DIM).transpose(0, 2, 1, 3)
        k = (x @ Wk).reshape(b, t, N_KV, HEAD_DIM).transpose(0, 2, 1, 3)
        v = (x @ Wv).reshape(b, t, N_KV, HEAD_DIM).transpose(0, 2, 1, 3)
        q = _apply_rope(q, cos, sin)
        k = _apply_rope(k, cos, sin)
        k_h = jnp.repeat(k, GROUP_SIZE, axis=1)
        v_h = jnp.repeat(v, GROUP_SIZE, axis=1)
        scores = jnp.einsum('bhqd,bhkd->bhqk', q, k_h) / math.sqrt(HEAD_DIM)
        causal = jnp.triu(jnp.ones((t, t), dtype=bool), k=1)
        scores = jnp.where(causal[None, None], jnp.finfo(scores.dtype).min, scores)
        attn = jax.nn.softmax(scores, axis=-1)
        ctx = jnp.einsum('bhqk,bhkd->bhqd', attn, v_h)
        ctx = ctx.transpose(0, 2, 1, 3).reshape(b, t, D_OUT)
        return ctx @ Wo

    def _L0_xattn_ref(Q, K, V):
        import jax, jax.numpy as jnp
        import numpy as np
        H = 8
        C = 2

        def _autocorrelation(Q, K, V):
            B, L, D = Q.shape
            d = D // H
            q = Q.reshape(B, L, H, d).transpose(0, 2, 1, 3)
            k = K.reshape(B, L, H, d).transpose(0, 2, 1, 3)
            v = V.reshape(B, L, H, d).transpose(0, 2, 1, 3)
            qf = jnp.fft.fft(q, axis=2)
            kf = jnp.fft.fft(k, axis=2)
            corr = jnp.fft.ifft(qf * jnp.conj(kf), axis=2).real
            topk = int(C * np.log(L))
            w, idx = jax.lax.top_k(corr.transpose(0, 1, 3, 2), topk)
            w = jax.nn.softmax(w, axis=-1)
            pos = jnp.arange(L)[:, None]
            out = jnp.zeros_like(v)
            for i in range(topk):
                g = jnp.minimum(idx[:, :, None, :, i] + pos, L - 1)
                out = out + w[:, :, None, :, i] * jnp.take_along_axis(v, g, axis=2)
            return out.transpose(0, 2, 1, 3).reshape(B, L, D)
        return _autocorrelation(Q, K, V)

    def _L0_ffn_ref(x, W_res, W_pre, W_post, H_res_base, H_pre_base, H_post_base, gate, W_branch):
        import jax, jax.numpy as jnp
        import numpy as np
        N_STREAMS = 4
        DIM = 256
        SINKHORN_ITERS = 50
        SINKHORN_TAU = 0.1
        RMS_EPS = 1.1920929e-07

        def sinkhorn_log(logits, num_iters=SINKHORN_ITERS, tau=SINKHORN_TAU):
            Z = logits / tau
            u0 = jnp.zeros(Z.shape[:-1], Z.dtype)
            v0 = jnp.zeros_like(u0)

            def step(carry, _):
                u, v = carry
                u = -jax.nn.logsumexp(Z + v[..., None, :], axis=-1)
                v = -jax.nn.logsumexp(Z + u[..., :, None], axis=-2)
                return ((u, v), None)
            (u, v), _ = jax.lax.scan(step, (u0, v0), None, length=num_iters)
            return jnp.exp(Z + u[..., :, None] + v[..., None, :])
        B, T, nC = x.shape
        n = N_STREAMS
        C = nC // n
        x_norm = x * jax.lax.rsqrt(jnp.mean(x * x, axis=-1, keepdims=True) + RMS_EPS)
        H_res_logits = (x_norm @ W_res.T).reshape(B, T, n, n) + H_res_base
        H_pre_logits = x_norm @ W_pre.T + H_pre_base
        H_post_logits = x_norm @ W_post.T + H_post_base
        H_res = sinkhorn_log(H_res_logits)
        H_pre = jax.nn.softmax(H_pre_logits, axis=-1)
        H_post = jax.nn.softmax(H_post_logits, axis=-1)
        g = jax.nn.sigmoid(gate)[0]
        I = jnp.eye(n, dtype=H_res.dtype)
        H_res = (1.0 - g) * I + g * H_res
        x_streams = x.reshape(B, T, n, C)
        x_pre = jnp.einsum('btnc,btn->btc', x_streams, H_pre)
        y = x_pre @ W_branch
        x_mixed = jnp.einsum('btij,btjc->btic', H_res, x_streams)
        y_distributed = jnp.einsum('btc,btn->btnc', y, H_post)
        return (x_mixed + y_distributed).reshape(B, T, nC)
    x = x + _L0_attn_ref(_layernorm(x, axis=-1), L0_attn_Wq, L0_attn_Wk, L0_attn_Wv, L0_attn_Wo)
    x = x + _L0_xattn_ref(_layernorm(x, axis=-1), ctx_4096, ctx_4096)
    x = x + _L0_ffn_ref(_layernorm(x, axis=-1), L0_ffn_W_res, L0_ffn_W_pre, L0_ffn_W_post, L0_ffn_H_res_base, L0_ffn_H_pre_base, L0_ffn_H_post_base, L0_ffn_gate, L0_ffn_W_branch)
    return x

_drawn_inputs = setup_inputs


def setup_inputs(seed=0):
    import zlib

    import numpy as np

    out = dict(_drawn_inputs(seed))
    spreads = {'L0_ffn_H_post_base': (0.0, 0.8)}
    factors = {'L0_ffn_W_pre': 3.709, 'L0_ffn_W_post': 2.958}
    for name, (base, spread) in spreads.items():
        noise = np.random.default_rng([zlib.crc32(name.encode()), seed]).standard_normal(out[name].shape)
        drawn = base * np.exp(spread * noise) if base else spread * noise
        out[name] = jnp.asarray(drawn.astype(out[name].dtype))
    for name, factor in factors.items():
        out[name] = (out[name] * factor).astype(out[name].dtype)
    return out
```

```python
from contextlib import ExitStack

import numpy as np
import concourse.bass as bass
from concourse import mybir

P = 128
B = 16
T = 128
D = 1024
KD = D // P
HALF = 512
NH, NKV, HD = 32, 8, 32
GROUP = NH // NKV
KVW = NKV * HD
QKVW = D + 2 * KVW
STRIPS = P // HD
LN_EPS = 1e-5

NS = 4
C = D // NS
NLOG = NS * NS + 2 * NS
SINKHORN_ITERS = 50
TAU = 0.1
RMS_EPS = 1.1920929e-07
AT_RES = D + C
AT_POST = AT_RES + NS * NS
AT_MEAN = AT_POST + NS
AT_SD = AT_MEAN + 1
ROW = AT_SD + 1
NEG = -3.0e38
FWD_A, FWD_ODD, INV_OUT, INV_CORR, N_DFT = 0, 4, 5, 9, 11

F32 = mybir.dt.float32
F32R = mybir.dt.float32r
BF16 = mybir.dt.bfloat16
ALU = mybir.AluOpType
ACT = mybir.ActivationFunctionType
AX = mybir.AxisListType


def attention_phase(nc, x, wq, wk, wv, wo, ident, causal, rope, x1):
    wo_v = wo.rearrange("(G s j d) n -> G j s d n", G=2, s=STRIPS, j=GROUP)

    with ExitStack() as ctx:
        def sb(name, shape, dt, stack=ctx):
            return stack.enter_context(nc.sbuf_tensor(name, shape, dt))

        def sem(name):
            return ctx.enter_context(nc.semaphore(name))

        w_hi = sb("w_hi", [P, KD, QKVW], F32R)
        w_lo = sb("w_lo", [P, KD, QKVW], F32R)
        wo_hi = sb("wo_hi", [P, KD, D], F32R)
        wo_lo = sb("wo_lo", [P, KD, D], F32R)
        idf = sb("idf", [P, P], F32)
        idb = sb("idb", [P, P], BF16)
        mask = sb("mask", [P, P], BF16)
        tab = sb("tab", [P, 4, HD], F32)
        xin = sb("xin", [P, D], F32)
        xT_hi = sb("xT_hi", [P, KD, T], F32R)
        xT_lo = sb("xT_lo", [P, KD, T], F32R)
        v_sb = sb("v_sb", [P, KVW], F32)
        qT = sb("qT", [P, 2, GROUP, T], F32)
        kT = sb("kT", [P, 2, T], F32)
        stats = sb("stats", [P, 2, 6], F32)
        mv = sb("mv", [P, 2], F32)
        veps = sb("veps", [P, 1], F32)
        rstd = sb("rstd", [P, 1], F32)
        mhalf = sb("mhalf", [P, 1], F32)
        pause = sb("pause", [P, 1], F32)
        negm = sb("negm", [P, NH], F32)
        lsum = sb("lsum", [P, NH], F32)
        rl = sb("rl", [P, NH], F32)
        with ExitStack() as shared:
            rc = sb("rc", [P, D + KVW], F32, shared)
            rs = sb("rs", [P, D + KVW], F32, shared)
        with ExitStack() as shared:
            prob = sb("prob", [P, 3, GROUP, T], F32, shared)
            pT = sb("pT", [P, 2, GROUP, T], F32, shared)
        sb("rc_prob_room", [P, 2 * (D + KVW)], F32)
        with ExitStack() as shared:
            w_stage = sb("w_stage", [P, 2, QKVW], F32, shared)
        aT_hi = sb("aT_hi", [P, 2, GROUP, T], F32R)
        aT_lo = sb("aT_lo", [P, 2, GROUP, T], F32R)
        with ExitStack() as shared:
            wo_stage = sb("wo_stage", [P, 2, HALF], F32, shared)
        xres = sb("xres", [P, D], F32)

        ps_qkv = ctx.enter_context(nc.psum_tensor("ps_qkv", [P, 3, HALF], F32))
        ps_s = ctx.enter_context(nc.psum_tensor("ps_s", [P, 2, HALF], F32))
        ps_t = ctx.enter_context(nc.psum_tensor("ps_t", [P, HALF], F32))
        ps_a = ctx.enter_context(nc.psum_tensor("ps_a", [P, 2, HALF], F32))

        const_in = sem("const_in")
        x_in = sem("x_in")
        w_in = [sem(f"w_in{i}") for i in range(2)]
        wo_in = [sem(f"wo_in{i}") for i in range(2)]
        xres_in = sem("xres_in")
        x1_out = sem("x1_out")
        mhalf_set = sem("mhalf_set")
        masks_done = sem("masks_done")
        w_hi_done = sem("w_hi_done")
        w_lo_done = sem("w_lo_done")
        wo_hi_done = sem("wo_hi_done")
        wo_lo_done = sem("wo_lo_done")
        stat_step = sem("stat_step")
        rstd_done = sem("rstd_done")
        xn_done = sem("xn_done")
        xT_ps = sem("xT_ps")
        xh_done = sem("xh_done")
        xl_done = sem("xl_done")
        qkv_ps = sem("qkv_ps")
        rope_done = sem("rope_done")
        v_done = sem("v_done")
        rsum_done = sem("rsum_done")
        qkT_ps = sem("qkT_ps")
        qkT_done = sem("qkT_done")
        s_ps = sem("s_ps")
        negm_done = sem("negm_done")
        e_done = sem("e_done")
        rl_done = sem("rl_done")
        p_done = sem("p_done")
        pT_ps = sem("pT_ps")
        pT_done = sem("pT_done")
        a_ps = sem("a_ps")
        ah_done = sem("ah_done")
        al_done = sem("al_done")
        o_ps = sem("o_ps")
        x1_done = sem("x1_done")

        block = ctx.enter_context(nc.Block())

        def iterations(engine, body):
            body(-2, attend=False, project=False, norm=True)
            body(-1, attend=False, project=True, norm=True)
            body(0, attend=True, project=True, norm=True, first=True)
            with engine.Fori(1, B - 2) as b:
                body(b, attend=True, project=True, norm=True)
            body(B - 2, attend=True, project=True, norm=False)
            body(B - 1, attend=True, project=False, norm=False)

        @block.sync
        def _(sp):
            sp.dma_start(xin[:], x[0]).then_inc(x_in, 16)
            sp.dma_start(idf[:], ident).then_inc(const_in, 16)
            sp.dma_start(kT[:, 0, :], causal).then_inc(const_in, 16)
            sp.dma_start(tab[:], rope).then_inc(const_in, 16)

            def body(b, attend, project, norm, first=False):
                if not attend and project:
                    for k in range(KD):
                        if k >= 2:
                            sp.wait_ge(w_hi_done, k - 1)
                            sp.wait_ge(w_lo_done, k - 1)
                        rows = slice(k * P, (k + 1) * P)
                        st = w_stage[:, k % 2, :]
                        sp.dma_start(st[:, 0:D], wq[rows, :]).then_inc(w_in[k % 2], 16)
                        sp.dma_start(st[:, D:D + KVW], wk[rows, :]).then_inc(w_in[k % 2], 16)
                        sp.dma_start(st[:, D + KVW:QKVW], wv[rows, :]).then_inc(w_in[k % 2], 16)
                if norm and (not isinstance(b, int) or b > -2):
                    sp.wait_ge(xT_ps, 2 * (b + 2))
                    sp.wait_ge(const_in, 48)
                    sp.dma_start(xin[:], x[b + 2]).then_inc(x_in, 16)
                if attend:
                    if first:
                        sp.wait_ge(w_hi_done, KD)
                        sp.wait_ge(w_lo_done, KD)
                        for n in range(2 * KD):
                            if n >= 2:
                                sp.wait_ge(wo_hi_done, n - 1)
                                sp.wait_ge(wo_lo_done, n - 1)
                            c, half = n // 2, n % 2
                            for s in range(STRIPS):
                                sp.dma_start(wo_stage[s * HD:(s + 1) * HD, n % 2, :],
                                             wo_v[c // GROUP, c % GROUP, s, :, half * HALF:(half + 1) * HALF]
                                             ).then_inc(wo_in[n % 2], 16)
                        sp.wait_ge(wo_hi_done, 2 * KD)
                        sp.wait_ge(wo_lo_done, 2 * KD)
                    else:
                        sp.wait_ge(x1_out, 16 * b)
                    sp.wait_ge(const_in, 48)
                    sp.dma_start(xres[:], x[b]).then_inc(xres_in, 16)
                    sp.wait_ge(x1_done, 2 * b + 2)
                    sp.wait_ge(const_in, 48)
                    sp.dma_start(x1[b], xres[:]).then_inc(x1_out, 16)

            iterations(sp, body)
            sp.wait_ge(x1_out, 16 * B)

        @block.tensor
        def _(pe):
            def body(b, attend, project, norm, first=False):
                def scores(g):
                    G, s = g // STRIPS, g % STRIPS
                    if g == 0:
                        pe.wait_ge(qkT_done, 3 * (b + 1))
                    if g < 2:
                        if not first:
                            pe.wait_ge(x1_done, 2 * b - 1 + g)
                    else:
                        pe.wait_ge(e_done, 8 * b + g - 1)
                    nc.tensor.matmul(ps_s[:, g % 2, :], idb[:], mask[:].rearrange("p (a k) -> p a k", a=1).to_broadcast([P, GROUP, P]),
                                     start=True, stop=False)
                    lanes = slice(s * HD, (s + 1) * HD)
                    for j in range(GROUP):
                        last = nc.tensor.matmul(ps_s[:, g % 2, j * T:(j + 1) * T], qT[lanes, G, j, :],
                                                kT[lanes, G, :], start=False, stop=j == GROUP - 1)
                    last.then_inc(s_ps, 1)

                def project_chunk(k):
                    if k == 0:
                        pe.wait_ge(xh_done, 2 * (b + 1) + 2)
                        pe.wait_ge(xl_done, 2 * (b + 1) + 2)
                        if attend:
                            pe.wait_ge(rope_done, 3 * (b + 1))
                            pe.wait_ge(v_done, b + 1)
                    if not attend:
                        pe.wait_ge(w_hi_done, k + 1)
                        pe.wait_ge(w_lo_done, k + 1)
                    for n in range(3):
                        cols = slice(n * HALF, (n + 1) * HALF)
                        nc.tensor.matmul(ps_qkv[:, n, :], xT_hi[:, k, :], w_hi[:, k, cols], start=k == 0, stop=False)
                        nc.tensor.matmul(ps_qkv[:, n, :], xT_hi[:, k, :], w_lo[:, k, cols], start=False, stop=False)
                    for n in range(3):
                        cols = slice(n * HALF, (n + 1) * HALF)
                        last = nc.tensor.matmul(ps_qkv[:, n, :], xT_lo[:, k, :], w_hi[:, k, cols],
                                                start=False, stop=k == KD - 1)
                    if k == KD - 1:
                        last.then_inc(qkv_ps, 1)

                def prob_transpose(g):
                    pe.wait_ge(p_done, 8 * b + g + 1)
                    if g > 0:
                        pe.wait_ge(pT_done, 8 * b + g)
                    for j in range(GROUP):
                        last = nc.tensor.transpose(ps_t[:, j * T:(j + 1) * T], prob[:, g % 3, j, :], idf[:])
                    last.then_inc(pT_ps, 1)

                def weigh_values(g):
                    G, s = g // STRIPS, g % STRIPS
                    pe.wait_ge(pT_done, 8 * b + g + 1)
                    last = nc.tensor.matmul(ps_a[s * HD:(s + 1) * HD, G, :], v_sb[:, g * HD:(g + 1) * HD],
                                            pT[:, g % 2, :, :], start=True, stop=True)
                    if s == STRIPS - 1:
                        last.then_inc(a_ps, 1)

                def x_transpose(half):
                    c = b + 2
                    if half == 0:
                        pe.wait_ge(xn_done, c + 1)
                        if attend:
                            pe.wait_ge(pT_done, 8 * b + 8)
                        elif project:
                            pe.wait_ge(xh_done, 2 * c)
                            pe.wait_ge(xl_done, 2 * c)
                    else:
                        pe.wait_ge(xh_done, 2 * c + 1)
                        pe.wait_ge(xl_done, 2 * c + 1)
                    for i in range(4):
                        k = 4 * half + i
                        last = nc.tensor.transpose(ps_t[:, i * T:(i + 1) * T], xin[:, k * P:(k + 1) * P], idf[:])
                    last.then_inc(xT_ps, 1)

                def qk_transpose():
                    for G in range(2):
                        pe.wait_ge(rsum_done, 3 * (b + 1) + G + 1)
                        if attend and G == 0:
                            pe.wait_ge(ah_done, 2 * b + 2)
                            pe.wait_ge(al_done, 2 * b + 2)
                        for j in range(GROUP):
                            last = nc.tensor.transpose(ps_a[:, G, j * T:(j + 1) * T], rc[:, G * HALF + j * P:G * HALF + (j + 1) * P], idf[:])
                        last.then_inc(qkT_ps, 1)
                    pe.wait_ge(rsum_done, 3 * (b + 1) + 3)
                    if norm:
                        pe.wait_ge(xh_done, 2 * (b + 2) + 2)
                        pe.wait_ge(xl_done, 2 * (b + 2) + 2)
                    for G in range(2):
                        last = nc.tensor.transpose(ps_t[:, G * T:(G + 1) * T], rc[:, D + G * P:D + (G + 1) * P], idf[:])
                    last.then_inc(qkT_ps, 1)

                def output_chunk(G, j, halves):
                    c = G * GROUP + j
                    if j == 0 and halves[0] == 0:
                        pe.wait_ge(ah_done, 2 * b + G + 1)
                        pe.wait_ge(al_done, 2 * b + G + 1)
                        if first and G == 0:
                            pe.wait_ge(wo_hi_done, 2 * KD)
                            pe.wait_ge(wo_lo_done, 2 * KD)
                    for left, right in ((aT_hi, wo_hi), (aT_hi, wo_lo), (aT_lo, wo_hi)):
                        for n in halves:
                            last = nc.tensor.matmul(ps_s[:, n, :], left[:, G, j, :], right[:, c, n * HALF:(n + 1) * HALF],
                                                    start=c == 0 and left is aT_hi and right is wo_hi,
                                                    stop=c == KD - 1 and left is aT_lo)
                    if c == KD - 1:
                        last.then_inc(o_ps, 1)

                if attend:
                    scores(0)
                    scores(1)
                for g in range(NKV):
                    if project:
                        project_chunk(g)
                    if attend:
                        prob_transpose(g)
                        if g + 2 < NKV:
                            scores(g + 2)
                        if g > 0:
                            weigh_values(g - 1)
                if attend:
                    weigh_values(NKV - 1)
                if norm:
                    x_transpose(0)
                if attend:
                    pe.wait_ge(e_done, 8 * b + 8)
                    for j in range(GROUP):
                        output_chunk(0, j, (0, 1))
                if norm:
                    x_transpose(1)
                if attend:
                    for j in range(GROUP):
                        output_chunk(1, j, (0,))
                if project:
                    qk_transpose()
                if attend:
                    for j in range(GROUP):
                        output_chunk(1, j, (1,))

            pe.wait_ge(const_in, 48)
            pe.wait_ge(masks_done, 2)
            iterations(pe, body)

        @block.scalar
        def _(act):
            act.wait_ge(const_in, 48)
            nc.scalar.activation(idb[:], idf[:], ACT.Copy).then_inc(masks_done, 1)
            nc.scalar.activation(mask[:], kT[:, 0, :], ACT.Copy).then_inc(masks_done, 1)

            def body(b, attend, project, norm, first=False):
                if project and not attend:
                    for k in range(KD):
                        act.wait_ge(w_in[k % 2], 48 * (k // 2 + 1))
                        nc.scalar.activation(w_hi[:, k, :], w_stage[:, k % 2, :], ACT.Copy).then_inc(w_hi_done, 1)

                def attend_out(G):
                    act.wait_ge(a_ps, 2 * b + G + 1)
                    if not first:
                        act.wait_ge(o_ps, 2 * b)
                    nc.scalar.activation(aT_hi[:, G, :, :], ps_a[:, G, :], ACT.Copy).then_inc(ah_done, 1)

                if attend:
                    for g in range(NKV):
                        act.wait_ge(negm_done, 8 * b + g + 1)
                        if g >= 3:
                            act.wait_ge(pT_ps, 8 * b + g - 2)
                        for j in range(GROUP):
                            h = g * GROUP + j
                            last = nc.scalar.activation(prob[:, g % 3, j, :], ps_s[:, g % 2, j * T:(j + 1) * T], ACT.Exp,
                                                        bias=negm[:, h:h + 1], accum_out=lsum[:, h:h + 1])
                        last.then_inc(e_done, 1)
                        if first:
                            for half in range(2):
                                n = 2 * g + half
                                act.wait_ge(wo_in[half], 64 * (g + 1))
                                nc.scalar.activation(wo_hi[:, g, half * HALF:(half + 1) * HALF], wo_stage[:, half, :],
                                                     ACT.Copy).then_inc(wo_hi_done, 1)
                        if g == 5:
                            attend_out(0)
                if project:
                    act.wait_ge(qkv_ps, b + 2)
                    if attend:
                        act.wait_ge(a_ps, 2 * b + 2)
                    nc.scalar.activation(v_sb[:], ps_qkv[:, 2, KVW:2 * KVW], ACT.Copy).then_inc(v_done, 1)
                if attend:
                    attend_out(1)
                if norm:
                    for half in range(2):
                        act.wait_ge(xT_ps, 2 * (b + 2) + half + 1)
                        if project:
                            act.wait_ge(qkv_ps, b + 2)
                        nc.scalar.activation(xT_hi[:, 4 * half:4 * half + 4, :], ps_t[:], ACT.Copy).then_inc(xh_done, 1)
                if project:
                    if attend:
                        act.wait_ge(s_ps, 8 * b + 8)
                    for G in range(2):
                        act.wait_ge(qkT_ps, 3 * (b + 1) + G + 1)
                        nc.scalar.activation(qT[:, G, :, :], ps_a[:, G, :], ACT.Copy).then_inc(qkT_done, 1)
                    act.wait_ge(qkT_ps, 3 * (b + 1) + 3)
                    nc.scalar.activation(kT[:, :, :], ps_t[:, 0:2 * T], ACT.Copy).then_inc(qkT_done, 1)

            iterations(act, body)

        @block.vector
        def _(dve):
            def row_negm(b, g):
                dve.wait_ge(s_ps, 8 * b + g + 1)
                nc.vector.tensor_reduce(negm[:, g * GROUP:(g + 1) * GROUP],
                                        ps_s[:, g % 2, :].rearrange("p (j k) -> p j k", j=GROUP),
                                        AX.X, ALU.max, negate=True).then_inc(negm_done, 1)

            def body(b, attend, project, norm, first=False):
                c = b + 2

                def norm_stats():
                    dve.wait_ge(x_in, 16 * (c + 1))
                    for i in range(2):
                        nc.vector.bn_stats(stats[:, i, :], xin[:, i * HALF:(i + 1) * HALF]).then_inc(stat_step, 1)
                    dve.wait_ge(stat_step, 4 * c + 2)
                    nc.vector.memset(pause[:], 0.0)
                    nc.vector.bn_aggr(mv[:], stats[:, :, :]).then_inc(stat_step, 1)
                    dve.wait_ge(stat_step, 4 * c + 3)
                    nc.vector.tensor_scalar(veps[:], mv[:, 1:2], LN_EPS, None, ALU.add).then_inc(stat_step, 1)

                def norm_apply():
                    dve.wait_ge(rstd_done, c + 1)
                    nc.vector.tensor_scalar(xin[:], xin[:], mv[:, 0:1], rstd[:], ALU.subtract, ALU.mult).then_inc(xn_done, 1)

                def attend_out(G):
                    dve.wait_ge(ah_done, 2 * b + G + 1)
                    nc.vector.tensor_tensor(aT_lo[:, G, :, :], ps_a[:, G, :].rearrange("p (j t) -> p j t", j=GROUP),
                                            aT_hi[:, G, :, :].bitcast(F32), ALU.subtract).then_inc(al_done, 1)

                def x_lo(half):
                    dve.wait_ge(xh_done, 2 * c + half + 1)
                    nc.vector.tensor_tensor(xT_lo[:, 4 * half:4 * half + 4, :], ps_t[:].rearrange("p (k t) -> p k t", k=4),
                                            xT_hi[:, 4 * half:4 * half + 4, :].bitcast(F32),
                                            ALU.subtract).then_inc(xl_done, 1)

                def rope_bank(n):
                    a, c = (STRIPS, GROUP) if n < 2 else (1, NKV)
                    w = a * c * HD
                    t = 0 if n < 2 else 2
                    at = slice(n * HALF, n * HALF + w)
                    src = ps_qkv[:, n, 0:w].rearrange("p (a c i) -> p a c i", a=a, c=c)
                    by_cos = rc[:, at].rearrange("p (c a i) -> p a c i", a=a, c=c)
                    by_sin = rs[:, at].rearrange("p (c a i) -> p a c i", a=a, c=c)
                    cos = tab[:, t:t + 1, :].rearrange("p o (r i) -> p o r i", r=1)
                    sin = tab[:, t + 1:t + 2, :].rearrange("p o (r i) -> p o r i", r=1)
                    nc.vector.tensor_tensor(by_cos, src, cos.to_broadcast([P, a, c, HD]), ALU.mult)
                    for lo, hi in ((0, HD // 2), (HD // 2, 0)):
                        to, of = slice(lo, lo + HD // 2), slice(hi, hi + HD // 2)
                        last = nc.vector.tensor_tensor(by_sin[:, :, :, to], src[:, :, :, of],
                                                       sin[:, :, :, to].to_broadcast([P, a, c, HD // 2]), ALU.mult)
                    last.then_inc(rope_done, 1)

                if project and not attend:
                    for k in range(KD):
                        dve.wait_ge(w_hi_done, k + 1)
                        nc.vector.tensor_tensor(w_lo[:, k, :], w_stage[:, k % 2, :], w_hi[:, k, :].bitcast(F32),
                                                ALU.subtract).then_inc(w_lo_done, 1)
                if attend:
                    row_negm(b, 0)
                    row_negm(b, 1)
                    for g in range(NKV):
                        dve.wait_ge(e_done, 8 * b + g + 1)
                        hs = slice(g * GROUP, (g + 1) * GROUP)
                        nc.vector.reciprocal(rl[:, hs], lsum[:, hs]).then_inc(rl_done, 1)
                        if first:
                            for half in range(2):
                                n = 2 * g + half
                                dve.wait_ge(wo_hi_done, n + 1)
                                cols = slice(half * HALF, (half + 1) * HALF)
                                nc.vector.tensor_tensor(wo_lo[:, g, cols], wo_stage[:, half, :],
                                                        wo_hi[:, g, cols].bitcast(F32), ALU.subtract).then_inc(wo_lo_done, 1)
                        dve.wait_ge(pT_ps, 8 * b + g + 1)
                        nc.vector.tensor_copy(pT[:, g % 2, :, :], ps_t[:].rearrange("p (j t) -> p j t", j=GROUP)).then_inc(pT_done, 1)
                        if g + 2 < NKV:
                            row_negm(b, g + 2)
                        if norm and g == 1:
                            norm_stats()
                        if norm and g == 4:
                            norm_apply()
                        if g == 5:
                            attend_out(0)
                elif norm:
                    norm_stats()
                    norm_apply()
                if project:
                    dve.wait_ge(qkv_ps, b + 2)
                    if attend:
                        dve.wait_ge(a_ps, 2 * b + 2)
                    rope_bank(0)
                if attend:
                    attend_out(1)
                if norm:
                    x_lo(0)
                if project:
                    rope_bank(1)
                    rope_bank(2)
                if norm:
                    x_lo(1)
                if attend:
                    dve.wait_ge(xres_in, 16 * (b + 1))
                    for n in range(2):
                        cols = slice(n * HALF, (n + 1) * HALF)
                        dve.wait_ge(o_ps, 2 * b + n + 1)
                        nc.vector.tensor_tensor(xres[:, cols], ps_s[:, n, :], xres[:, cols], ALU.add).then_inc(x1_done, 1)

            dve.wait_ge(const_in, 48)
            iterations(dve, body)

        @block.gpsimd
        def _(pool):
            nc.gpsimd.memset(mhalf[:], -0.5).then_inc(mhalf_set, 1)
            pool.wait_ge(mhalf_set, 1)

            def body(b, attend, project, norm, first=False):
                def norm_rstd():
                    pool.wait_ge(stat_step, 4 * (b + 2) + 4)
                    nc.gpsimd.tensor_tensor(rstd[:], veps[:], mhalf[:], ALU.pow).then_inc(rstd_done, 1)

                if attend:
                    for g in range(NKV):
                        pool.wait_ge(rl_done, 8 * b + g + 1)
                        nc.gpsimd.tensor_tensor(prob[:, g % 3, :, :], prob[:, g % 3, :, :],
                                                rl[:, g * GROUP:(g + 1) * GROUP].rearrange("p (j o) -> p j o", o=1).to_broadcast([P, GROUP, T]),
                                                ALU.mult).then_inc(p_done, 1)
                        if norm and g == 2:
                            norm_rstd()
                elif norm:
                    norm_rstd()
                if project:
                    for n in range(3):
                        at = slice(n * HALF, min((n + 1) * HALF, D + KVW))
                        pool.wait_ge(rope_done, 3 * (b + 1) + n + 1)
                        nc.gpsimd.tensor_tensor(rc[:, at], rc[:, at], rs[:, at], ALU.add).then_inc(rsum_done, 1)

            iterations(pool, body)


def autocorrelation_phase(nc, x1, ctx_in, ident, dft, w24, base, wb, rows):
    with ExitStack() as ctx:
        def sb(name, shape, dt=F32):
            return ctx.enter_context(nc.sbuf_tensor("c_" + name, shape, dt))

        def sem(name):
            return ctx.enter_context(nc.semaphore("c_" + name))

        idf = sb("b_idf", [P, P])
        mats = sb("mats", [P, N_DFT, P])
        fwd_hi = sb("fwd_hi", [P, 4, P], F32R)
        fwd_lo = sb("fwd_lo", [P, 4, P], F32R)
        w24_sb = sb("w24_sb", [P, KD, NLOG])
        base_sb = sb("base_sb", [P, NLOG])
        wb_sb = sb("wb_sb", [P, 2, C])
        xin = sb("xin", [P, D])
        xn = sb("xn", [P, D])
        xres = sb("b_xres", [P, D])
        cin = sb("cin", [P, D])
        c_hi = [sb(f"c_hi{i}", [P, D], F32R) for i in range(2)]
        c_lo = [sb(f"c_lo{i}", [P, D], F32R) for i in range(2)]
        spec = [[sb(f"spec{i}{n}", [P, D]) for n in range(4)] for i in range(2)]
        row = [sb(f"row{i}", [P, ROW]) for i in range(2)]
        tq = [sb(f"tq{i}", [P, D]) for i in range(2)]
        tw = [sb(f"tw{i}", [P, D]) for i in range(4)]
        pause = sb("pause", [P, 4])
        top = sb("top", [P, KD, 8])
        ntop = sb("ntop", [P, KD])
        corr = sb("corr", [P, KD, T])
        rest = sb("rest", [P, KD, T])
        ninth = sb("ninth", [P, KD])
        ex = sb("ex", [P, KD, T])
        wgt = sb("wgt", [P, KD, T])
        wsum = sb("wsum", [P, KD])
        wrec = sb("wrec", [P, KD])
        wT = sb("wT", [P, D])
        x2 = sb("x2", [P, D])
        x3T = sb("x3T", [P, KD, T])
        xp = sb("xp", [P, C])
        xpT = sb("xpT", [P, 2, T])
        st2 = sb("st2", [P, 2, 6])
        mv2 = sb("mv2", [P, 2])
        ve2 = sb("ve2", [P, 1])
        rstd2 = sb("rstd2", [P, 1])
        st3 = sb("st3", [P, 2, 6])
        mv3 = sb("mv3", [P, 2])
        ve3 = sb("ve3", [P, 1])
        rstd3 = sb("rstd3", [P, 1])
        nb2 = sb("nb2", [P, 2])
        nb3 = sb("nb3", [P, 2])
        ms = sb("ms", [P, 3])
        rs = sb("rs", [P, 1])
        consts = sb("consts", [P, 4])
        mhalf, one, rms_eps, minus = (consts[:, i:i + 1] for i in range(4))
        lg = sb("lg", [P, NLOG])
        hx = sb("hx", [P, 2])
        hd = sb("hd", [P, 2, NS])
        he = sb("he", [P, 2, NS])
        hs = sb("hs", [P, 2])
        hr = sb("hr", [P, 2])
        hp = sb("hp", [P, NS])

        pair = [ctx.enter_context(nc.psum_tensor(f"pair{i}", [P, 2, HALF], F32)) for i in range(4)]
        p_a, p_b, p_c, p_d = pair
        flat = [p[:, :, :].rearrange("p a n -> p (a n)") for p in pair]
        f_a, f_b, f_c, f_d = flat
        logits = p_d[:, 0, 0:NLOG]
        y_ps_at = p_d[:, 0, C:2 * C]
        xpT_at = p_d[:, 1, 0:2 * T]

        const_in = sem("const_in"); fwd_hi_done = sem("fwd_hi_done"); fwd_lo_done = sem("fwd_lo_done")
        consts_set = sem("consts_set")
        x_in = sem("x_in"); xres_in = sem("xres_in"); cin_in = sem("cin_in")
        row_out = [sem(f"row_out{i}") for i in range(2)]
        n2_step = sem("n2_step"); rstd2_done = sem("rstd2_done"); nb2_step = sem("nb2_step"); xn_done = sem("xn_done")
        chi_done = sem("chi_done"); clo_done = sem("clo_done")
        k_ps = sem("k_ps"); k_done = sem("k_done"); v_ps = sem("v_ps"); v_done = sem("v_done")
        q_ps = sem("q_ps"); tq_done = sem("tq_done"); corr_ps = sem("corr_ps"); corr_done = sem("corr_done")
        max_done = sem("max_done"); ntop_done = sem("ntop_done"); rest_done = sem("rest_done")
        ninth_done = sem("ninth_done"); exp_done = sem("exp_done"); pick_done = sem("pick_done")
        wrec_done = sem("wrec_done"); w_done = sem("w_done")
        wT_ps = sem("wT_ps"); wT_done = sem("wT_done"); ws_ps = sem("ws_ps"); tw_done = sem("tw_done")
        out_ps = sem("out_ps"); x2_done = sem("x2_done"); n3_step = sem("n3_step"); rstd3_done = sem("rstd3_done")
        x3_done = sem("x3_done"); x3T_ps = sem("x3T_ps"); x3T_done = sem("x3T_done"); lg_ps = sem("lg_ps")
        pool_step = sem("pool_step"); rs_done = sem("rs_done"); h_step = sem("h_step"); he_done = sem("he_done")
        xp_step = sem("xp_step"); xpT_ps = sem("xpT_ps"); xpT_done = sem("xpT_done"); y_ps = sem("y_ps")
        y_done = sem("y_done")
        N3, PS, HS, XS = 4, 7, 8, 4

        block = ctx.enter_context(nc.Block())

        def iterations(engine, body):
            body(-1, 1, near=True, far=False, last=False, tail=False, ahead=True)
            body(0, 0, near=True, far=True, last=False, tail=False, ahead=True)
            body(1, 1, near=True, far=True, last=True, tail=False, ahead=True)
            body(2, 0, near=True, far=True, last=True, tail=True, ahead=True)
            with engine.Fori(0, (B - 6) // 2) as u:
                body(2 * u + 3, 1, near=True, far=True, last=True, tail=True, ahead=True)
                body(2 * u + 4, 0, near=True, far=True, last=True, tail=True, ahead=True)
            body(B - 3, 1, near=True, far=True, last=True, tail=True, ahead=True)
            body(B - 2, 0, near=True, far=True, last=True, tail=True, ahead=False)
            body(B - 1, 1, near=False, far=True, last=True, tail=True, ahead=False)
            body(B, 0, near=False, far=False, last=True, tail=True, ahead=False)
            body(B + 1, 1, near=False, far=False, last=False, tail=True, ahead=False)

        def later(b, first):
            return not isinstance(b, int) or b > first

        def turns(n, par):
            return n // 2 if isinstance(n, int) else (n - par) // 2

        @block.sync
        def _(sp):
            sp.dma_start(cin[:], ctx_in[0]).then_inc(cin_in, 16)
            sp.dma_start(mats[:], dft).then_inc(const_in, 16)
            sp.dma_start(xin[:], x1[0]).then_inc(x_in, 16)
            sp.dma_start(idf[:], ident).then_inc(const_in, 16)
            sp.dma_start(w24_sb[:], w24).then_inc(const_in, 16)
            sp.dma_start(base_sb[:], base).then_inc(const_in, 16)
            sp.dma_start(wb_sb[:], wb.rearrange("(k p) n -> p k n", k=2)).then_inc(const_in, 16)

            def body(b, par, near, far, last, tail, ahead):
                if tail:
                    sp.wait_ge(y_done, b - 1)
                    sp.dma_start(rows[b - 2], row[par][:]).then_inc(row_out[par], 16)
                if ahead:
                    sp.wait_ge(chi_done, b + 2)
                    sp.wait_ge(clo_done, b + 2)
                    sp.dma_start(cin[:], ctx_in[b + 2]).then_inc(cin_in, 16)
                    sp.wait_ge(xn_done, b + 2)
                    sp.dma_start(xin[:], x1[b + 2]).then_inc(x_in, 16)
                if far:
                    if near or last:
                        if later(b, 0):
                            sp.wait_ge(x2_done, 2 * b)
                    sp.dma_start(xres[:], x1[b]).then_inc(xres_in, 16)

            iterations(sp, body)
            for i in range(2):
                sp.wait_ge(row_out[i], 8 * B)

        @block.tensor
        def _(pe):
            def split3(dst, i, par):
                for n in range(2):
                    cols = slice(n * HALF, (n + 1) * HALF)
                    nc.tensor.matmul(dst[:, n, :], fwd_hi[:, i, :], c_hi[par][:, cols], start=True, stop=False)
                    nc.tensor.matmul(dst[:, n, :], fwd_hi[:, i, :], c_lo[par][:, cols], start=False, stop=False)
                    r = nc.tensor.matmul(dst[:, n, :], fwd_lo[:, i, :], c_hi[par][:, cols], start=False, stop=True)
                return r

            def spectrum(dst, i, src):
                for n in range(2):
                    r = nc.tensor.matmul(dst[:, n, :], mats[:, i, :], src[:, n * HALF:(n + 1) * HALF], start=True, stop=True)
                return r

            def out_half(n):
                for i in range(4):
                    r = nc.tensor.matmul(p_b[:, n, :], mats[:, INV_OUT + i, :], tw[i][:, n * HALF:(n + 1) * HALF],
                                         start=i == 0, stop=i == 3)
                r.then_inc(out_ps, 1)

            def body(b, par, near, far, last, tail, ahead):
                c = b + 1
                if near:
                    pe.wait_ge(xn_done, c + 1)
                    if far:
                        pe.wait_ge(v_done, 2 * b + 1)
                    spectrum(p_a, FWD_A, xn).then_inc(q_ps, 1)
                if tail:
                    pe.wait_ge(xp_step, XS * (b - 1))
                    pe.wait_ge(x3T_done, 2 * (b - 1))
                    for i in range(2):
                        r = nc.tensor.transpose(xpT_at[:, i * T:(i + 1) * T], xp[:, i * P:(i + 1) * P], idf[:])
                    r.then_inc(xpT_ps, 1)
                if near:
                    pe.wait_ge(chi_done, c + 1)
                    pe.wait_ge(clo_done, c + 1)
                    if last:
                        pe.wait_ge(x2_done, 2 * b)
                    split3(p_b, 0, 1 - par).then_inc(k_ps, 1)
                if tail:
                    pe.wait_ge(xpT_done, b - 1)
                    for i in range(2):
                        r = nc.tensor.matmul(y_ps_at, xpT[:, i, :], wb_sb[:, i, :], start=i == 0, stop=i == 1)
                    r.then_inc(y_ps, 1)
                    pe.wait_ge(y_done, b - 1)
                if far:
                    pe.wait_ge(w_done, b + 1)
                    for i in range(KD):
                        r = nc.tensor.transpose(f_d[:, i * T:(i + 1) * T], wgt[:, i, :], idf[:])
                    r.then_inc(wT_ps, 1)
                if near:
                    if far:
                        pe.wait_ge(v_done, 2 * b + 2)
                    split3(p_c, 1, 1 - par).then_inc(k_ps, 1)
                if far:
                    pe.wait_ge(wT_done, 2 * b + 2)
                    if near:
                        pe.wait_ge(k_done, 2 * c + 1)
                    else:
                        pe.wait_ge(x2_done, 2 * b)
                        pe.wait_ge(v_done, 2 * b + 2)
                    spectrum(p_b, FWD_A, wT).then_inc(ws_ps, 1)
                    if near:
                        pe.wait_ge(k_done, 2 * c + 2)
                    spectrum(p_c, FWD_ODD, wT).then_inc(ws_ps, 1)
                if near:
                    for n in range(2):
                        pe.wait_ge(tq_done, 2 * c + 2)
                        for i in range(4 * n, 4 * n + 4):
                            for t in range(2):
                                r = nc.tensor.matmul(f_a[:, i * T:(i + 1) * T], tq[t][:, i * P:(i + 1) * P], mats[:, INV_CORR + t, :],
                                                     start=t == 0, stop=t == 1)
                        r.then_inc(corr_ps, 1)
                if last:
                    pe.wait_ge(x3_done, b)
                    for i in range(KD):
                        r = nc.tensor.transpose(f_d[:, i * T:(i + 1) * T], row[1 - par][:, i * P:(i + 1) * P], idf[:])
                        if i % 4 == 3:
                            r.then_inc(x3T_ps, 1)
                if far:
                    pe.wait_ge(tw_done, 4 * b + 4)
                    out_half(0)
                if last:
                    pe.wait_ge(x3T_done, 2 * b)
                    for i in range(KD):
                        r = nc.tensor.matmul(logits, x3T[:, i, :], w24_sb[:, i, :], start=i == 0, stop=i == KD - 1)
                    r.then_inc(lg_ps, 1)
                if far:
                    out_half(1)
                if near:
                    pe.wait_ge(corr_done, 2 * c + 2)
                    split3(p_a, 2, 1 - par).then_inc(v_ps, 1)
                    split3(p_c, 3, 1 - par).then_inc(v_ps, 1)

            pe.wait_ge(const_in, 80)
            pe.wait_ge(fwd_hi_done, 1)
            pe.wait_ge(fwd_lo_done, 1)
            iterations(pe, body)

        @block.scalar
        def _(act):
            act.wait_ge(const_in, 80)
            nc.scalar.activation(fwd_hi[:, :, :], mats[:, 0:4, :], ACT.Copy).then_inc(fwd_hi_done, 1)

            def split_context(n, par):
                act.wait_ge(cin_in, 16 * (n + 1))
                if later(n, 1):
                    act.wait_ge(v_ps, 2 * (n - 1))
                nc.scalar.activation(c_hi[par][:], cin[:], ACT.Copy).then_inc(chi_done, 1)

            def normalise(n):
                act.wait_ge(nb2_step, 2 * (n + 1))
                if later(n, 0):
                    act.wait_ge(q_ps, n)
                nc.scalar.activation(xn[:], xin[:], ACT.Identity, bias=nb2[:, 1:2], scale=rstd2[:]).then_inc(xn_done, 1)

            split_context(0, 0)
            normalise(0)

            def body(b, par, near, far, last, tail, ahead):
                c = b + 1

                def key_spectrum(i, src):
                    act.wait_ge(k_ps, 2 * c + i + 1)
                    if last:
                        act.wait_ge(tw_done, 4 * b)
                    nc.scalar.activation(spec[1 - par][i][:], src, ACT.Copy).then_inc(k_done, 1)

                if tail:
                    act.wait_ge(xpT_ps, b - 1)
                    nc.scalar.activation(xpT[:, :, :], xpT_at, ACT.Copy).then_inc(xpT_done, 1)
                if near:
                    key_spectrum(0, f_b)
                if tail:
                    act.wait_ge(y_ps, b - 1)
                    nc.scalar.activation(row[par][:, D:D + C], y_ps_at, ACT.Copy).then_inc(y_done, 1)
                if far:
                    act.wait_ge(wT_ps, b + 1)
                    for n in range(2):
                        nc.scalar.activation(wT[:, n * HALF:(n + 1) * HALF], p_d[:, n, :], ACT.Copy).then_inc(wT_done, 1)
                if near:
                    key_spectrum(1, f_c)
                if last:
                    act.wait_ge(pool_step, PS * (b - 1) + 2)
                    if tail and later(b, 2):
                        act.wait_ge(row_out[1 - par], 16 * turns(b - 1, 1 - par))
                    nc.scalar.activation(row[1 - par][:, 0:D], x2[:], ACT.Identity, bias=nb3[:, 1:2],
                                         scale=rstd3[:]).then_inc(x3_done, 1)
                if ahead:
                    split_context(b + 2, par)
                if near:
                    if far:
                        act.wait_ge(pick_done, 8 * c)
                    for n in range(2):
                        act.wait_ge(corr_ps, 2 * c + n + 1)
                        nc.scalar.activation(corr[:, 4 * n:4 * n + 4, :], p_a[:, n, :], ACT.Copy).then_inc(corr_done, 1)
                if last:
                    for n in range(2):
                        act.wait_ge(x3T_ps, 2 * (b - 1) + n + 1)
                        nc.scalar.activation(x3T[:, 4 * n:4 * n + 4, :], p_d[:, n, :], ACT.Copy).then_inc(x3T_done, 1)
                if ahead:
                    normalise(b + 2)
                if near:
                    act.wait_ge(ntop_done, c + 1)
                    for i in range(KD):
                        nc.scalar.activation(ex[:, i, :], corr[:, i, :], ACT.Exp,
                                             bias=ntop[:, i:i + 1]).then_inc(exp_done, 1)
                if last:
                    act.wait_ge(h_step, HS * (b - 1) + 3)
                    nc.scalar.activation(he[:, :, :], hd[:, :, :], ACT.Exp).then_inc(he_done, 1)
                if near:
                    for i, src in ((2, f_a), (3, f_c)):
                        act.wait_ge(v_ps, 2 * c + i - 1)
                        nc.scalar.activation(spec[1 - par][i][:], src, ACT.Copy).then_inc(v_done, 1)

            iterations(act, body)

        @block.vector
        def _(dve):
            dve.wait_ge(fwd_hi_done, 1)
            nc.vector.tensor_tensor(fwd_lo[:, :, :], mats[:, 0:4, :], fwd_hi[:, :, :].bitcast(F32),
                                    ALU.subtract).then_inc(fwd_lo_done, 1)

            def norm2_stats(n):
                dve.wait_ge(x_in, 16 * (n + 1))
                for i in range(2):
                    nc.vector.bn_stats(st2[:, i, :], xin[:, i * HALF:(i + 1) * HALF]).then_inc(n2_step, 1)
                dve.wait_ge(n2_step, 4 * n + 2)
                nc.vector.memset(pause[:, 2:3], 0.0)
                nc.vector.bn_aggr(mv2[:], st2[:, :, :]).then_inc(n2_step, 1)
                dve.wait_ge(n2_step, 4 * n + 3)
                nc.vector.tensor_scalar(ve2[:], mv2[:, 1:2], LN_EPS, None, ALU.add).then_inc(n2_step, 1)

            norm2_stats(0)

            def body(b, par, near, far, last, tail, ahead):
                c = b + 1
                m = b - 1

                def products():
                    for i, src in enumerate((f_b, f_b, f_c, f_c)):
                        if i % 2 == 0:
                            dve.wait_ge(ws_ps, 2 * b + i // 2 + 1)
                            if i == 0:
                                dve.wait_ge(v_done, 2 * b + 2)
                                if last:
                                    dve.wait_ge(out_ps, 2 * b)
                        nc.vector.tensor_tensor(tw[i][:], src, spec[par][i][:], ALU.mult).then_inc(tw_done, 1)

                def h_steps(first, to):
                    pp = lg[:, NS * NS:NLOG].rearrange("p (a n) -> p a n", a=2)
                    r = row[1 - par]
                    for k in range(first, to + 1):
                        if k == 1:
                            dve.wait_ge(lg_ps, b)
                            dve.wait_ge(rs_done, b)
                            ins = nc.vector.scalar_tensor_tensor(lg[:], logits, rs[:], base_sb[:], ALU.mult, ALU.add)
                        else:
                            dve.wait_ge(h_step, HS * m + k - 1)
                        if k == 2:
                            ins = nc.vector.tensor_reduce(hx[:], pp, AX.X, ALU.max)
                        if k == 3:
                            ins = nc.vector.tensor_tensor(hd[:, :, :], pp, hx[:].rearrange("p (a o) -> p a o", o=1).to_broadcast([P, 2, NS]), ALU.subtract)
                        if k == 4:
                            ins = nc.vector.tensor_scalar(r[:, AT_RES:AT_RES + NS * NS], lg[:, 0:NS * NS], 1.0 / TAU, None, ALU.mult)
                        if k == 5:
                            dve.wait_ge(he_done, b)
                            ins = nc.vector.tensor_reduce(hs[:], he[:, :, :], AX.X, ALU.add)
                        if k == 6:
                            ins = nc.vector.reciprocal(hr[:], hs[:])
                        if k == 7:
                            ins = nc.vector.tensor_scalar(r[:, AT_POST:AT_POST + NS], he[:, 1, :], hr[:, 1:2], None, ALU.mult)
                        if k == 8:
                            ins = nc.vector.tensor_scalar(hp[:], he[:, 0, :], hr[:, 0:1], None, ALU.mult)
                        ins.then_inc(h_step, 1)

                def branch_in(n):
                    x = row[1 - par][:, n * C:(n + 1) * C]
                    if n == 0:
                        dve.wait_ge(h_step, HS * m + HS)
                        if later(b, 1):
                            dve.wait_ge(xpT_ps, b - 1)
                        ins = nc.vector.tensor_scalar(xp[:], x, hp[:, 0:1], None, ALU.mult)
                    else:
                        dve.wait_ge(xp_step, XS * m + n)
                        ins = nc.vector.scalar_tensor_tensor(xp[:], x, hp[:, n:n + 1], xp[:], ALU.mult, ALU.add)
                    ins.then_inc(xp_step, 1)

                if near:
                    dve.wait_ge(q_ps, c + 1)
                    if far:
                        dve.wait_ge(corr_ps, 2 * c)
                    for i in range(2):
                        dve.wait_ge(k_done, 2 * c + i + 1)
                        nc.vector.tensor_tensor(tq[i][:], f_a, spec[1 - par][i][:], ALU.mult).then_inc(tq_done, 1)
                if far:
                    products()
                if ahead:
                    norm2_stats(b + 2)
                if near:
                    for i in range(KD):
                        if i % 4 == 0:
                            dve.wait_ge(corr_done, 2 * c + i // 4 + 1)
                            nc.vector.memset(pause[:, i // 4:i // 4 + 1], 0.0)
                        nc.vector.max(top[:, i, :], corr[:, i, :]).then_inc(max_done, 1)
                    dve.wait_ge(max_done, 8 * c + 8)
                    nc.vector.tensor_scalar(ntop[:], top[:, :, 0], -1.0, None, ALU.mult).then_inc(ntop_done, 1)
                    for i in range(KD):
                        nc.vector.match_replace(rest[:, i, :], top[:, i, :], corr[:, i, :], NEG).then_inc(rest_done, 1)
                if last:
                    h_steps(1, 2)
                if near:
                    dve.wait_ge(rest_done, 8 * c + 8)
                    nc.vector.tensor_reduce(ninth[:], rest[:, :, :], AX.X, ALU.max).then_inc(ninth_done, 1)
                if last:
                    h_steps(3, 4)
                if near:
                    dve.wait_ge(ninth_done, c + 1)
                    if far:
                        dve.wait_ge(wT_ps, b + 1)
                    for i in range(KD):
                        dve.wait_ge(exp_done, 8 * c + i + 1)
                        nc.vector.scalar_tensor_tensor(wgt[:, i, :], corr[:, i, :], ninth[:, i:i + 1], ex[:, i, :],
                                                       ALU.is_ge, ALU.mult, accum_out=wsum[:, i:i + 1]).then_inc(pick_done, 1)
                if near:
                    dve.wait_ge(pick_done, 8 * c + 8)
                    nc.vector.reciprocal(wrec[:], wsum[:]).then_inc(wrec_done, 1)
                if last:
                    h_steps(5, 8)
                    branch_in(0)
                if far:
                    dve.wait_ge(xres_in, 16 * (b + 1))
                    if last:
                        dve.wait_ge(x3_done, b)
                for n in range(2):
                    if far:
                        dve.wait_ge(out_ps, 2 * b + n + 1)
                        cols = slice(n * HALF, (n + 1) * HALF)
                        nc.vector.tensor_tensor(x2[:, cols], p_b[:, n, :], xres[:, cols], ALU.add).then_inc(x2_done, 1)
                    if last:
                        branch_in(n + 1)
                if last:
                    branch_in(3)
                if far:
                    for n in range(2):
                        dve.wait_ge(x2_done, 2 * b + n + 1)
                        nc.vector.bn_stats(st3[:, n, :], x2[:, n * HALF:(n + 1) * HALF]).then_inc(n3_step, 1)
                    dve.wait_ge(n3_step, N3 * b + 2)
                    if last:
                        dve.wait_ge(pool_step, PS * b)
                    nc.vector.memset(pause[:, 3:4], 0.0)
                    nc.vector.bn_aggr(mv3[:], st3[:, :, :]).then_inc(n3_step, 1)
                    dve.wait_ge(n3_step, N3 * b + 3)
                    nc.vector.tensor_scalar(ve3[:], mv3[:, 1:2], LN_EPS, None, ALU.add).then_inc(n3_step, 1)

            iterations(dve, body)

        @block.gpsimd
        def _(pool):
            for at, value in ((mhalf, -0.5), (one, 1.0), (rms_eps, RMS_EPS), (minus, -1.0)):
                nc.gpsimd.memset(at, value).then_inc(consts_set, 1)
            pool.wait_ge(consts_set, 4)
            TT = nc.gpsimd.tensor_tensor

            def split_context(n, par):
                pool.wait_ge(chi_done, n + 1)
                if later(n, 1):
                    pool.wait_ge(v_ps, 2 * (n - 1))
                TT(c_lo[par][:], cin[:], c_hi[par][:].bitcast(F32), ALU.subtract).then_inc(clo_done, 1)

            def norm2(n):
                pool.wait_ge(n2_step, 4 * n + 4)
                TT(rstd2[:], ve2[:], mhalf, ALU.pow).then_inc(rstd2_done, 1)
                pool.wait_ge(rstd2_done, n + 1)
                TT(nb2[:, 0:1], mv2[:, 0:1], rstd2[:], ALU.mult).then_inc(nb2_step, 1)
                pool.wait_ge(nb2_step, 2 * n + 1)
                TT(nb2[:, 1:2], nb2[:, 0:1], minus, ALU.mult).then_inc(nb2_step, 1)

            norm2(0)
            split_context(0, 0)

            def body(b, par, near, far, last, tail, ahead):
                c = b + 1
                if ahead:
                    split_context(b + 2, par)
                    norm2(b + 2)
                if near:
                    pool.wait_ge(wrec_done, c + 1)
                    TT(wgt[:, :, :], wgt[:, :, :], wrec[:].rearrange("p (k o) -> p k o", o=1).to_broadcast([P, KD, T]),
                       ALU.mult).then_inc(w_done, 1)
                if far:
                    def step(k, ins):
                        ins.then_inc(pool_step, 1)
                        pool.wait_ge(pool_step, PS * b + k)

                    pool.wait_ge(n3_step, N3 * b + 4)
                    TT(rstd3[:], ve3[:], mhalf, ALU.pow).then_inc(rstd3_done, 1)
                    pool.wait_ge(rstd3_done, b + 1)
                    step(1, TT(nb3[:, 0:1], mv3[:, 0:1], rstd3[:], ALU.mult))
                    step(2, TT(nb3[:, 1:2], nb3[:, 0:1], minus, ALU.mult))
                    if last and later(b, 1):
                        pool.wait_ge(row_out[par], 16 * turns(b, par))
                    step(3, TT(row[par][:, AT_SD:AT_SD + 1], ve3[:], rstd3[:], ALU.mult))
                    step(4, TT(row[par][:, AT_MEAN:AT_MEAN + 1], mv3[:, 0:1], one, ALU.mult))
                    step(5, TT(ms[:, 0:1], mv3[:, 1:2], rstd3[:], ALU.mult))
                    step(6, TT(ms[:, 1:2], ms[:, 0:1], rstd3[:], ALU.mult))
                    step(7, TT(ms[:, 2:3], ms[:, 1:2], rms_eps, ALU.add))
                    if last:
                        pool.wait_ge(h_step, HS * (b - 1) + 1)
                    TT(rs[:], ms[:, 2:3], mhalf, ALU.pow).then_inc(rs_done, 1)

            iterations(pool, body)


def mixing_phase(nc, rows, gate, out):
    with ExitStack() as ctx:
        def sb(name, shape, dt=F32):
            return ctx.enter_context(nc.sbuf_tensor("m_" + name, shape, dt))

        def sem(name):
            return ctx.enter_context(nc.semaphore("m_" + name))

        HB = B // 2
        N2 = NS * NS
        tail = sb("tail", [P, B, ROW - AT_RES])
        logm = sb("logm", [P, B, N2])
        mat = sb("mat", [P, B, N2])
        tmp = sb("tmp", [P, B, N2])
        ra = sb("ra", [P, B, NS])
        cb = sb("cb", [P, B, NS])
        red = sb("red", [P, B, NS])
        lra = sb("lra", [P, B, NS])
        lcb = sb("lcb", [P, B, NS])
        coef = sb("coef", [P, B, N2 + NS + 1])
        now = [sb(f"now{i}", [P, N2 + NS + 1]) for i in range(2)]
        gt = sb("gt", [P, 4])
        xr = [sb(f"xr{i}", [P, AT_RES]) for i in range(2)]
        ot = [sb(f"ot{i}", [P, D]) for i in range(2)]

        tail_in = sem("tail_in"); g_step = sem("g_step"); g_exp = sem("g_exp")
        step = [sem(f"step{i}") for i in range(2)]
        logs = [sem(f"logs{i}") for i in range(2)]
        coef_step = sem("coef_step")
        row_in = [sem(f"row_in{i}") for i in range(2)]
        now_done = sem("now_done"); mix_step = sem("mix_step")
        stored = [sem(f"stored{i}") for i in range(2)]

        block = ctx.enter_context(nc.Block())

        BLOCKS, ITERS = 7, (SINKHORN_ITERS - 1) // 7
        assert 1 + BLOCKS * ITERS == SINKHORN_ITERS
        FIRST, BLOCK = 8, 1 + 6 * ITERS + 2
        LFIRST, LBLOCK = 4, 3

        @block.sync
        def _(sp):
            sp.dma_start(tail[:, :, :], rows.rearrange("b p n -> p b n")[:, :, AT_RES:ROW]).then_inc(tail_in, 16)
            sp.dma_start(gt[:, 0:1], gate).then_inc(tail_in, 16)
            rows_v = rows.rearrange("(u s) p n -> u s p n", s=2)
            out_v = out.rearrange("(u s) p n -> u s p n", s=2)
            for i in range(2):
                sp.dma_start(xr[i][:], rows_v[0, i, :, 0:AT_RES]).then_inc(row_in[i], 16)
            with sp.Fori(0, B // 2 - 1) as u:
                for i in range(2):
                    sp.wait_ge(mix_step, 20 * (2 * u + i + 1))
                    sp.wait_ge(tail_in, 32)
                    sp.dma_start(out_v[u, i], ot[i][:]).then_inc(stored[i], 16)
                    sp.dma_start(xr[i][:], rows_v[u + 1, i, :, 0:AT_RES]).then_inc(row_in[i], 16)
            for i in range(2):
                sp.wait_ge(mix_step, 20 * (B - 2 + i + 1))
                sp.wait_ge(tail_in, 32)
                sp.dma_start(out_v[B // 2 - 1, i], ot[i][:]).then_inc(stored[i], 16)
            for i in range(2):
                sp.wait_ge(stored[i], 8 * B)

        @block.scalar
        def _(act):
            act.wait_ge(tail_in, 32)
            nc.scalar.activation(gt[:, 1:2], gt[:, 0:1], ACT.Exp, scale=-1.0).then_inc(g_exp, 1)

            def op(h, src, dst, func, after, k):
                act.wait_ge(step[h], after)
                part = slice(h * HB, (h + 1) * HB)
                nc.scalar.activation(dst[:, part, :], src[:, part, :], func).then_inc(logs[h], 1)

            for k, (src, dst, func, after) in enumerate(((tmp, mat, ACT.Exp, 2), (red, lra, ACT.Ln, 3),
                                                         (tmp, mat, ACT.Exp, 6), (red, lcb, ACT.Ln, 7))):
                for h in range(2):
                    op(h, src, dst, func, after, k)
            for h in range(2):
                op(h, logm, mat, ACT.Exp, FIRST, 0)
            with act.Fori(0, BLOCKS) as n:
                for src, dst, func, after in ((ra, lra, ACT.Ln, BLOCK - 2), (cb, lcb, ACT.Ln, BLOCK - 2), (logm, mat, ACT.Exp, BLOCK)):
                    for h in range(2):
                        op(h, src, dst, func, FIRST + n * BLOCK + after, 0)

        @block.vector
        def _(dve):
            def grid(t, h):
                return t[:, h * HB:(h + 1) * HB, :].rearrange("p b (i j) -> p b i j", i=NS)

            def turned(t, h):
                return t[:, h * HB:(h + 1) * HB, :].rearrange("p b (i j) -> p b j i", i=NS)

            def vec(t, h):
                return t[:, h * HB:(h + 1) * HB, :]

            def over_j(t, h):
                return vec(t, h).rearrange("p b (i o) -> p b i o", o=1).to_broadcast([P, HB, NS, NS])

            def over_i(t, h):
                return vec(t, h).rearrange("p b (o j) -> p b o j", o=1).to_broadcast([P, HB, NS, NS])

            def both(base, k, fn):
                for h in range(2):
                    if not (isinstance(base, int) and base + k == 1):
                        dve.wait_ge(step[h], base + k - 1)
                    fn(h).then_inc(step[h], 1)

            TT, RED = nc.vector.tensor_tensor, nc.vector.tensor_reduce
            dve.wait_ge(tail_in, 32)
            z = tail[:, :, 0:N2]
            def zg(h): return z[:, h * HB:(h + 1) * HB, :].rearrange("p b (i j) -> p b i j", i=NS)
            both(0, 1, lambda h: RED(vec(red, h), zg(h), AX.X, ALU.max))
            both(0, 2, lambda h: TT(grid(tmp, h), zg(h), over_j(red, h), ALU.subtract))
            for h in range(2):
                dve.wait_ge(logs[h], 1)
            both(0, 3, lambda h: RED(vec(red, h), grid(mat, h), AX.X, ALU.add))
            for h in range(2):
                dve.wait_ge(logs[h], 2)
            both(0, 4, lambda h: TT(grid(logm, h), grid(tmp, h), over_j(lra, h), ALU.subtract))
            both(0, 5, lambda h: RED(vec(red, h), turned(logm, h), AX.X, ALU.max))
            both(0, 6, lambda h: TT(grid(tmp, h), grid(logm, h), over_i(red, h), ALU.subtract))
            for h in range(2):
                dve.wait_ge(logs[h], 3)
            both(0, 7, lambda h: RED(vec(red, h), turned(mat, h), AX.X, ALU.add))
            for h in range(2):
                dve.wait_ge(logs[h], 4)
            both(0, 8, lambda h: TT(grid(logm, h), grid(tmp, h), over_i(lcb, h), ALU.subtract))

            with dve.Fori(0, BLOCKS) as n:
                base = FIRST + n * BLOCK
                for h in range(2):
                    dve.wait_ge(logs[h], LFIRST + 1 + n * LBLOCK)
                both(base, 1, lambda h: nc.vector.memset(vec(cb, h), 1.0))
                for i in range(ITERS):
                    k = 1 + 6 * i
                    both(base, k + 1, lambda h: TT(grid(tmp, h), grid(mat, h), over_i(cb, h), ALU.mult))
                    both(base, k + 2, lambda h: RED(vec(red, h), grid(tmp, h), AX.X, ALU.add))
                    both(base, k + 3, lambda h: nc.vector.reciprocal(vec(ra, h), vec(red, h)))
                    both(base, k + 4, lambda h: TT(grid(tmp, h), grid(mat, h), over_j(ra, h), ALU.mult))
                    both(base, k + 5, lambda h: RED(vec(red, h), turned(tmp, h), AX.X, ALU.add))
                    both(base, k + 6, lambda h: nc.vector.reciprocal(vec(cb, h), vec(red, h)))
                for h in range(2):
                    dve.wait_ge(logs[h], LFIRST + 1 + n * LBLOCK + 2)
                both(base, BLOCK - 1, lambda h: TT(grid(logm, h), grid(logm, h), over_j(lra, h), ALU.add))
                both(base, BLOCK, lambda h: TT(grid(logm, h), grid(logm, h), over_i(lcb, h), ALU.add))

            k = [0]

            def link(ins):
                k[0] += 1
                ins.then_inc(coef_step, 1)
                dve.wait_ge(coef_step, k[0])

            for h in range(2):
                dve.wait_ge(logs[h], LFIRST + 1 + BLOCKS * LBLOCK)
            dve.wait_ge(g_exp, 1)
            link(nc.vector.tensor_scalar(gt[:, 2:3], gt[:, 1:2], 1.0, None, ALU.add))
            link(nc.vector.reciprocal(gt[:, 3:4], gt[:, 2:3]))
            link(nc.vector.tensor_scalar(gt[:, 0:1], gt[:, 3:4], -1.0, 1.0, ALU.mult, ALU.add))
            link(nc.vector.tensor_scalar(coef[:, :, 0:N2], mat[:, :, :], gt[:, 3:4], None, ALU.mult))
            diag = coef[:, :, 0:N2:NS + 1]
            sd = tail[:, :, AT_SD - AT_RES:AT_SD - AT_RES + 1].to_broadcast([P, B, NS])
            link(nc.vector.scalar_tensor_tensor(diag, diag, gt[:, 0:1], sd, ALU.add, ALU.add))
            link(nc.vector.tensor_copy(coef[:, :, N2:N2 + NS + 1], tail[:, :, N2:N2 + NS + 1]))

            coef_v = coef[:, :, :].rearrange("p (u s) n -> p u s n", s=2)

            def mix(u, first):
                for s in range(2):
                    b = 2 * u
                    dve.wait_ge(row_in[s], 16 * u + 16)
                    nc.vector.tensor_copy(now[s][:], coef_v[:, u, s, :]).then_inc(now_done, 1)
                    dve.wait_ge(now_done, b + s + 1)
                    if not first:
                        dve.wait_ge(stored[s], 16 * u)
                    w, x, o = now[s], xr[s], ot[s]
                    for j in range(NS + 1):
                        for i in range(NS):
                            dst = o[:, i * C:(i + 1) * C]
                            if j == 0:
                                r = nc.vector.tensor_scalar(dst, x[:, 0:C], w[:, NS * i:NS * i + 1], w[:, N2 + NS:N2 + NS + 1], ALU.mult, ALU.add)
                            else:
                                at = NS * i + j if j < NS else N2 + i
                                dve.wait_ge(mix_step, 20 * (b + s) + 4 * (j - 1) + i + 1)
                                r = nc.vector.scalar_tensor_tensor(dst, x[:, j * C:(j + 1) * C], w[:, at:at + 1], dst, ALU.mult, ALU.add)
                            r.then_inc(mix_step, 1)

            mix(0, True)
            with dve.Fori(1, B // 2) as u:
                mix(u, False)


def dft_matrices():
    t = np.arange(T, dtype=np.float64)
    f = np.arange(T // 2, dtype=np.float64)
    H = T // 2
    even = 2 * np.pi * np.outer(t, f) / T
    odd = 2 * np.pi * np.outer(t, f + 0.5) / T
    a = np.concatenate([np.cos(even), -np.sin(even)], 1)
    a[:, H] = (-1.0) ** t
    b = np.concatenate([a[:, H:], a[:, :H]], 1)
    b[:, 0] = t == T - 1
    o = np.concatenate([np.cos(odd), -np.sin(odd)], 1)
    ov = o.copy()
    ov[T - 1] -= o.sum(0)
    ovb = np.concatenate([ov[:, H:], ov[:, :H]], 1)
    c1 = 2 / T * np.concatenate([np.cos(even).T, np.cos(even).T], 0)
    c1[0] = 1 / T
    c1[H] = (-1.0) ** t / T
    c2 = 2 / T * np.concatenate([np.sin(even).T, -np.sin(even).T], 0)
    o1 = -c2 / 2
    o1[0] = 0.5
    o2 = np.concatenate([np.cos(odd).T, np.cos(odd).T], 0) / T
    o3 = np.concatenate([-np.sin(odd).T, np.sin(odd).T], 0) / T
    return np.stack([a, b, ov, ovb, o, c1 / 2, o1, o2, o3, c1, c2], 1).astype(np.float32)


def build(nc, x, ctx, wq, wk, wv, wo, w24, base, wb, gate, ident, causal, rope, dft, out):
    x1 = nc.dram_tensor("x1", [B, T, D], F32).ap()
    rows = nc.dram_tensor("rows", [B, T, ROW], F32).ap()
    attention_phase(nc, x, wq, wk, wv, wo, ident, causal, rope, x1)
    autocorrelation_phase(nc, x1, ctx, ident, dft, w24, base, wb, rows)
    mixing_phase(nc, rows, gate, out)


def rope_tables():
    inv = (1.0 / 500000.0 ** (np.arange(0, HD, 2, dtype=np.float32) / np.float32(HD))).astype(np.float32)
    f = (np.arange(T, dtype=np.float32)[:, None] * inv[None, :]).astype(np.float64)
    c, s = np.cos(f), np.sin(f)
    cc, ss = np.concatenate([c, c], 1), np.concatenate([-s, s], 1)
    scale = 1.0 / np.sqrt(HD)
    return np.stack([cc * scale, ss * scale, cc, ss], 1).astype(np.float32)


def constants():
    eye = np.eye(P, dtype=np.float32)
    causal = np.where(np.arange(T)[None, :] > np.arange(T)[:, None], -1e30, 0.0)
    return {
        "ident": eye,
        "causal": causal.astype(np.float32),
        "rope": rope_tables(),
        "dft": dft_matrices(),
    }


_ORDER = ["x", "ctx", "wq", "wk", "wv", "wo", "w24", "base", "wb", "gate", "ident", "causal", "rope", "dft"]


def laid_out(inputs):
    w = np.concatenate([np.asarray(inputs["L0_ffn_W_" + n]) for n in ("res", "pre", "post")], 0)
    base = np.concatenate([np.asarray(inputs["L0_ffn_H_" + n + "_base"]).reshape(-1) for n in ("res", "pre", "post")])
    return {
        "x": inputs["x"], "ctx": inputs["ctx_4096"],
        "wq": inputs["L0_attn_Wq"], "wk": inputs["L0_attn_Wk"], "wv": inputs["L0_attn_Wv"], "wo": inputs["L0_attn_Wo"],
        "w24": w.T.reshape(KD, P, NLOG).transpose(1, 0, 2),
        "base": np.broadcast_to(base, (P, NLOG)),
        "wb": inputs["L0_ffn_W_branch"],
        "gate": np.broadcast_to(np.asarray(inputs["L0_ffn_gate"]), (P, 1)),
        **constants(),
    }


def kernel(**inputs):
    import concourse.bacc as bacc
    from concourse.bass_utils import run_bass_kernel_spmd

    nc = bacc.Bacc("TRN2", target_bir_lowering=False, num_devices=1)
    laid = laid_out(inputs)
    arrays, args = {}, []
    for name in _ORDER:
        a = np.ascontiguousarray(laid[name])
        arrays["in_" + name] = a
        args.append(nc.dram_tensor("in_" + name, a.shape, mybir.dt.from_np(a.dtype), kind="ExternalInput").ap())
    out = nc.dram_tensor("out", (B, T, D), F32, kind="ExternalOutput").ap()
    build(nc, *args, out)
    r = run_bass_kernel_spmd(nc, [arrays], core_ids=[0])
    return r.results[0]["out"]
```

```python
from contextlib import ExitStack

import numpy as np
import concourse.bass as bass
from concourse import mybir

P = 128
B = 16
T = 128
D = 1024
KD = D // P
HALF = 512
NH, NKV, HD = 32, 8, 32
GROUP = NH // NKV
KVW = NKV * HD
QKVW = D + 2 * KVW
STRIPS = P // HD
LN_EPS = 1e-5

NS = 4
C = D // NS
NLOG = NS * NS + 2 * NS
SINKHORN_ITERS = 50
TAU = 0.1
RMS_EPS = 1.1920929e-07
ROW = D + C
AT_POST = NS * NS
AT_MEAN = AT_POST + NS
AT_SD = AT_MEAN + 1
FACTS = AT_SD + 1
NEG = -3.0e38
FWD_A, FWD_ODD, INV_OUT, INV_CORR, N_DFT = 0, 4, 5, 9, 11

F32 = mybir.dt.float32
F32R = mybir.dt.float32r
BF16 = mybir.dt.bfloat16
ALU = mybir.AluOpType
ACT = mybir.ActivationFunctionType
AX = mybir.AxisListType


def attention_phase(nc, x, wq, wk, wv, wo, ident, causal, rope, x1):
    wo_v = wo.rearrange("(G s j d) n -> G j s d n", G=2, s=STRIPS, j=GROUP)

    with ExitStack() as ctx:
        def sb(name, shape, dt, stack=ctx):
            return stack.enter_context(nc.sbuf_tensor(name, shape, dt))

        def sem(name):
            return ctx.enter_context(nc.semaphore(name))

        w_hi = sb("w_hi", [P, KD, QKVW], F32R)
        w_lo = sb("w_lo", [P, KD, QKVW], F32R)
        wo_hi = sb("wo_hi", [P, KD, D], F32R)
        wo_lo = sb("wo_lo", [P, KD, D], F32R)
        idf = sb("idf", [P, P], F32)
        idb = sb("idb", [P, P], BF16)
        mask = sb("mask", [P, P], BF16)
        tab = sb("tab", [P, 4, HD], F32)
        xin = sb("xin", [P, D], F32)
        xT_hi = sb("xT_hi", [P, KD, T], F32R)
        xT_lo = sb("xT_lo", [P, KD, T], F32R)
        v_sb = sb("v_sb", [P, KVW], F32)
        qT = sb("qT", [P, 2, GROUP, T], F32)
        kT = sb("kT", [P, 2, T], F32)
        stats = sb("stats", [P, 2, 6], F32)
        mv = sb("mv", [P, 2], F32)
        veps = sb("veps", [P, 1], F32)
        rstd = sb("rstd", [P, 1], F32)
        mhalf = sb("mhalf", [P, 1], F32)
        pause = sb("pause", [P, 1], F32)
        negm = sb("negm", [P, NH], F32)
        lsum = sb("lsum", [P, NH], F32)
        rl = sb("rl", [P, NH], F32)
        with ExitStack() as shared:
            rc = sb("rc", [P, D + KVW], F32, shared)
            rs = sb("rs", [P, D + KVW], F32, shared)
        with ExitStack() as shared:
            prob = sb("prob", [P, 3, GROUP, T], F32, shared)
            pT = sb("pT", [P, 2, GROUP, T], F32, shared)
        sb("rc_prob_room", [P, 2 * (D + KVW)], F32)
        with ExitStack() as shared:
            w_stage = sb("w_stage", [P, 2, QKVW], F32, shared)
        aT_hi = sb("aT_hi", [P, 2, GROUP, T], F32R)
        aT_lo = sb("aT_lo", [P, 2, GROUP, T], F32R)
        with ExitStack() as shared:
            wo_stage = sb("wo_stage", [P, 2, HALF], F32, shared)
        xres = sb("xres", [P, D], F32)

        ps_qkv = ctx.enter_context(nc.psum_tensor("ps_qkv", [P, 3, HALF], F32))
        ps_s = ctx.enter_context(nc.psum_tensor("ps_s", [P, 2, HALF], F32))
        ps_t = ctx.enter_context(nc.psum_tensor("ps_t", [P, HALF], F32))
        ps_a = ctx.enter_context(nc.psum_tensor("ps_a", [P, 2, HALF], F32))

        const_in = sem("const_in")
        x_in = sem("x_in")
        w_in = [sem(f"w_in{i}") for i in range(2)]
        wo_in = [sem(f"wo_in{i}") for i in range(2)]
        xres_in = sem("xres_in")
        x1_out = sem("x1_out")
        mhalf_set = sem("mhalf_set")
        masks_done = sem("masks_done")
        w_hi_done = sem("w_hi_done")
        w_lo_done = sem("w_lo_done")
        wo_hi_done = sem("wo_hi_done")
        wo_lo_done = sem("wo_lo_done")
        stat_step = sem("stat_step")
        rstd_done = sem("rstd_done")
        xn_done = sem("xn_done")
        xT_ps = sem("xT_ps")
        xh_done = sem("xh_done")
        xl_done = sem("xl_done")
        qkv_ps = sem("qkv_ps")
        rope_done = sem("rope_done")
        v_done = sem("v_done")
        rsum_done = sem("rsum_done")
        qkT_ps = sem("qkT_ps")
        qkT_done = sem("qkT_done")
        s_ps = sem("s_ps")
        negm_done = sem("negm_done")
        e_done = sem("e_done")
        rl_done = sem("rl_done")
        p_done = sem("p_done")
        pT_ps = sem("pT_ps")
        pT_done = sem("pT_done")
        a_ps = sem("a_ps")
        ah_done = sem("ah_done")
        al_done = sem("al_done")
        o_ps = sem("o_ps")
        x1_done = sem("x1_done")

        block = ctx.enter_context(nc.Block())

        def iterations(engine, body):
            body(-2, attend=False, project=False, norm=True)
            body(-1, attend=False, project=True, norm=True)
            body(0, attend=True, project=True, norm=True, first=True)
            with engine.Fori(1, B - 2) as b:
                body(b, attend=True, project=True, norm=True)
            body(B - 2, attend=True, project=True, norm=False)
            body(B - 1, attend=True, project=False, norm=False)

        @block.sync
        def _(sp):
            sp.dma_start(xin[:], x[0]).then_inc(x_in, 16)
            sp.dma_start(idf[:], ident).then_inc(const_in, 16)
            sp.dma_start(kT[:, 0, :], causal).then_inc(const_in, 16)
            sp.dma_start(tab[:], rope).then_inc(const_in, 16)

            def body(b, attend, project, norm, first=False):
                if not attend and project:
                    for k in range(KD):
                        if k >= 2:
                            sp.wait_ge(w_hi_done, k - 1)
                            sp.wait_ge(w_lo_done, k - 1)
                        rows = slice(k * P, (k + 1) * P)
                        st = w_stage[:, k % 2, :]
                        sp.dma_start(st[:, 0:D], wq[rows, :]).then_inc(w_in[k % 2], 16)
                        sp.dma_start(st[:, D:D + KVW], wk[rows, :]).then_inc(w_in[k % 2], 16)
                        sp.dma_start(st[:, D + KVW:QKVW], wv[rows, :]).then_inc(w_in[k % 2], 16)
                if norm and (not isinstance(b, int) or b > -2):
                    sp.wait_ge(xT_ps, 2 * (b + 2))
                    sp.wait_ge(const_in, 48)
                    sp.dma_start(xin[:], x[b + 2]).then_inc(x_in, 16)
                if attend:
                    if first:
                        sp.wait_ge(w_hi_done, KD)
                        sp.wait_ge(w_lo_done, KD)
                        for n in range(2 * KD):
                            if n >= 2:
                                sp.wait_ge(wo_hi_done, n - 1)
                                sp.wait_ge(wo_lo_done, n - 1)
                            c, half = n // 2, n % 2
                            for s in range(STRIPS):
                                sp.dma_start(wo_stage[s * HD:(s + 1) * HD, n % 2, :],
                                             wo_v[c // GROUP, c % GROUP, s, :, half * HALF:(half + 1) * HALF]
                                             ).then_inc(wo_in[n % 2], 16)
                        sp.wait_ge(wo_hi_done, 2 * KD)
                        sp.wait_ge(wo_lo_done, 2 * KD)
                    else:
                        sp.wait_ge(x1_out, 16 * b)
                    sp.wait_ge(const_in, 48)
                    sp.dma_start(xres[:], x[b]).then_inc(xres_in, 16)
                    sp.wait_ge(x1_done, 2 * b + 2)
                    sp.wait_ge(const_in, 48)
                    sp.dma_start(x1[b], xres[:]).then_inc(x1_out, 16)

            iterations(sp, body)
            sp.wait_ge(x1_out, 16 * B)

        @block.tensor
        def _(pe):
            def body(b, attend, project, norm, first=False):
                def scores(g):
                    G, s = g // STRIPS, g % STRIPS
                    if g == 0:
                        pe.wait_ge(qkT_done, 3 * (b + 1))
                    if g < 2:
                        if not first:
                            pe.wait_ge(x1_done, 2 * b - 1 + g)
                    else:
                        pe.wait_ge(e_done, 8 * b + g - 1)
                    nc.tensor.matmul(ps_s[:, g % 2, :], idb[:], mask[:].rearrange("p (a k) -> p a k", a=1).to_broadcast([P, GROUP, P]),
                                     start=True, stop=False)
                    lanes = slice(s * HD, (s + 1) * HD)
                    for j in range(GROUP):
                        last = nc.tensor.matmul(ps_s[:, g % 2, j * T:(j + 1) * T], qT[lanes, G, j, :],
                                                kT[lanes, G, :], start=False, stop=j == GROUP - 1)
                    last.then_inc(s_ps, 1)

                def project_chunk(k):
                    if k == 0:
                        pe.wait_ge(xh_done, 2 * (b + 1) + 2)
                        pe.wait_ge(xl_done, 2 * (b + 1) + 2)
                        if attend:
                            pe.wait_ge(rope_done, 3 * (b + 1))
                            pe.wait_ge(v_done, b + 1)
                    if not attend:
                        pe.wait_ge(w_hi_done, k + 1)
                        pe.wait_ge(w_lo_done, k + 1)
                    for n in range(3):
                        cols = slice(n * HALF, (n + 1) * HALF)
                        nc.tensor.matmul(ps_qkv[:, n, :], xT_hi[:, k, :], w_hi[:, k, cols], start=k == 0, stop=False)
                        nc.tensor.matmul(ps_qkv[:, n, :], xT_hi[:, k, :], w_lo[:, k, cols], start=False, stop=False)
                    for n in range(3):
                        cols = slice(n * HALF, (n + 1) * HALF)
                        last = nc.tensor.matmul(ps_qkv[:, n, :], xT_lo[:, k, :], w_hi[:, k, cols],
                                                start=False, stop=k == KD - 1)
                    if k == KD - 1:
                        last.then_inc(qkv_ps, 1)

                def prob_transpose(g):
                    pe.wait_ge(p_done, 8 * b + g + 1)
                    if g > 0:
                        pe.wait_ge(pT_done, 8 * b + g)
                    for j in range(GROUP):
                        last = nc.tensor.transpose(ps_t[:, j * T:(j + 1) * T], prob[:, g % 3, j, :], idf[:])
                    last.then_inc(pT_ps, 1)

                def weigh_values(g):
                    G, s = g // STRIPS, g % STRIPS
                    pe.wait_ge(pT_done, 8 * b + g + 1)
                    last = nc.tensor.matmul(ps_a[s * HD:(s + 1) * HD, G, :], v_sb[:, g * HD:(g + 1) * HD],
                                            pT[:, g % 2, :, :], start=True, stop=True)
                    if s == STRIPS - 1:
                        last.then_inc(a_ps, 1)

                def x_transpose(half):
                    c = b + 2
                    if half == 0:
                        pe.wait_ge(xn_done, c + 1)
                        if attend:
                            pe.wait_ge(pT_done, 8 * b + 8)
                        elif project:
                            pe.wait_ge(xh_done, 2 * c)
                            pe.wait_ge(xl_done, 2 * c)
                    else:
                        pe.wait_ge(xh_done, 2 * c + 1)
                        pe.wait_ge(xl_done, 2 * c + 1)
                    for i in range(4):
                        k = 4 * half + i
                        last = nc.tensor.transpose(ps_t[:, i * T:(i + 1) * T], xin[:, k * P:(k + 1) * P], idf[:])
                    last.then_inc(xT_ps, 1)

                def qk_transpose():
                    for G in range(2):
                        pe.wait_ge(rsum_done, 3 * (b + 1) + G + 1)
                        if attend and G == 0:
                            pe.wait_ge(ah_done, 2 * b + 2)
                            pe.wait_ge(al_done, 2 * b + 2)
                        for j in range(GROUP):
                            last = nc.tensor.transpose(ps_a[:, G, j * T:(j + 1) * T], rc[:, G * HALF + j * P:G * HALF + (j + 1) * P], idf[:])
                        last.then_inc(qkT_ps, 1)
                    pe.wait_ge(rsum_done, 3 * (b + 1) + 3)
                    if norm:
                        pe.wait_ge(xh_done, 2 * (b + 2) + 2)
                        pe.wait_ge(xl_done, 2 * (b + 2) + 2)
                    for G in range(2):
                        last = nc.tensor.transpose(ps_t[:, G * T:(G + 1) * T], rc[:, D + G * P:D + (G + 1) * P], idf[:])
                    last.then_inc(qkT_ps, 1)

                def output_chunk(G, j, halves):
                    c = G * GROUP + j
                    if j == 0 and halves[0] == 0:
                        pe.wait_ge(ah_done, 2 * b + G + 1)
                        pe.wait_ge(al_done, 2 * b + G + 1)
                        if first and G == 0:
                            pe.wait_ge(wo_hi_done, 2 * KD)
                            pe.wait_ge(wo_lo_done, 2 * KD)
                    for left, right in ((aT_hi, wo_hi), (aT_hi, wo_lo), (aT_lo, wo_hi)):
                        for n in halves:
                            last = nc.tensor.matmul(ps_s[:, n, :], left[:, G, j, :], right[:, c, n * HALF:(n + 1) * HALF],
                                                    start=c == 0 and left is aT_hi and right is wo_hi,
                                                    stop=c == KD - 1 and left is aT_lo)
                    if c == KD - 1:
                        last.then_inc(o_ps, 1)

                if attend:
                    scores(0)
                    scores(1)
                for g in range(NKV):
                    if project:
                        project_chunk(g)
                    if attend:
                        prob_transpose(g)
                        if g + 2 < NKV:
                            scores(g + 2)
                        if g > 0:
                            weigh_values(g - 1)
                if attend:
                    weigh_values(NKV - 1)
                if norm:
                    x_transpose(0)
                if attend:
                    pe.wait_ge(e_done, 8 * b + 8)
                    for j in range(GROUP):
                        output_chunk(0, j, (0, 1))
                if norm:
                    x_transpose(1)
                if attend:
                    for j in range(GROUP):
                        output_chunk(1, j, (0,))
                if project:
                    qk_transpose()
                if attend:
                    for j in range(GROUP):
                        output_chunk(1, j, (1,))

            pe.wait_ge(const_in, 48)
            pe.wait_ge(masks_done, 2)
            iterations(pe, body)

        @block.scalar
        def _(act):
            act.wait_ge(const_in, 48)
            nc.scalar.activation(idb[:], idf[:], ACT.Copy).then_inc(masks_done, 1)
            nc.scalar.activation(mask[:], kT[:, 0, :], ACT.Copy).then_inc(masks_done, 1)

            def body(b, attend, project, norm, first=False):
                if project and not attend:
                    for k in range(KD):
                        act.wait_ge(w_in[k % 2], 48 * (k // 2 + 1))
                        nc.scalar.activation(w_hi[:, k, :], w_stage[:, k % 2, :], ACT.Copy).then_inc(w_hi_done, 1)

                def attend_out(G):
                    act.wait_ge(a_ps, 2 * b + G + 1)
                    if not first:
                        act.wait_ge(o_ps, 2 * b)
                    nc.scalar.activation(aT_hi[:, G, :, :], ps_a[:, G, :], ACT.Copy).then_inc(ah_done, 1)

                if attend:
                    for g in range(NKV):
                        act.wait_ge(negm_done, 8 * b + g + 1)
                        if g >= 3:
                            act.wait_ge(pT_ps, 8 * b + g - 2)
                        for j in range(GROUP):
                            h = g * GROUP + j
                            last = nc.scalar.activation(prob[:, g % 3, j, :], ps_s[:, g % 2, j * T:(j + 1) * T], ACT.Exp,
                                                        bias=negm[:, h:h + 1], accum_out=lsum[:, h:h + 1])
                        last.then_inc(e_done, 1)
                        if first:
                            for half in range(2):
                                n = 2 * g + half
                                act.wait_ge(wo_in[half], 64 * (g + 1))
                                nc.scalar.activation(wo_hi[:, g, half * HALF:(half + 1) * HALF], wo_stage[:, half, :],
                                                     ACT.Copy).then_inc(wo_hi_done, 1)
                        if g == 5:
                            attend_out(0)
                if project:
                    act.wait_ge(qkv_ps, b + 2)
                    if attend:
                        act.wait_ge(a_ps, 2 * b + 2)
                    nc.scalar.activation(v_sb[:], ps_qkv[:, 2, KVW:2 * KVW], ACT.Copy).then_inc(v_done, 1)
                if attend:
                    attend_out(1)
                if norm:
                    for half in range(2):
                        act.wait_ge(xT_ps, 2 * (b + 2) + half + 1)
                        if project:
                            act.wait_ge(qkv_ps, b + 2)
                        nc.scalar.activation(xT_hi[:, 4 * half:4 * half + 4, :], ps_t[:], ACT.Copy).then_inc(xh_done, 1)
                if project:
                    if attend:
                        act.wait_ge(s_ps, 8 * b + 8)
                    for G in range(2):
                        act.wait_ge(qkT_ps, 3 * (b + 1) + G + 1)
                        nc.scalar.activation(qT[:, G, :, :], ps_a[:, G, :], ACT.Copy).then_inc(qkT_done, 1)
                    act.wait_ge(qkT_ps, 3 * (b + 1) + 3)
                    nc.scalar.activation(kT[:, :, :], ps_t[:, 0:2 * T], ACT.Copy).then_inc(qkT_done, 1)

            iterations(act, body)

        @block.vector
        def _(dve):
            def row_negm(b, g):
                dve.wait_ge(s_ps, 8 * b + g + 1)
                nc.vector.tensor_reduce(negm[:, g * GROUP:(g + 1) * GROUP],
                                        ps_s[:, g % 2, :].rearrange("p (j k) -> p j k", j=GROUP),
                                        AX.X, ALU.max, negate=True).then_inc(negm_done, 1)

            def body(b, attend, project, norm, first=False):
                c = b + 2

                def norm_stats():
                    dve.wait_ge(x_in, 16 * (c + 1))
                    for i in range(2):
                        nc.vector.bn_stats(stats[:, i, :], xin[:, i * HALF:(i + 1) * HALF]).then_inc(stat_step, 1)
                    dve.wait_ge(stat_step, 4 * c + 2)
                    nc.vector.memset(pause[:], 0.0)
                    nc.vector.bn_aggr(mv[:], stats[:, :, :]).then_inc(stat_step, 1)
                    dve.wait_ge(stat_step, 4 * c + 3)
                    nc.vector.tensor_scalar(veps[:], mv[:, 1:2], LN_EPS, None, ALU.add).then_inc(stat_step, 1)

                def norm_apply():
                    dve.wait_ge(rstd_done, c + 1)
                    nc.vector.tensor_scalar(xin[:], xin[:], mv[:, 0:1], rstd[:], ALU.subtract, ALU.mult).then_inc(xn_done, 1)

                def attend_out(G):
                    dve.wait_ge(ah_done, 2 * b + G + 1)
                    nc.vector.tensor_tensor(aT_lo[:, G, :, :], ps_a[:, G, :].rearrange("p (j t) -> p j t", j=GROUP),
                                            aT_hi[:, G, :, :].bitcast(F32), ALU.subtract).then_inc(al_done, 1)

                def x_lo(half):
                    dve.wait_ge(xh_done, 2 * c + half + 1)
                    nc.vector.tensor_tensor(xT_lo[:, 4 * half:4 * half + 4, :], ps_t[:].rearrange("p (k t) -> p k t", k=4),
                                            xT_hi[:, 4 * half:4 * half + 4, :].bitcast(F32),
                                            ALU.subtract).then_inc(xl_done, 1)

                def rope_bank(n):
                    a, c = (STRIPS, GROUP) if n < 2 else (1, NKV)
                    w = a * c * HD
                    t = 0 if n < 2 else 2
                    at = slice(n * HALF, n * HALF + w)
                    src = ps_qkv[:, n, 0:w].rearrange("p (a c i) -> p a c i", a=a, c=c)
                    by_cos = rc[:, at].rearrange("p (c a i) -> p a c i", a=a, c=c)
                    by_sin = rs[:, at].rearrange("p (c a i) -> p a c i", a=a, c=c)
                    cos = tab[:, t:t + 1, :].rearrange("p o (r i) -> p o r i", r=1)
                    sin = tab[:, t + 1:t + 2, :].rearrange("p o (r i) -> p o r i", r=1)
                    nc.vector.tensor_tensor(by_cos, src, cos.to_broadcast([P, a, c, HD]), ALU.mult)
                    for lo, hi in ((0, HD // 2), (HD // 2, 0)):
                        to, of = slice(lo, lo + HD // 2), slice(hi, hi + HD // 2)
                        last = nc.vector.tensor_tensor(by_sin[:, :, :, to], src[:, :, :, of],
                                                       sin[:, :, :, to].to_broadcast([P, a, c, HD // 2]), ALU.mult)
                    last.then_inc(rope_done, 1)

                if project and not attend:
                    for k in range(KD):
                        dve.wait_ge(w_hi_done, k + 1)
                        nc.vector.tensor_tensor(w_lo[:, k, :], w_stage[:, k % 2, :], w_hi[:, k, :].bitcast(F32),
                                                ALU.subtract).then_inc(w_lo_done, 1)
                if attend:
                    row_negm(b, 0)
                    row_negm(b, 1)
                    for g in range(NKV):
                        dve.wait_ge(e_done, 8 * b + g + 1)
                        hs = slice(g * GROUP, (g + 1) * GROUP)
                        nc.vector.reciprocal(rl[:, hs], lsum[:, hs]).then_inc(rl_done, 1)
                        if first:
                            for half in range(2):
                                n = 2 * g + half
                                dve.wait_ge(wo_hi_done, n + 1)
                                cols = slice(half * HALF, (half + 1) * HALF)
                                nc.vector.tensor_tensor(wo_lo[:, g, cols], wo_stage[:, half, :],
                                                        wo_hi[:, g, cols].bitcast(F32), ALU.subtract).then_inc(wo_lo_done, 1)
                        dve.wait_ge(pT_ps, 8 * b + g + 1)
                        nc.vector.tensor_copy(pT[:, g % 2, :, :], ps_t[:].rearrange("p (j t) -> p j t", j=GROUP)).then_inc(pT_done, 1)
                        if g + 2 < NKV:
                            row_negm(b, g + 2)
                        if norm and g == 1:
                            norm_stats()
                        if norm and g == 4:
                            norm_apply()
                        if g == 5:
                            attend_out(0)
                elif norm:
                    norm_stats()
                    norm_apply()
                if project:
                    dve.wait_ge(qkv_ps, b + 2)
                    if attend:
                        dve.wait_ge(a_ps, 2 * b + 2)
                    rope_bank(0)
                if attend:
                    attend_out(1)
                if norm:
                    x_lo(0)
                if project:
                    rope_bank(1)
                    rope_bank(2)
                if norm:
                    x_lo(1)
                if attend:
                    dve.wait_ge(xres_in, 16 * (b + 1))
                    for n in range(2):
                        cols = slice(n * HALF, (n + 1) * HALF)
                        dve.wait_ge(o_ps, 2 * b + n + 1)
                        nc.vector.tensor_tensor(xres[:, cols], ps_s[:, n, :], xres[:, cols], ALU.add).then_inc(x1_done, 1)

            dve.wait_ge(const_in, 48)
            iterations(dve, body)

        @block.gpsimd
        def _(pool):
            nc.gpsimd.memset(mhalf[:], -0.5).then_inc(mhalf_set, 1)
            pool.wait_ge(mhalf_set, 1)

            def body(b, attend, project, norm, first=False):
                def norm_rstd():
                    pool.wait_ge(stat_step, 4 * (b + 2) + 4)
                    nc.gpsimd.tensor_tensor(rstd[:], veps[:], mhalf[:], ALU.pow).then_inc(rstd_done, 1)

                if attend:
                    for g in range(NKV):
                        pool.wait_ge(rl_done, 8 * b + g + 1)
                        nc.gpsimd.tensor_tensor(prob[:, g % 3, :, :], prob[:, g % 3, :, :],
                                                rl[:, g * GROUP:(g + 1) * GROUP].rearrange("p (j o) -> p j o", o=1).to_broadcast([P, GROUP, T]),
                                                ALU.mult).then_inc(p_done, 1)
                        if norm and g == 2:
                            norm_rstd()
                elif norm:
                    norm_rstd()
                if project:
                    for n in range(3):
                        at = slice(n * HALF, min((n + 1) * HALF, D + KVW))
                        pool.wait_ge(rope_done, 3 * (b + 1) + n + 1)
                        nc.gpsimd.tensor_tensor(rc[:, at], rc[:, at], rs[:, at], ALU.add).then_inc(rsum_done, 1)

            iterations(pool, body)


def autocorrelation_phase(nc, x1, ctx_in, ident, dft, w24, base, wb, facts, rows):
    with ExitStack() as ctx:
        def sb(name, shape, dt=F32):
            return ctx.enter_context(nc.sbuf_tensor("c_" + name, shape, dt))

        def sem(name):
            return ctx.enter_context(nc.semaphore("c_" + name))

        idf = sb("b_idf", [P, P])
        mats = sb("mats", [P, N_DFT, P])
        fwd_hi = sb("fwd_hi", [P, 4, P], F32R)
        fwd_lo = sb("fwd_lo", [P, 4, P], F32R)
        w24_sb = sb("w24_sb", [P, KD, NLOG])
        base_sb = sb("base_sb", [P, NLOG])
        wb_sb = sb("wb_sb", [P, 2, C])
        xin = sb("xin", [P, D])
        xn = sb("xn", [P, D])
        xres = sb("b_xres", [P, D])
        cin = sb("cin", [P, D])
        c_hi = [sb(f"c_hi{i}", [P, D], F32R) for i in range(2)]
        c_lo = [sb(f"c_lo{i}", [P, D], F32R) for i in range(2)]
        spec = [[sb(f"spec{i}{n}", [P, D]) for n in range(4)] for i in range(2)]
        row = [sb(f"row{i}", [P, ROW]) for i in range(2)]
        tq = [sb(f"tq{i}", [P, D]) for i in range(2)]
        tw = [sb(f"tw{i}", [P, D]) for i in range(4)]
        pause = sb("pause", [P, 4])
        top = sb("top", [P, KD, 8])
        ntop = sb("ntop", [P, KD])
        corr = sb("corr", [P, KD, T])
        rest = sb("rest", [P, KD, T])
        ninth = sb("ninth", [P, KD])
        ex = sb("ex", [P, KD, T])
        wgt = sb("wgt", [P, KD, T])
        wsum = sb("wsum", [P, KD])
        wrec = sb("wrec", [P, KD])
        wT = sb("wT", [P, D])
        x2 = sb("x2", [P, D])
        x3T = sb("x3T", [P, KD, T])
        xp = sb("xp", [P, C])
        xpT = sb("xpT", [P, 2, T])
        st2 = sb("st2", [P, 2, 6])
        mv2 = sb("mv2", [P, 2])
        ve2 = sb("ve2", [P, 1])
        rstd2 = sb("rstd2", [P, 1])
        st3 = sb("st3", [P, 2, 6])
        mv3 = sb("mv3", [P, 2])
        ve3 = sb("ve3", [P, 1])
        rstd3 = sb("rstd3", [P, 1])
        nb2 = sb("nb2", [P, 2])
        nb3 = sb("nb3", [P, 2])
        ms = sb("ms", [P, 3])
        rs = sb("rs", [P, 1])
        consts = sb("consts", [P, 4])
        mhalf, one, rms_eps, minus = (consts[:, i:i + 1] for i in range(4))
        lg = sb("lg", [P, NLOG])
        hx = sb("hx", [P, 2])
        hd = sb("hd", [P, 2, NS])
        he = sb("he", [P, 2, NS])
        hs = sb("hs", [P, 2])
        hr = sb("hr", [P, 2])
        hp = sb("hp", [P, NS])

        pair = [ctx.enter_context(nc.psum_tensor(f"pair{i}", [P, 2, HALF], F32)) for i in range(4)]
        p_a, p_b, p_c, p_d = pair
        flat = [p[:, :, :].rearrange("p a n -> p (a n)") for p in pair]
        f_a, f_b, f_c, f_d = flat
        logits = p_d[:, 0, 0:NLOG]
        y_ps_at = p_d[:, 0, C:2 * C]
        xpT_at = p_d[:, 1, 0:2 * T]

        const_in = sem("const_in"); fwd_hi_done = sem("fwd_hi_done"); fwd_lo_done = sem("fwd_lo_done")
        consts_set = sem("consts_set")
        x_in = sem("x_in"); xres_in = sem("xres_in"); cin_in = sem("cin_in")
        row_out = [sem(f"row_out{i}") for i in range(2)]
        n2_step = sem("n2_step"); rstd2_done = sem("rstd2_done"); nb2_step = sem("nb2_step"); xn_done = sem("xn_done")
        chi_done = sem("chi_done"); clo_done = sem("clo_done")
        k_ps = sem("k_ps"); k_done = sem("k_done"); v_ps = sem("v_ps"); v_done = sem("v_done")
        q_ps = sem("q_ps"); tq_done = sem("tq_done"); corr_ps = sem("corr_ps"); corr_done = sem("corr_done")
        max_done = sem("max_done"); ntop_done = sem("ntop_done"); rest_done = sem("rest_done")
        ninth_done = sem("ninth_done"); exp_done = sem("exp_done"); pick_done = sem("pick_done")
        wrec_done = sem("wrec_done"); w_done = sem("w_done")
        wT_ps = sem("wT_ps"); wT_done = sem("wT_done"); ws_ps = sem("ws_ps"); tw_done = sem("tw_done")
        out_ps = sem("out_ps"); x2_done = sem("x2_done"); n3_step = sem("n3_step"); rstd3_done = sem("rstd3_done")
        x3_done = sem("x3_done"); x3T_ps = sem("x3T_ps"); x3T_done = sem("x3T_done"); lg_ps = sem("lg_ps")
        pool_step = sem("pool_step"); rs_done = sem("rs_done"); h_step = sem("h_step"); he_done = sem("he_done")
        xp_step = sem("xp_step"); xpT_ps = sem("xpT_ps"); xpT_done = sem("xpT_done"); y_ps = sem("y_ps")
        y_done = sem("y_done")
        N3, PS, HS, XS = 4, 7, 8, 4

        block = ctx.enter_context(nc.Block())

        def iterations(engine, body):
            body(-1, 1, near=True, far=False, last=False, tail=False, ahead=True)
            body(0, 0, near=True, far=True, last=False, tail=False, ahead=True)
            body(1, 1, near=True, far=True, last=True, tail=False, ahead=True)
            body(2, 0, near=True, far=True, last=True, tail=True, ahead=True)
            with engine.Fori(0, (B - 6) // 2) as u:
                body(2 * u + 3, 1, near=True, far=True, last=True, tail=True, ahead=True)
                body(2 * u + 4, 0, near=True, far=True, last=True, tail=True, ahead=True)
            body(B - 3, 1, near=True, far=True, last=True, tail=True, ahead=True)
            body(B - 2, 0, near=True, far=True, last=True, tail=True, ahead=False)
            body(B - 1, 1, near=False, far=True, last=True, tail=True, ahead=False)
            body(B, 0, near=False, far=False, last=True, tail=True, ahead=False)
            body(B + 1, 1, near=False, far=False, last=False, tail=True, ahead=False)

        def later(b, first):
            return not isinstance(b, int) or b > first

        def turns(n, par):
            return n // 2 if isinstance(n, int) else (n - par) // 2

        facts_v = facts[:, :, :].rearrange("p (u s) n -> p u s n", s=2)

        def fact(n, par, at, width):
            return facts_v[:, turns(n, par), par, at:at + width]

        @block.sync
        def _(sp):
            sp.dma_start(cin[:], ctx_in[0]).then_inc(cin_in, 16)
            sp.dma_start(mats[:], dft).then_inc(const_in, 16)
            sp.dma_start(xin[:], x1[0]).then_inc(x_in, 16)
            sp.dma_start(idf[:], ident).then_inc(const_in, 16)
            sp.dma_start(w24_sb[:], w24).then_inc(const_in, 16)
            sp.dma_start(base_sb[:], base).then_inc(const_in, 16)
            sp.dma_start(wb_sb[:], wb.rearrange("(k p) n -> p k n", k=2)).then_inc(const_in, 16)

            def body(b, par, near, far, last, tail, ahead):
                if tail:
                    sp.wait_ge(y_done, b - 1)
                    sp.dma_start(rows[b - 2], row[par][:]).then_inc(row_out[par], 16)
                if ahead:
                    sp.wait_ge(chi_done, b + 2)
                    sp.wait_ge(clo_done, b + 2)
                    sp.dma_start(cin[:], ctx_in[b + 2]).then_inc(cin_in, 16)
                    sp.wait_ge(xn_done, b + 2)
                    sp.dma_start(xin[:], x1[b + 2]).then_inc(x_in, 16)
                if far:
                    if near or last:
                        if later(b, 0):
                            sp.wait_ge(x2_done, 2 * b)
                    sp.dma_start(xres[:], x1[b]).then_inc(xres_in, 16)

            iterations(sp, body)
            for i in range(2):
                sp.wait_ge(row_out[i], 8 * B)

        @block.tensor
        def _(pe):
            def split3(dst, i, par):
                for n in range(2):
                    cols = slice(n * HALF, (n + 1) * HALF)
                    nc.tensor.matmul(dst[:, n, :], fwd_hi[:, i, :], c_hi[par][:, cols], start=True, stop=False)
                    nc.tensor.matmul(dst[:, n, :], fwd_hi[:, i, :], c_lo[par][:, cols], start=False, stop=False)
                    r = nc.tensor.matmul(dst[:, n, :], fwd_lo[:, i, :], c_hi[par][:, cols], start=False, stop=True)
                return r

            def spectrum(dst, i, src):
                for n in range(2):
                    r = nc.tensor.matmul(dst[:, n, :], mats[:, i, :], src[:, n * HALF:(n + 1) * HALF], start=True, stop=True)
                return r

            def out_half(n):
                for i in range(4):
                    r = nc.tensor.matmul(p_b[:, n, :], mats[:, INV_OUT + i, :], tw[i][:, n * HALF:(n + 1) * HALF],
                                         start=i == 0, stop=i == 3)
                r.then_inc(out_ps, 1)

            def body(b, par, near, far, last, tail, ahead):
                c = b + 1
                if near:
                    pe.wait_ge(xn_done, c + 1)
                    if far:
                        pe.wait_ge(v_done, 2 * b + 1)
                    spectrum(p_a, FWD_A, xn).then_inc(q_ps, 1)
                if tail:
                    pe.wait_ge(xp_step, XS * (b - 1))
                    pe.wait_ge(x3T_done, 2 * (b - 1))
                    for i in range(2):
                        r = nc.tensor.transpose(xpT_at[:, i * T:(i + 1) * T], xp[:, i * P:(i + 1) * P], idf[:])
                    r.then_inc(xpT_ps, 1)
                if near:
                    pe.wait_ge(chi_done, c + 1)
                    pe.wait_ge(clo_done, c + 1)
                    if last:
                        pe.wait_ge(x2_done, 2 * b)
                    split3(p_b, 0, 1 - par).then_inc(k_ps, 1)
                if tail:
                    pe.wait_ge(xpT_done, b - 1)
                    for i in range(2):
                        r = nc.tensor.matmul(y_ps_at, xpT[:, i, :], wb_sb[:, i, :], start=i == 0, stop=i == 1)
                    r.then_inc(y_ps, 1)
                    pe.wait_ge(y_done, b - 1)
                if far:
                    pe.wait_ge(w_done, b + 1)
                    for i in range(KD):
                        r = nc.tensor.transpose(f_d[:, i * T:(i + 1) * T], wgt[:, i, :], idf[:])
                    r.then_inc(wT_ps, 1)
                if near:
                    if far:
                        pe.wait_ge(v_done, 2 * b + 2)
                    split3(p_c, 1, 1 - par).then_inc(k_ps, 1)
                if far:
                    pe.wait_ge(wT_done, 2 * b + 2)
                    if near:
                        pe.wait_ge(k_done, 2 * c + 1)
                    else:
                        pe.wait_ge(x2_done, 2 * b)
                        pe.wait_ge(v_done, 2 * b + 2)
                    spectrum(p_b, FWD_A, wT).then_inc(ws_ps, 1)
                    if near:
                        pe.wait_ge(k_done, 2 * c + 2)
                    spectrum(p_c, FWD_ODD, wT).then_inc(ws_ps, 1)
                if near:
                    for n in range(2):
                        pe.wait_ge(tq_done, 2 * c + 2)
                        for i in range(4 * n, 4 * n + 4):
                            for t in range(2):
                                r = nc.tensor.matmul(f_a[:, i * T:(i + 1) * T], tq[t][:, i * P:(i + 1) * P], mats[:, INV_CORR + t, :],
                                                     start=t == 0, stop=t == 1)
                        r.then_inc(corr_ps, 1)
                if last:
                    pe.wait_ge(x3_done, b)
                    for i in range(KD):
                        r = nc.tensor.transpose(f_d[:, i * T:(i + 1) * T], row[1 - par][:, i * P:(i + 1) * P], idf[:])
                        if i % 4 == 3:
                            r.then_inc(x3T_ps, 1)
                if far:
                    pe.wait_ge(tw_done, 4 * b + 4)
                    out_half(0)
                if last:
                    pe.wait_ge(x3T_done, 2 * b)
                    for i in range(KD):
                        r = nc.tensor.matmul(logits, x3T[:, i, :], w24_sb[:, i, :], start=i == 0, stop=i == KD - 1)
                    r.then_inc(lg_ps, 1)
                if far:
                    out_half(1)
                if near:
                    pe.wait_ge(corr_done, 2 * c + 2)
                    split3(p_a, 2, 1 - par).then_inc(v_ps, 1)
                    split3(p_c, 3, 1 - par).then_inc(v_ps, 1)

            pe.wait_ge(const_in, 80)
            pe.wait_ge(fwd_hi_done, 1)
            pe.wait_ge(fwd_lo_done, 1)
            iterations(pe, body)

        @block.scalar
        def _(act):
            act.wait_ge(const_in, 80)
            nc.scalar.activation(fwd_hi[:, :, :], mats[:, 0:4, :], ACT.Copy).then_inc(fwd_hi_done, 1)

            def split_context(n, par):
                act.wait_ge(cin_in, 16 * (n + 1))
                if later(n, 1):
                    act.wait_ge(v_ps, 2 * (n - 1))
                nc.scalar.activation(c_hi[par][:], cin[:], ACT.Copy).then_inc(chi_done, 1)

            def normalise(n):
                act.wait_ge(nb2_step, 2 * (n + 1))
                if later(n, 0):
                    act.wait_ge(q_ps, n)
                nc.scalar.activation(xn[:], xin[:], ACT.Identity, bias=nb2[:, 1:2], scale=rstd2[:]).then_inc(xn_done, 1)

            split_context(0, 0)
            normalise(0)

            def body(b, par, near, far, last, tail, ahead):
                c = b + 1

                def key_spectrum(i, src):
                    act.wait_ge(k_ps, 2 * c + i + 1)
                    if last:
                        act.wait_ge(tw_done, 4 * b)
                    nc.scalar.activation(spec[1 - par][i][:], src, ACT.Copy).then_inc(k_done, 1)

                if tail:
                    act.wait_ge(xpT_ps, b - 1)
                    nc.scalar.activation(xpT[:, :, :], xpT_at, ACT.Copy).then_inc(xpT_done, 1)
                if near:
                    key_spectrum(0, f_b)
                if tail:
                    act.wait_ge(y_ps, b - 1)
                    nc.scalar.activation(row[par][:, D:D + C], y_ps_at, ACT.Copy).then_inc(y_done, 1)
                if far:
                    act.wait_ge(wT_ps, b + 1)
                    for n in range(2):
                        nc.scalar.activation(wT[:, n * HALF:(n + 1) * HALF], p_d[:, n, :], ACT.Copy).then_inc(wT_done, 1)
                if near:
                    key_spectrum(1, f_c)
                if last:
                    act.wait_ge(pool_step, PS * (b - 1) + 2)
                    if tail and later(b, 2):
                        act.wait_ge(row_out[1 - par], 16 * turns(b - 1, 1 - par))
                    nc.scalar.activation(row[1 - par][:, 0:D], x2[:], ACT.Identity, bias=nb3[:, 1:2],
                                         scale=rstd3[:]).then_inc(x3_done, 1)
                if ahead:
                    split_context(b + 2, par)
                if near:
                    if far:
                        act.wait_ge(pick_done, 8 * c)
                    for n in range(2):
                        act.wait_ge(corr_ps, 2 * c + n + 1)
                        nc.scalar.activation(corr[:, 4 * n:4 * n + 4, :], p_a[:, n, :], ACT.Copy).then_inc(corr_done, 1)
                if last:
                    for n in range(2):
                        act.wait_ge(x3T_ps, 2 * (b - 1) + n + 1)
                        nc.scalar.activation(x3T[:, 4 * n:4 * n + 4, :], p_d[:, n, :], ACT.Copy).then_inc(x3T_done, 1)
                if ahead:
                    normalise(b + 2)
                if near:
                    act.wait_ge(ntop_done, c + 1)
                    for i in range(KD):
                        nc.scalar.activation(ex[:, i, :], corr[:, i, :], ACT.Exp,
                                             bias=ntop[:, i:i + 1]).then_inc(exp_done, 1)
                if last:
                    act.wait_ge(h_step, HS * (b - 1) + 3)
                    nc.scalar.activation(he[:, :, :], hd[:, :, :], ACT.Exp).then_inc(he_done, 1)
                if near:
                    for i, src in ((2, f_a), (3, f_c)):
                        act.wait_ge(v_ps, 2 * c + i - 1)
                        nc.scalar.activation(spec[1 - par][i][:], src, ACT.Copy).then_inc(v_done, 1)

            iterations(act, body)

        @block.vector
        def _(dve):
            dve.wait_ge(fwd_hi_done, 1)
            nc.vector.tensor_tensor(fwd_lo[:, :, :], mats[:, 0:4, :], fwd_hi[:, :, :].bitcast(F32),
                                    ALU.subtract).then_inc(fwd_lo_done, 1)

            def norm2_stats(n):
                dve.wait_ge(x_in, 16 * (n + 1))
                for i in range(2):
                    nc.vector.bn_stats(st2[:, i, :], xin[:, i * HALF:(i + 1) * HALF]).then_inc(n2_step, 1)
                dve.wait_ge(n2_step, 4 * n + 2)
                nc.vector.memset(pause[:, 2:3], 0.0)
                nc.vector.bn_aggr(mv2[:], st2[:, :, :]).then_inc(n2_step, 1)
                dve.wait_ge(n2_step, 4 * n + 3)
                nc.vector.tensor_scalar(ve2[:], mv2[:, 1:2], LN_EPS, None, ALU.add).then_inc(n2_step, 1)

            norm2_stats(0)

            def body(b, par, near, far, last, tail, ahead):
                c = b + 1
                m = b - 1

                def products():
                    for i, src in enumerate((f_b, f_b, f_c, f_c)):
                        if i % 2 == 0:
                            dve.wait_ge(ws_ps, 2 * b + i // 2 + 1)
                            if i == 0:
                                dve.wait_ge(v_done, 2 * b + 2)
                                if last:
                                    dve.wait_ge(out_ps, 2 * b)
                        nc.vector.tensor_tensor(tw[i][:], src, spec[par][i][:], ALU.mult).then_inc(tw_done, 1)

                def h_steps(first, to):
                    pp = lg[:, NS * NS:NLOG].rearrange("p (a n) -> p a n", a=2)
                    for k in range(first, to + 1):
                        if k == 1:
                            dve.wait_ge(lg_ps, b)
                            dve.wait_ge(rs_done, b)
                            ins = nc.vector.scalar_tensor_tensor(lg[:], logits, rs[:], base_sb[:], ALU.mult, ALU.add)
                        else:
                            dve.wait_ge(h_step, HS * m + k - 1)
                        if k == 2:
                            ins = nc.vector.tensor_reduce(hx[:], pp, AX.X, ALU.max)
                        if k == 3:
                            ins = nc.vector.tensor_tensor(hd[:, :, :], pp, hx[:].rearrange("p (a o) -> p a o", o=1).to_broadcast([P, 2, NS]), ALU.subtract)
                        if k == 4:
                            ins = nc.vector.tensor_scalar(fact(m, 1 - par, 0, NS * NS), lg[:, 0:NS * NS], 1.0 / TAU, None, ALU.mult)
                        if k == 5:
                            dve.wait_ge(he_done, b)
                            ins = nc.vector.tensor_reduce(hs[:], he[:, :, :], AX.X, ALU.add)
                        if k == 6:
                            ins = nc.vector.reciprocal(hr[:], hs[:])
                        if k == 7:
                            ins = nc.vector.tensor_scalar(fact(m, 1 - par, AT_POST, NS), he[:, 1, :], hr[:, 1:2], None, ALU.mult)
                        if k == 8:
                            ins = nc.vector.tensor_scalar(hp[:], he[:, 0, :], hr[:, 0:1], None, ALU.mult)
                        ins.then_inc(h_step, 1)

                def branch_in(n):
                    x = row[1 - par][:, n * C:(n + 1) * C]
                    if n == 0:
                        dve.wait_ge(h_step, HS * m + HS)
                        if later(b, 1):
                            dve.wait_ge(xpT_ps, b - 1)
                        ins = nc.vector.tensor_scalar(xp[:], x, hp[:, 0:1], None, ALU.mult)
                    else:
                        dve.wait_ge(xp_step, XS * m + n)
                        ins = nc.vector.scalar_tensor_tensor(xp[:], x, hp[:, n:n + 1], xp[:], ALU.mult, ALU.add)
                    ins.then_inc(xp_step, 1)

                if near:
                    dve.wait_ge(q_ps, c + 1)
                    if far:
                        dve.wait_ge(corr_ps, 2 * c)
                    for i in range(2):
                        dve.wait_ge(k_done, 2 * c + i + 1)
                        nc.vector.tensor_tensor(tq[i][:], f_a, spec[1 - par][i][:], ALU.mult).then_inc(tq_done, 1)
                if far:
                    products()
                if ahead:
                    norm2_stats(b + 2)
                if near:
                    for i in range(KD):
                        if i % 4 == 0:
                            dve.wait_ge(corr_done, 2 * c + i // 4 + 1)
                            nc.vector.memset(pause[:, i // 4:i // 4 + 1], 0.0)
                        nc.vector.max(top[:, i, :], corr[:, i, :]).then_inc(max_done, 1)
                    dve.wait_ge(max_done, 8 * c + 8)
                    nc.vector.tensor_scalar(ntop[:], top[:, :, 0], -1.0, None, ALU.mult).then_inc(ntop_done, 1)
                    for i in range(KD):
                        nc.vector.match_replace(rest[:, i, :], top[:, i, :], corr[:, i, :], NEG).then_inc(rest_done, 1)
                if last:
                    h_steps(1, 2)
                if near:
                    dve.wait_ge(rest_done, 8 * c + 8)
                    nc.vector.tensor_reduce(ninth[:], rest[:, :, :], AX.X, ALU.max).then_inc(ninth_done, 1)
                if last:
                    h_steps(3, 4)
                if near:
                    dve.wait_ge(ninth_done, c + 1)
                    if far:
                        dve.wait_ge(wT_ps, b + 1)
                    for i in range(KD):
                        dve.wait_ge(exp_done, 8 * c + i + 1)
                        nc.vector.scalar_tensor_tensor(wgt[:, i, :], corr[:, i, :], ninth[:, i:i + 1], ex[:, i, :],
                                                       ALU.is_ge, ALU.mult, accum_out=wsum[:, i:i + 1]).then_inc(pick_done, 1)
                if near:
                    dve.wait_ge(pick_done, 8 * c + 8)
                    nc.vector.reciprocal(wrec[:], wsum[:]).then_inc(wrec_done, 1)
                if last:
                    h_steps(5, 8)
                    branch_in(0)
                if far:
                    dve.wait_ge(xres_in, 16 * (b + 1))
                    if last:
                        dve.wait_ge(x3_done, b)
                for n in range(2):
                    if far:
                        dve.wait_ge(out_ps, 2 * b + n + 1)
                        cols = slice(n * HALF, (n + 1) * HALF)
                        nc.vector.tensor_tensor(x2[:, cols], p_b[:, n, :], xres[:, cols], ALU.add).then_inc(x2_done, 1)
                    if last:
                        branch_in(n + 1)
                if last:
                    branch_in(3)
                if far:
                    for n in range(2):
                        dve.wait_ge(x2_done, 2 * b + n + 1)
                        nc.vector.bn_stats(st3[:, n, :], x2[:, n * HALF:(n + 1) * HALF]).then_inc(n3_step, 1)
                    dve.wait_ge(n3_step, N3 * b + 2)
                    if last:
                        dve.wait_ge(pool_step, PS * b)
                    nc.vector.memset(pause[:, 3:4], 0.0)
                    nc.vector.bn_aggr(mv3[:], st3[:, :, :]).then_inc(n3_step, 1)
                    dve.wait_ge(n3_step, N3 * b + 3)
                    nc.vector.tensor_scalar(ve3[:], mv3[:, 1:2], LN_EPS, None, ALU.add).then_inc(n3_step, 1)

            iterations(dve, body)

        @block.gpsimd
        def _(pool):
            for at, value in ((mhalf, -0.5), (one, 1.0), (rms_eps, RMS_EPS), (minus, -1.0)):
                nc.gpsimd.memset(at, value).then_inc(consts_set, 1)
            pool.wait_ge(consts_set, 4)
            TT = nc.gpsimd.tensor_tensor

            def split_context(n, par):
                pool.wait_ge(chi_done, n + 1)
                if later(n, 1):
                    pool.wait_ge(v_ps, 2 * (n - 1))
                TT(c_lo[par][:], cin[:], c_hi[par][:].bitcast(F32), ALU.subtract).then_inc(clo_done, 1)

            def norm2(n):
                pool.wait_ge(n2_step, 4 * n + 4)
                TT(rstd2[:], ve2[:], mhalf, ALU.pow).then_inc(rstd2_done, 1)
                pool.wait_ge(rstd2_done, n + 1)
                TT(nb2[:, 0:1], mv2[:, 0:1], rstd2[:], ALU.mult).then_inc(nb2_step, 1)
                pool.wait_ge(nb2_step, 2 * n + 1)
                TT(nb2[:, 1:2], nb2[:, 0:1], minus, ALU.mult).then_inc(nb2_step, 1)

            norm2(0)
            split_context(0, 0)

            def body(b, par, near, far, last, tail, ahead):
                c = b + 1
                if ahead:
                    split_context(b + 2, par)
                    norm2(b + 2)
                if near:
                    pool.wait_ge(wrec_done, c + 1)
                    TT(wgt[:, :, :], wgt[:, :, :], wrec[:].rearrange("p (k o) -> p k o", o=1).to_broadcast([P, KD, T]),
                       ALU.mult).then_inc(w_done, 1)
                if far:
                    def step(k, ins):
                        ins.then_inc(pool_step, 1)
                        pool.wait_ge(pool_step, PS * b + k)

                    pool.wait_ge(n3_step, N3 * b + 4)
                    TT(rstd3[:], ve3[:], mhalf, ALU.pow).then_inc(rstd3_done, 1)
                    pool.wait_ge(rstd3_done, b + 1)
                    step(1, TT(nb3[:, 0:1], mv3[:, 0:1], rstd3[:], ALU.mult))
                    step(2, TT(nb3[:, 1:2], nb3[:, 0:1], minus, ALU.mult))
                    step(3, TT(fact(b, par, AT_SD, 1), ve3[:], rstd3[:], ALU.mult))
                    step(4, TT(fact(b, par, AT_MEAN, 1), mv3[:, 0:1], one, ALU.mult))
                    step(5, TT(ms[:, 0:1], mv3[:, 1:2], rstd3[:], ALU.mult))
                    step(6, TT(ms[:, 1:2], ms[:, 0:1], rstd3[:], ALU.mult))
                    step(7, TT(ms[:, 2:3], ms[:, 1:2], rms_eps, ALU.add))
                    if last:
                        pool.wait_ge(h_step, HS * (b - 1) + 1)
                    TT(rs[:], ms[:, 2:3], mhalf, ALU.pow).then_inc(rs_done, 1)

            iterations(pool, body)


def mixing_phase(nc, rows, facts, gate, ident, out):
    with ExitStack() as ctx:
        def sb(name, shape, dt=F32):
            return ctx.enter_context(nc.sbuf_tensor("m_" + name, shape, dt))

        def sem(name):
            return ctx.enter_context(nc.semaphore("m_" + name))

        PE_SEQS = 8
        HB = B // 2
        N2 = NS * NS
        NC = N2 + NS + 1
        logm = sb("logm", [P, B, N2])
        mat = sb("mat", [P, B, N2])
        tmp = sb("tmp", [P, B, N2])
        ra = sb("ra", [P, B, NS])
        cb = sb("cb", [P, B, NS])
        red = sb("red", [P, B, NS])
        lra = sb("lra", [P, B, NS])
        lcb = sb("lcb", [P, B, NS])
        coef = sb("coef", [P, B, NC])
        gt = sb("gt", [P, 4])
        ones = sb("ones", [P, NC])

        gate_in = sem("gate_in"); g_exp = sem("g_exp")
        step = [sem(f"step{i}") for i in range(2)]
        logs = [sem(f"logs{i}") for i in range(2)]
        coef_step = sem("coef_step"); ones_set = sem("ones_set"); id_in = sem("id_in")
        mean_done = sem("mean_done"); diag_done = sem("diag_done"); pe_done = sem("pe_done")
        COEF_STEPS = 6
        ident_sb = sb("ident_sb", [P, P])

        PRODUCTS = NS * (NS + 1)

        class Mixer:
            def __init__(self, name, first, to, steps):
                self.first, self.count, self.steps = first, to - first, steps
                self.xr = [sb(f"xr_{name}{i}", [P, ROW]) for i in range(2)]
                self.ot = [sb(f"ot_{name}{i}", [P, D]) for i in range(2)]
                self.row_in = [sem(f"row_in_{name}{i}") for i in range(2)]
                self.stored = [sem(f"stored_{name}{i}") for i in range(2)]
                self.mixed = sem(f"mixed_{name}")

        by_pe, by_dve = Mixer("pe", 0, PE_SEQS, 1), Mixer("dve", PE_SEQS, B, PRODUCTS)
        now = [sb(f"now{i}", [P, NC]) for i in range(2)]
        now_done = sem("now_done")
        mean = [sb(f"mean{i}", [P, 1]) for i in range(2)]
        diag = [sb(f"diag{i}", [P, PRODUCTS, P]) for i in range(2)]
        p_out = [ctx.enter_context(nc.psum_tensor(f"p_out{i}", [P, D], F32)) for i in range(2)]

        block = ctx.enter_context(nc.Block())

        SIZES = (17, 16, 16)
        UNROLL = 4
        assert 1 + sum(SIZES) == SINKHORN_ITERS
        FIRST = 8
        BASES = [FIRST + sum(3 + 6 * s for s in SIZES[:n]) for n in range(len(SIZES) + 1)]
        LFIRST, LBLOCK = 4, 3

        def turn(n, i):
            return 16 * (n // 2) if isinstance(n, int) else 8 * (n - i)

        def in_turn(engine, m, body):
            body(0, 0, True)
            body(1, 1, True)
            with engine.Fori(1, m.count // 2) as u:
                for i in range(2):
                    body(2 * u + i, i, False)
            if m.count % 2:
                body(m.count - 1, 0, False)

        @block.sync
        def _(sp):
            sp.dma_start(gt[:, 0:1], gate).then_inc(gate_in, 16)
            sp.dma_start(ident_sb[:], ident).then_inc(id_in, 16)

            def bring(m, n, i):
                sp.dma_start(m.xr[i][:], rows[m.first + n]).then_inc(m.row_in[i], 16)

            def keep(m, n, i):
                sp.wait_ge(m.mixed, m.steps * (n + 1))
                sp.wait_ge(gate_in, 16)
                sp.dma_start(out[m.first + n], m.ot[i][:]).then_inc(m.stored[i], 16)

            mixers = (by_pe, by_dve)
            for n in range(2):
                for m in mixers:
                    bring(m, n, n)
            for n in range(max(m.count for m in mixers)):
                for m in mixers:
                    if n < m.count:
                        keep(m, n, n % 2)
                        if n + 2 < m.count:
                            bring(m, n + 2, n % 2)
            for m in mixers:
                for i in range(2):
                    sp.wait_ge(m.stored[i], 16 * ((m.count + 1 - i) // 2))

        @block.tensor
        def _(pe):
            m = by_pe

            def mix(n, i, first):
                pe.wait_ge(m.row_in[i], turn(n, i) + 16)
                pe.wait_ge(diag_done, n + 1)
                if not first:
                    pe.wait_ge(m.mixed, n - 1)
                for to in range(NS):
                    for j in range(NS + 1):
                        at = NS * to + j if j < NS else N2 + to
                        r = nc.tensor.matmul(p_out[i][:, to * C:(to + 1) * C], diag[i][:, at, :], m.xr[i][:, j * C:(j + 1) * C],
                                             start=j == 0, stop=j == NS)
                r.then_inc(pe_done, 1)

            in_turn(pe, by_pe, mix)

        @block.scalar
        def _(act):
            act.wait_ge(gate_in, 16)
            nc.scalar.activation(gt[:, 1:2], gt[:, 0:1], ACT.Exp, scale=-1.0).then_inc(g_exp, 1)

            def op(h, src, dst, func, after):
                act.wait_ge(step[h], after)
                part = slice(h * HB, (h + 1) * HB)
                nc.scalar.activation(dst[:, part, :], src[:, part, :], func).then_inc(logs[h], 1)

            for src, dst, func, after in ((tmp, mat, ACT.Exp, 2), (red, lra, ACT.Ln, 3),
                                          (tmp, mat, ACT.Exp, 6), (red, lcb, ACT.Ln, 7), (logm, mat, ACT.Exp, 8)):
                for h in range(2):
                    op(h, src, dst, func, after)
            for end in BASES[1:]:
                for src, dst, func, after in ((ra, lra, ACT.Ln, end - 2), (cb, lcb, ACT.Ln, end - 2), (logm, mat, ACT.Exp, end)):
                    for h in range(2):
                        op(h, src, dst, func, after)

            m = by_pe

            def out_of_psum(n, i, first):
                act.wait_ge(pe_done, n + 1)
                act.wait_ge(mean_done, n + 1)
                if not first:
                    act.wait_ge(m.stored[i], turn(n, i))
                nc.scalar.activation(m.ot[i][:], p_out[i][:], ACT.Identity, bias=mean[i][:]).then_inc(m.mixed, 1)

            in_turn(act, by_pe, out_of_psum)

        @block.vector
        def _(dve):
            def grid(t, h):
                return t[:, h * HB:(h + 1) * HB, :].rearrange("p b (i j) -> p b i j", i=NS)

            def turned(t, h):
                return t[:, h * HB:(h + 1) * HB, :].rearrange("p b (i j) -> p b j i", i=NS)

            def vec(t, h):
                return t[:, h * HB:(h + 1) * HB, :]

            def over_j(t, h):
                return vec(t, h).rearrange("p b (i o) -> p b i o", o=1).to_broadcast([P, HB, NS, NS])

            def over_i(t, h):
                return vec(t, h).rearrange("p b (o j) -> p b o j", o=1).to_broadcast([P, HB, NS, NS])

            def both(k, fn):
                for h in range(2):
                    if not isinstance(k, int) or k > 1:
                        dve.wait_ge(step[h], k - 1)
                    fn(h).then_inc(step[h], 1)

            TT, RED = nc.vector.tensor_tensor, nc.vector.tensor_reduce
            z = facts[:, :, 0:N2]
            both(1, lambda h: RED(vec(red, h), grid(z, h), AX.X, ALU.max))
            both(2, lambda h: TT(grid(tmp, h), grid(z, h), over_j(red, h), ALU.subtract))
            for h in range(2):
                dve.wait_ge(logs[h], 1)
            both(3, lambda h: RED(vec(red, h), grid(mat, h), AX.X, ALU.add))
            for h in range(2):
                dve.wait_ge(logs[h], 2)
            both(4, lambda h: TT(grid(logm, h), grid(tmp, h), over_j(lra, h), ALU.subtract))
            both(5, lambda h: RED(vec(red, h), turned(logm, h), AX.X, ALU.max))
            both(6, lambda h: TT(grid(tmp, h), grid(logm, h), over_i(red, h), ALU.subtract))
            for h in range(2):
                dve.wait_ge(logs[h], 3)
            both(7, lambda h: RED(vec(red, h), turned(mat, h), AX.X, ALU.add))
            for h in range(2):
                dve.wait_ge(logs[h], 4)
            both(8, lambda h: TT(grid(logm, h), grid(tmp, h), over_i(lcb, h), ALU.subtract))

            def iteration(base):
                both(base + 1, lambda h: TT(grid(tmp, h), grid(mat, h), over_i(cb, h), ALU.mult))
                both(base + 2, lambda h: RED(vec(red, h), grid(tmp, h), AX.X, ALU.add))
                both(base + 3, lambda h: nc.vector.reciprocal(vec(ra, h), vec(red, h)))
                both(base + 4, lambda h: TT(grid(tmp, h), grid(mat, h), over_j(ra, h), ALU.mult))
                both(base + 5, lambda h: RED(vec(red, h), turned(tmp, h), AX.X, ALU.add))
                both(base + 6, lambda h: nc.vector.reciprocal(vec(cb, h), vec(red, h)))

            for n, size in enumerate(SIZES):
                for h in range(2):
                    dve.wait_ge(logs[h], LFIRST + 1 + n * LBLOCK)
                both(BASES[n] + 1, lambda h: nc.vector.memset(vec(cb, h), 1.0))
                first = BASES[n] + 1
                for i in range(size % UNROLL):
                    iteration(first + 6 * i)
                first += 6 * (size % UNROLL)
                with dve.Fori(0, size // UNROLL) as t:
                    for i in range(UNROLL):
                        iteration(first + 6 * UNROLL * t + 6 * i)
                for h in range(2):
                    dve.wait_ge(logs[h], LFIRST + 1 + n * LBLOCK + 2)
                both(BASES[n + 1] - 1, lambda h: TT(grid(logm, h), grid(logm, h), over_j(lra, h), ALU.add))
                both(BASES[n + 1], lambda h: TT(grid(logm, h), grid(logm, h), over_i(lcb, h), ALU.add))

            k = [0]

            def link(ins):
                k[0] += 1
                ins.then_inc(coef_step, 1)
                dve.wait_ge(coef_step, k[0])

            for h in range(2):
                dve.wait_ge(logs[h], LFIRST + 1 + len(SIZES) * LBLOCK)
            dve.wait_ge(g_exp, 1)
            link(nc.vector.tensor_scalar(gt[:, 2:3], gt[:, 1:2], 1.0, None, ALU.add))
            link(nc.vector.reciprocal(gt[:, 3:4], gt[:, 2:3]))
            link(nc.vector.tensor_scalar(gt[:, 0:1], gt[:, 3:4], -1.0, 1.0, ALU.mult, ALU.add))
            link(nc.vector.tensor_scalar(coef[:, :, 0:N2], mat[:, :, :], gt[:, 3:4], None, ALU.mult))
            of_self = coef[:, :, 0:N2:NS + 1]
            sd = facts[:, :, AT_SD:AT_SD + 1].to_broadcast([P, B, NS])
            link(nc.vector.scalar_tensor_tensor(of_self, of_self, gt[:, 0:1], sd, ALU.add, ALU.add))
            link(nc.vector.tensor_copy(coef[:, :, N2:NC], facts[:, :, N2:NC]))

            m = by_dve

            def mix(n, i, first):
                nc.vector.tensor_copy(now[i][:], coef[:, m.first + n, :]).then_inc(now_done, 1)
                dve.wait_ge(m.row_in[i], turn(n, i) + 16)
                if not first:
                    dve.wait_ge(m.stored[i], turn(n, i))
                dve.wait_ge(now_done, n + 1)
                w, x, o = now[i], m.xr[i], m.ot[i]
                for j in range(NS + 1):
                    for to in range(NS):
                        dst = o[:, to * C:(to + 1) * C]
                        if j == 0:
                            r = nc.vector.tensor_scalar(dst, x[:, 0:C], w[:, NS * to:NS * to + 1], w[:, NC - 1:NC], ALU.mult, ALU.add)
                        else:
                            at = NS * to + j if j < NS else N2 + to
                            dve.wait_ge(m.mixed, PRODUCTS * n + 4 * (j - 1) + to + 1)
                            r = nc.vector.scalar_tensor_tensor(dst, x[:, j * C:(j + 1) * C], w[:, at:at + 1], dst, ALU.mult, ALU.add)
                        r.then_inc(m.mixed, 1)

            in_turn(dve, by_dve, mix)

        @block.gpsimd
        def _(pool):
            nc.gpsimd.memset(ones[:], 1.0).then_inc(ones_set, 1)
            pool.wait_ge(ones_set, 1)
            pool.wait_ge(coef_step, COEF_STEPS)
            pool.wait_ge(id_in, 16)

            def diagonals(n, i, first):
                if not first:
                    pool.wait_ge(by_pe.mixed, n - 1)
                at = coef[:, by_pe.first + n, :]
                nc.gpsimd.tensor_tensor(diag[i][:, :, :], ident_sb[:, :].rearrange("p (o t) -> p o t", o=1).to_broadcast([P, PRODUCTS, P]),
                                        at[:, 0:PRODUCTS].rearrange("p (k o) -> p k o", o=1).to_broadcast([P, PRODUCTS, P]),
                                        ALU.mult).then_inc(diag_done, 1)
                nc.gpsimd.tensor_tensor(mean[i][:], at[:, PRODUCTS:NC], ones[:, 0:1], ALU.mult).then_inc(mean_done, 1)

            in_turn(pool, by_pe, diagonals)


def dft_matrices():
    t = np.arange(T, dtype=np.float64)
    f = np.arange(T // 2, dtype=np.float64)
    H = T // 2
    even = 2 * np.pi * np.outer(t, f) / T
    odd = 2 * np.pi * np.outer(t, f + 0.5) / T
    a = np.concatenate([np.cos(even), -np.sin(even)], 1)
    a[:, H] = (-1.0) ** t
    b = np.concatenate([a[:, H:], a[:, :H]], 1)
    b[:, 0] = t == T - 1
    o = np.concatenate([np.cos(odd), -np.sin(odd)], 1)
    ov = o.copy()
    ov[T - 1] -= o.sum(0)
    ovb = np.concatenate([ov[:, H:], ov[:, :H]], 1)
    c1 = 2 / T * np.concatenate([np.cos(even).T, np.cos(even).T], 0)
    c1[0] = 1 / T
    c1[H] = (-1.0) ** t / T
    c2 = 2 / T * np.concatenate([np.sin(even).T, -np.sin(even).T], 0)
    o1 = -c2 / 2
    o1[0] = 0.5
    o2 = np.concatenate([np.cos(odd).T, np.cos(odd).T], 0) / T
    o3 = np.concatenate([-np.sin(odd).T, np.sin(odd).T], 0) / T
    return np.stack([a, b, ov, ovb, o, c1 / 2, o1, o2, o3, c1, c2], 1).astype(np.float32)


def build(nc, x, ctx, wq, wk, wv, wo, w24, base, wb, gate, ident, causal, rope, dft, out):
    x1 = nc.dram_tensor("x1", [B, T, D], F32).ap()
    rows = nc.dram_tensor("rows", [B, T, ROW], F32).ap()
    attention_phase(nc, x, wq, wk, wv, wo, ident, causal, rope, x1)
    with nc.sbuf_tensor("facts", [P, B, FACTS], F32) as facts:
        autocorrelation_phase(nc, x1, ctx, ident, dft, w24, base, wb, facts, rows)
        mixing_phase(nc, rows, facts, gate, ident, out)


def rope_tables():
    inv = (1.0 / 500000.0 ** (np.arange(0, HD, 2, dtype=np.float32) / np.float32(HD))).astype(np.float32)
    f = (np.arange(T, dtype=np.float32)[:, None] * inv[None, :]).astype(np.float64)
    c, s = np.cos(f), np.sin(f)
    cc, ss = np.concatenate([c, c], 1), np.concatenate([-s, s], 1)
    scale = 1.0 / np.sqrt(HD)
    return np.stack([cc * scale, ss * scale, cc, ss], 1).astype(np.float32)


def constants():
    eye = np.eye(P, dtype=np.float32)
    causal = np.where(np.arange(T)[None, :] > np.arange(T)[:, None], -1e30, 0.0)
    return {
        "ident": eye,
        "causal": causal.astype(np.float32),
        "rope": rope_tables(),
        "dft": dft_matrices(),
    }


_ORDER = ["x", "ctx", "wq", "wk", "wv", "wo", "w24", "base", "wb", "gate", "ident", "causal", "rope", "dft"]


def laid_out(inputs):
    w = np.concatenate([np.asarray(inputs["L0_ffn_W_" + n]) for n in ("res", "pre", "post")], 0)
    base = np.concatenate([np.asarray(inputs["L0_ffn_H_" + n + "_base"]).reshape(-1) for n in ("res", "pre", "post")])
    return {
        "x": inputs["x"], "ctx": inputs["ctx_4096"],
        "wq": inputs["L0_attn_Wq"], "wk": inputs["L0_attn_Wk"], "wv": inputs["L0_attn_Wv"], "wo": inputs["L0_attn_Wo"],
        "w24": w.T.reshape(KD, P, NLOG).transpose(1, 0, 2),
        "base": np.broadcast_to(base, (P, NLOG)),
        "wb": inputs["L0_ffn_W_branch"],
        "gate": np.broadcast_to(np.asarray(inputs["L0_ffn_gate"]), (P, 1)),
        **constants(),
    }


def kernel(**inputs):
    import concourse.bacc as bacc
    from concourse.bass_utils import run_bass_kernel_spmd

    nc = bacc.Bacc("TRN2", target_bir_lowering=False, num_devices=1)
    laid = laid_out(inputs)
    arrays, args = {}, []
    for name in _ORDER:
        a = np.ascontiguousarray(laid[name])
        arrays["in_" + name] = a
        args.append(nc.dram_tensor("in_" + name, a.shape, mybir.dt.from_np(a.dtype), kind="ExternalInput").ap())
    out = nc.dram_tensor("out", (B, T, D), F32, kind="ExternalOutput").ap()
    build(nc, *args, out)
    r = run_bass_kernel_spmd(nc, [arrays], core_ids=[0])
    return r.results[0]["out"]
```

```python
from contextlib import ExitStack

import numpy as np
import concourse.bass as bass
from concourse import mybir

P = 128
B = 16
T = 128
D = 1024
KD = D // P
HALF = 512
NH, NKV, HD = 32, 8, 32
GROUP = NH // NKV
KVW = NKV * HD
QKVW = D + 2 * KVW
STRIPS = P // HD
LN_EPS = 1e-5

NS = 4
C = D // NS
NLOG = NS * NS + 2 * NS
SINKHORN_ITERS = 50
EARLY = 6
RESTART = 13
EARLY_LEFT = 3
TAU = 0.1
RMS_EPS = 1.1920929e-07
ROW = D + C
AT_POST = NS * NS
AT_MEAN = AT_POST + NS
AT_SD = AT_MEAN + 1
FACTS = AT_SD + 1
NEG = -3.0e38
WO_SLOTS = 4
FWD_A, FWD_ODD, INV_OUT, INV_CORR, N_DFT = 0, 4, 5, 9, 11

F32 = mybir.dt.float32
F32R = mybir.dt.float32r
BF16 = mybir.dt.bfloat16
ALU = mybir.AluOpType
ACT = mybir.ActivationFunctionType
AX = mybir.AxisListType


def attention_phase(nc, x, wq, wk, wv, wo, ident, causal, rope, x1):
    wo_v = wo.rearrange("(G s j d) n -> G j s d n", G=2, s=STRIPS, j=GROUP)

    with ExitStack() as ctx:
        def sb(name, shape, dt, stack=ctx):
            return stack.enter_context(nc.sbuf_tensor(name, shape, dt))

        def sem(name):
            return ctx.enter_context(nc.semaphore(name))

        w_hi = sb("w_hi", [P, KD, QKVW], F32R)
        w_lo = sb("w_lo", [P, KD, QKVW], F32R)
        wo_hi = sb("wo_hi", [P, KD, D], F32R)
        wo_lo = sb("wo_lo", [P, KD, D], F32R)
        idf = sb("idf", [P, P], F32)
        mask = sb("mask", [P, P], F32)
        tab = sb("tab", [P, 4, HD], F32)
        xin = sb("xin", [P, D], F32)
        xT_hi = sb("xT_hi", [P, KD, T], F32R)
        xT_lo = sb("xT_lo", [P, KD, T], F32R)
        v_sb = sb("v_sb", [P, KVW], F32)
        qT = sb("qT", [P, 2, GROUP, T], F32)
        kT = sb("kT", [P, 2, T], F32)
        stats = sb("stats", [P, 2, 6], F32)
        mv = sb("mv", [P, 2], F32)
        veps = sb("veps", [P, 1], F32)
        rstd = sb("rstd", [P, 1], F32)
        mhalf = sb("mhalf", [P, 1], F32)
        pause = sb("pause", [P, 1], F32)
        negm = sb("negm", [P, NH], F32)
        lsum = sb("lsum", [P, NH], F32)
        rl = sb("rl", [P, NH], F32)
        with ExitStack() as shared:
            rc = sb("rc", [P, D + KVW], F32, shared)
            rs = sb("rs", [P, D + KVW], F32, shared)
        with ExitStack() as shared:
            prob = sb("prob", [P, 3, GROUP, T], F32, shared)
            pT = sb("pT", [P, 2, GROUP, T], F32, shared)
        with ExitStack() as shared:
            w_third = sb("w_third", [P, QKVW], F32, shared)
        sb("rc_prob_room", [P, 2 * (D + KVW)], F32)
        with ExitStack() as shared:
            w_pair = sb("w_pair", [P, 2, QKVW], F32, shared)
        w_stage = [w_pair[:, 0, :], w_pair[:, 1, :], w_third[:]]
        aT_hi = sb("aT_hi", [P, 2, GROUP, T], F32R)
        aT_lo = sb("aT_lo", [P, 2, GROUP, T], F32R)
        with ExitStack() as shared:
            wo_stage = sb("wo_stage", [P, WO_SLOTS, HALF], F32, shared)
        xres = sb("xres", [P, D], F32)

        ps_qkv = ctx.enter_context(nc.psum_tensor("ps_qkv", [P, 3, HALF], F32))
        ps_s = ctx.enter_context(nc.psum_tensor("ps_s", [P, 2, HALF], F32))
        ps_t = ctx.enter_context(nc.psum_tensor("ps_t", [P, HALF], F32))
        ps_a = ctx.enter_context(nc.psum_tensor("ps_a", [P, 2, HALF], F32))

        const_in = sem("const_in")
        x_in = sem("x_in")
        w_in = [sem(f"w_in{i}") for i in range(3)]
        wo_in = [sem(f"wo_in{i}") for i in range(WO_SLOTS)]
        xres_in = sem("xres_in")
        x1_out = sem("x1_out")
        mhalf_set = sem("mhalf_set")
        w_hi_done = sem("w_hi_done")
        w_lo_done = sem("w_lo_done")
        wo_hi_done = sem("wo_hi_done")
        wo_lo_done = sem("wo_lo_done")
        stat_step = sem("stat_step")
        rstd_done = sem("rstd_done")
        xn_done = sem("xn_done")
        xT_ps = sem("xT_ps")
        xh_done = sem("xh_done")
        xl_done = sem("xl_done")
        qkv_ps = sem("qkv_ps")
        rope_done = sem("rope_done")
        v_done = sem("v_done")
        rsum_done = sem("rsum_done")
        qkT_ps = sem("qkT_ps")
        qkT_done = sem("qkT_done")
        s_ps = sem("s_ps")
        masked = sem("masked")
        negm_done = sem("negm_done")
        e_done = sem("e_done")
        rl_done = sem("rl_done")
        p_done = sem("p_done")
        pT_ps = sem("pT_ps")
        pT_done = sem("pT_done")
        a_ps = sem("a_ps")
        ah_done = sem("ah_done")
        al_done = sem("al_done")
        o_ps = sem("o_ps")
        x1_done = sem("x1_done")

        block = ctx.enter_context(nc.Block())

        def iterations(engine, body):
            body(-2, attend=False, project=False, norm=True)
            body(-1, attend=False, project=True, norm=True)
            body(0, attend=True, project=True, norm=True, first=True)
            with engine.Fori(1, B - 2) as b:
                body(b, attend=True, project=True, norm=True)
            body(B - 2, attend=True, project=True, norm=False)
            body(B - 1, attend=True, project=False, norm=False)

        @block.sync
        def _(sp):
            sp.dma_start(xin[:], x[0]).then_inc(x_in, 16)
            sp.dma_start(idf[:], ident).then_inc(const_in, 16)
            sp.dma_start(mask[:], causal).then_inc(const_in, 16)
            sp.dma_start(tab[:], rope).then_inc(const_in, 16)

            def body(b, attend, project, norm, first=False):
                if not attend and project:
                    for k in range(KD):
                        if k >= 3:
                            sp.wait_ge(w_hi_done, k - 2)
                            sp.wait_ge(w_lo_done, k - 2)
                        rows = slice(k * P, (k + 1) * P)
                        st = w_stage[k % 3]
                        sp.dma_start(st[:, 0:D], wq[rows, :]).then_inc(w_in[k % 3], 16)
                        sp.dma_start(st[:, D:D + KVW], wk[rows, :]).then_inc(w_in[k % 3], 16)
                        sp.dma_start(st[:, D + KVW:QKVW], wv[rows, :]).then_inc(w_in[k % 3], 16)
                if norm and (not isinstance(b, int) or b > -2):
                    sp.wait_ge(xT_ps, 2 * (b + 2))
                    sp.wait_ge(const_in, 48)
                    sp.dma_start(xin[:], x[b + 2]).then_inc(x_in, 16)
                if attend:
                    if first:
                        sp.wait_ge(w_hi_done, KD)
                        sp.wait_ge(w_lo_done, KD)
                        for n in range(2 * KD):
                            if n >= WO_SLOTS:
                                sp.wait_ge(wo_hi_done, n - WO_SLOTS + 1)
                                sp.wait_ge(wo_lo_done, n - WO_SLOTS + 1)
                            c, half = n // 2, n % 2
                            for s in range(STRIPS):
                                sp.dma_start(wo_stage[s * HD:(s + 1) * HD, n % WO_SLOTS, :],
                                             wo_v[c // GROUP, c % GROUP, s, :, half * HALF:(half + 1) * HALF]
                                             ).then_inc(wo_in[n % WO_SLOTS], 16)
                        sp.wait_ge(wo_hi_done, 2 * KD)
                        sp.wait_ge(wo_lo_done, 2 * KD)
                    else:
                        sp.wait_ge(x1_out, 16 * b)
                    sp.wait_ge(const_in, 48)
                    sp.dma_start(xres[:], x[b]).then_inc(xres_in, 16)
                    sp.wait_ge(x1_done, 2 * b + 2)
                    sp.wait_ge(const_in, 48)
                    sp.dma_start(x1[b], xres[:]).then_inc(x1_out, 16)

            iterations(sp, body)
            sp.wait_ge(x1_out, 16 * B)

        @block.tensor
        def _(pe):
            def body(b, attend, project, norm, first=False):
                def scores(g, b=b, first=first):
                    G, s = g // STRIPS, g % STRIPS
                    if g == 0:
                        pe.wait_ge(qkT_done, 3 * (b + 1))
                    if g < 2:
                        if not first:
                            pe.wait_ge(x1_done, 2 * b - 1 + g)
                    else:
                        pe.wait_ge(masked, 8 * b + g - 1)
                    lanes = slice(s * HD, (s + 1) * HD)
                    for j in range(GROUP):
                        last = nc.tensor.matmul(ps_s[:, g % 2, j * T:(j + 1) * T], qT[lanes, G, j, :],
                                                kT[lanes, G, :], start=True, stop=True)
                    last.then_inc(s_ps, 1)

                def project_chunk(k):
                    if k == 0:
                        pe.wait_ge(xh_done, 2 * (b + 1) + 2)
                        pe.wait_ge(xl_done, 2 * (b + 1) + 2)
                        if attend:
                            pe.wait_ge(rope_done, 3 * (b + 1))
                            pe.wait_ge(v_done, b + 1)
                    if not attend:
                        pe.wait_ge(w_hi_done, k + 1)
                        pe.wait_ge(w_lo_done, k + 1)
                    for n in range(3):
                        cols = slice(n * HALF, (n + 1) * HALF)
                        nc.tensor.matmul(ps_qkv[:, n, :], xT_hi[:, k, :], w_hi[:, k, cols], start=k == 0, stop=False)
                        nc.tensor.matmul(ps_qkv[:, n, :], xT_hi[:, k, :], w_lo[:, k, cols], start=False, stop=False)
                    for n in range(3):
                        cols = slice(n * HALF, (n + 1) * HALF)
                        last = nc.tensor.matmul(ps_qkv[:, n, :], xT_lo[:, k, :], w_hi[:, k, cols],
                                                start=False, stop=k == KD - 1)
                    if k == KD - 1:
                        last.then_inc(qkv_ps, 1)

                def prob_transpose(g):
                    pe.wait_ge(p_done, 8 * b + g + 1)
                    if g > 0:
                        pe.wait_ge(pT_done, 8 * b + g)
                    for j in range(GROUP):
                        last = nc.tensor.transpose(ps_t[:, j * T:(j + 1) * T], prob[:, g % 3, j, :], idf[:])
                    last.then_inc(pT_ps, 1)

                def weigh_values(g):
                    G, s = g // STRIPS, g % STRIPS
                    pe.wait_ge(pT_done, 8 * b + g + 1)
                    last = nc.tensor.matmul(ps_a[s * HD:(s + 1) * HD, G, :], v_sb[:, g * HD:(g + 1) * HD],
                                            pT[:, g % 2, :, :], start=True, stop=True)
                    if s == STRIPS - 1:
                        last.then_inc(a_ps, 1)

                def x_transpose(half):
                    c = b + 2
                    if half == 0:
                        pe.wait_ge(xn_done, c + 1)
                        if attend:
                            pe.wait_ge(pT_done, 8 * b + 8)
                        elif project:
                            pe.wait_ge(xh_done, 2 * c)
                            pe.wait_ge(xl_done, 2 * c)
                    else:
                        pe.wait_ge(xh_done, 2 * c + 1)
                        pe.wait_ge(xl_done, 2 * c + 1)
                    for i in range(4):
                        k = 4 * half + i
                        last = nc.tensor.transpose(ps_t[:, i * T:(i + 1) * T], xin[:, k * P:(k + 1) * P], idf[:])
                    last.then_inc(xT_ps, 1)

                def qk_transpose():
                    for G in range(2):
                        pe.wait_ge(rsum_done, 3 * (b + 1) + G + 1)
                        if attend and G == 0:
                            pe.wait_ge(ah_done, 2 * b + 2)
                            pe.wait_ge(al_done, 2 * b + 2)
                        for j in range(GROUP):
                            last = nc.tensor.transpose(ps_a[:, G, j * T:(j + 1) * T], rc[:, G * HALF + j * P:G * HALF + (j + 1) * P], idf[:])
                        last.then_inc(qkT_ps, 1)
                    pe.wait_ge(rsum_done, 3 * (b + 1) + 3)
                    if norm:
                        pe.wait_ge(xh_done, 2 * (b + 2) + 2)
                        pe.wait_ge(xl_done, 2 * (b + 2) + 2)
                    for G in range(2):
                        last = nc.tensor.transpose(ps_t[:, G * T:(G + 1) * T], rc[:, D + G * P:D + (G + 1) * P], idf[:])
                    last.then_inc(qkT_ps, 1)

                def output_chunk(G, j, halves):
                    c = G * GROUP + j
                    if j == 0 and halves[0] == 0:
                        pe.wait_ge(ah_done, 2 * b + G + 1)
                        pe.wait_ge(al_done, 2 * b + G + 1)
                        if first and G == 0:
                            pe.wait_ge(wo_hi_done, 2 * KD)
                            pe.wait_ge(wo_lo_done, 2 * KD)
                    for left, right in ((aT_hi, wo_hi), (aT_hi, wo_lo), (aT_lo, wo_hi)):
                        for n in halves:
                            last = nc.tensor.matmul(ps_s[:, n, :], left[:, G, j, :], right[:, c, n * HALF:(n + 1) * HALF],
                                                    start=c == 0 and left is aT_hi and right is wo_hi,
                                                    stop=c == KD - 1 and left is aT_lo)
                    if c == KD - 1:
                        last.then_inc(o_ps, 1)

                for g in range(NKV):
                    if project:
                        project_chunk(g)
                    if attend:
                        if g == 0:
                            scores(1)
                        if g + 2 < NKV:
                            scores(g + 2)
                        prob_transpose(g)
                        if g > 0:
                            weigh_values(g - 1)
                if attend:
                    pe.wait_ge(masked, 8 * b + 8)
                    output_chunk(0, 0, (0, 1))
                    weigh_values(NKV - 1)
                if norm:
                    x_transpose(0)
                if attend:
                    for j in range(1, GROUP):
                        output_chunk(0, j, (0, 1))
                if norm:
                    x_transpose(1)
                if attend:
                    for j in range(GROUP):
                        output_chunk(1, j, (0,))
                if project:
                    qk_transpose()
                for j in range(GROUP):
                    if attend:
                        output_chunk(1, j, (1,))
                    if project and j == 1:
                        scores(0, b + 1, not attend)

            pe.wait_ge(const_in, 48)
            iterations(pe, body)

        @block.scalar
        def _(act):
            act.wait_ge(const_in, 48)

            def body(b, attend, project, norm, first=False):
                if project and not attend:
                    for k in range(KD):
                        act.wait_ge(w_in[k % 3], 48 * (k // 3 + 1))
                        nc.scalar.activation(w_hi[:, k, :], w_stage[k % 3], ACT.Copy).then_inc(w_hi_done, 1)

                def attend_out(G):
                    act.wait_ge(a_ps, 2 * b + G + 1)
                    if not first:
                        act.wait_ge(o_ps, 2 * b)
                    nc.scalar.activation(aT_hi[:, G, :, :], ps_a[:, G, :], ACT.Copy).then_inc(ah_done, 1)

                if attend:
                    for g in range(NKV):
                        act.wait_ge(negm_done, 8 * b + g + 1)
                        for j in range(GROUP):
                            h = g * GROUP + j
                            last = nc.scalar.activation(prob[:, g % 3, j, :], prob[:, g % 3, j, :], ACT.Exp,
                                                        bias=negm[:, h:h + 1], accum_out=lsum[:, h:h + 1])
                        last.then_inc(e_done, 1)
                        if first:
                            for half in range(2):
                                n = 2 * g + half
                                act.wait_ge(wo_in[n % WO_SLOTS], 64 * (n // WO_SLOTS + 1))
                                nc.scalar.activation(wo_hi[:, g, half * HALF:(half + 1) * HALF], wo_stage[:, n % WO_SLOTS, :],
                                                     ACT.Copy).then_inc(wo_hi_done, 1)
                        if g == 5:
                            attend_out(0)
                if project:
                    act.wait_ge(qkv_ps, b + 2)
                    if attend:
                        act.wait_ge(a_ps, 2 * b + 2)
                    nc.scalar.activation(v_sb[:], ps_qkv[:, 2, KVW:2 * KVW], ACT.Copy).then_inc(v_done, 1)
                if attend:
                    attend_out(1)
                if norm:
                    for half in range(2):
                        act.wait_ge(xT_ps, 2 * (b + 2) + half + 1)
                        if project:
                            act.wait_ge(qkv_ps, b + 2)
                        nc.scalar.activation(xT_hi[:, 4 * half:4 * half + 4, :], ps_t[:], ACT.Copy).then_inc(xh_done, 1)
                if project:
                    if attend:
                        act.wait_ge(s_ps, 8 * b + 8)
                    for G in range(2):
                        act.wait_ge(qkT_ps, 3 * (b + 1) + G + 1)
                        nc.scalar.activation(qT[:, G, :, :], ps_a[:, G, :], ACT.Copy).then_inc(qkT_done, 1)
                    act.wait_ge(qkT_ps, 3 * (b + 1) + 3)
                    nc.scalar.activation(kT[:, :, :], ps_t[:, 0:2 * T], ACT.Copy).then_inc(qkT_done, 1)

            iterations(act, body)

        @block.vector
        def _(dve):
            def row_negm(b, g):
                dve.wait_ge(s_ps, 8 * b + g + 1)
                nc.vector.tensor_tensor(prob[:, g % 3, :, :], ps_s[:, g % 2, :].rearrange("p (j k) -> p j k", j=GROUP),
                                        mask[:].rearrange("p (a k) -> p a k", a=1).to_broadcast([P, GROUP, P]),
                                        ALU.add).then_inc(masked, 1)
                dve.wait_ge(masked, 8 * b + g + 1)
                nc.vector.tensor_reduce(negm[:, g * GROUP:(g + 1) * GROUP], prob[:, g % 3, :, :],
                                        AX.X, ALU.max, negate=True).then_inc(negm_done, 1)

            def body(b, attend, project, norm, first=False):
                c = b + 2

                def norm_stats():
                    dve.wait_ge(x_in, 16 * (c + 1))
                    for i in range(2):
                        nc.vector.bn_stats(stats[:, i, :], xin[:, i * HALF:(i + 1) * HALF]).then_inc(stat_step, 1)
                    dve.wait_ge(stat_step, 4 * c + 2)
                    nc.vector.memset(pause[:], 0.0)
                    nc.vector.bn_aggr(mv[:], stats[:, :, :]).then_inc(stat_step, 1)
                    dve.wait_ge(stat_step, 4 * c + 3)
                    nc.vector.tensor_scalar(veps[:], mv[:, 1:2], LN_EPS, None, ALU.add).then_inc(stat_step, 1)

                def norm_apply():
                    dve.wait_ge(rstd_done, c + 1)
                    nc.vector.tensor_scalar(xin[:], xin[:], mv[:, 0:1], rstd[:], ALU.subtract, ALU.mult).then_inc(xn_done, 1)

                def attend_out(G):
                    dve.wait_ge(ah_done, 2 * b + G + 1)
                    nc.vector.tensor_tensor(aT_lo[:, G, :, :], ps_a[:, G, :].rearrange("p (j t) -> p j t", j=GROUP),
                                            aT_hi[:, G, :, :].bitcast(F32), ALU.subtract).then_inc(al_done, 1)

                def x_lo(half):
                    dve.wait_ge(xh_done, 2 * c + half + 1)
                    nc.vector.tensor_tensor(xT_lo[:, 4 * half:4 * half + 4, :], ps_t[:].rearrange("p (k t) -> p k t", k=4),
                                            xT_hi[:, 4 * half:4 * half + 4, :].bitcast(F32),
                                            ALU.subtract).then_inc(xl_done, 1)

                def rope_bank(n):
                    a, c = (STRIPS, GROUP) if n < 2 else (1, NKV)
                    w = a * c * HD
                    t = 0 if n < 2 else 2
                    at = slice(n * HALF, n * HALF + w)
                    src = ps_qkv[:, n, 0:w].rearrange("p (a c i) -> p a c i", a=a, c=c)
                    by_cos = rc[:, at].rearrange("p (c a i) -> p a c i", a=a, c=c)
                    by_sin = rs[:, at].rearrange("p (c a i) -> p a c i", a=a, c=c)
                    cos = tab[:, t:t + 1, :].rearrange("p o (r i) -> p o r i", r=1)
                    sin = tab[:, t + 1:t + 2, :].rearrange("p o (r i) -> p o r i", r=1)
                    nc.vector.tensor_tensor(by_cos, src, cos.to_broadcast([P, a, c, HD]), ALU.mult)
                    for lo, hi in ((0, HD // 2), (HD // 2, 0)):
                        to, of = slice(lo, lo + HD // 2), slice(hi, hi + HD // 2)
                        last = nc.vector.tensor_tensor(by_sin[:, :, :, to], src[:, :, :, of],
                                                       sin[:, :, :, to].to_broadcast([P, a, c, HD // 2]), ALU.mult)
                    last.then_inc(rope_done, 1)

                if project and not attend:
                    for k in range(KD):
                        dve.wait_ge(w_hi_done, k + 1)
                        nc.vector.tensor_tensor(w_lo[:, k, :], w_stage[k % 3], w_hi[:, k, :].bitcast(F32),
                                                ALU.subtract).then_inc(w_lo_done, 1)
                if attend:
                    def row_reciprocal(g):
                        dve.wait_ge(e_done, 8 * b + g + 1)
                        hs = slice(g * GROUP, (g + 1) * GROUP)
                        nc.vector.reciprocal(rl[:, hs], lsum[:, hs]).then_inc(rl_done, 1)

                    def prob_copy(g):
                        dve.wait_ge(pT_ps, 8 * b + g + 1)
                        nc.vector.tensor_copy(pT[:, g % 2, :, :], ps_t[:].rearrange("p (j t) -> p j t", j=GROUP)).then_inc(pT_done, 1)

                    row_reciprocal(0)
                    row_negm(b, 1)
                    for g in range(NKV):
                        if first:
                            for half in range(2):
                                n = 2 * g + half
                                dve.wait_ge(wo_hi_done, n + 1)
                                cols = slice(half * HALF, (half + 1) * HALF)
                                nc.vector.tensor_tensor(wo_lo[:, g, cols], wo_stage[:, n % WO_SLOTS, :],
                                                        wo_hi[:, g, cols].bitcast(F32), ALU.subtract).then_inc(wo_lo_done, 1)
                        if g == 0:
                            prob_copy(0)
                        if g + 1 < NKV:
                            row_reciprocal(g + 1)
                        if g + 2 < NKV:
                            row_negm(b, g + 2)
                        if g > 0:
                            prob_copy(g)
                        if norm and g == 1:
                            norm_stats()
                        if norm and g == 4:
                            norm_apply()
                        if g == 5:
                            attend_out(0)
                elif norm:
                    norm_stats()
                    norm_apply()
                if project:
                    dve.wait_ge(qkv_ps, b + 2)
                    if attend:
                        dve.wait_ge(a_ps, 2 * b + 2)
                    rope_bank(0)
                if attend:
                    attend_out(1)
                if norm:
                    x_lo(0)
                if project:
                    rope_bank(1)
                    rope_bank(2)
                if norm:
                    x_lo(1)
                if attend:
                    dve.wait_ge(xres_in, 16 * (b + 1))
                    for n in range(2):
                        cols = slice(n * HALF, (n + 1) * HALF)
                        dve.wait_ge(o_ps, 2 * b + n + 1)
                        nc.vector.tensor_tensor(xres[:, cols], ps_s[:, n, :], xres[:, cols], ALU.add).then_inc(x1_done, 1)
                        if project and n == 0:
                            row_negm(b + 1, 0)
                elif project:
                    row_negm(b + 1, 0)

            dve.wait_ge(const_in, 48)
            iterations(dve, body)

        @block.gpsimd
        def _(pool):
            nc.gpsimd.memset(mhalf[:], -0.5).then_inc(mhalf_set, 1)
            pool.wait_ge(mhalf_set, 1)

            def body(b, attend, project, norm, first=False):
                def norm_rstd():
                    pool.wait_ge(stat_step, 4 * (b + 2) + 4)
                    nc.gpsimd.tensor_tensor(rstd[:], veps[:], mhalf[:], ALU.pow).then_inc(rstd_done, 1)

                if attend:
                    for g in range(NKV):
                        pool.wait_ge(rl_done, 8 * b + g + 1)
                        nc.gpsimd.tensor_tensor(prob[:, g % 3, :, :], prob[:, g % 3, :, :],
                                                rl[:, g * GROUP:(g + 1) * GROUP].rearrange("p (j o) -> p j o", o=1).to_broadcast([P, GROUP, T]),
                                                ALU.mult).then_inc(p_done, 1)
                        if norm and g == 2:
                            norm_rstd()
                elif norm:
                    norm_rstd()
                if project:
                    for n in range(3):
                        at = slice(n * HALF, min((n + 1) * HALF, D + KVW))
                        pool.wait_ge(rope_done, 3 * (b + 1) + n + 1)
                        nc.gpsimd.tensor_tensor(rc[:, at], rc[:, at], rs[:, at], ALU.add).then_inc(rsum_done, 1)

            iterations(pool, body)


BLOCK_ITERS = (25, 24)
assert 1 + sum(BLOCK_ITERS) == SINKHORN_ITERS
FIRST = 8
FIRST_LOGS, BLOCK_LOGS = 5, 3
BASES = [FIRST + sum(3 + 6 * s for s in BLOCK_ITERS[:n]) for n in range(len(BLOCK_ITERS) + 1)]


class Chain:
    def __init__(self, nc, ctx, name, z, mat):
        n = self.n = mat.shape[1]
        def sb(what, width):
            return ctx.enter_context(nc.sbuf_tensor(f"{name}_{what}", [P, n, width], F32))
        self.nc, self.z, self.mat = nc, z, mat
        self.logm, self.tmp = sb("logm", NS * NS), sb("tmp", NS * NS)
        self.ra, self.cb, self.red, self.lra, self.lcb = (sb(w, NS) for w in ("ra", "cb", "red", "lra", "lcb"))
        self.step = ctx.enter_context(nc.semaphore(f"{name}_step"))
        self.logs = ctx.enter_context(nc.semaphore(f"{name}_logs"))

    def grid(self, t):
        return t[:, :, :].rearrange("p b (i j) -> p b i j", i=NS)

    def turned(self, t):
        return t[:, :, :].rearrange("p b (i j) -> p b j i", i=NS)

    def over_j(self, t):
        return t[:, :, :].rearrange("p b (i o) -> p b i o", o=1).to_broadcast([P, self.n, NS, NS])

    def over_i(self, t):
        return t[:, :, :].rearrange("p b (o j) -> p b o j", o=1).to_broadcast([P, self.n, NS, NS])

    def rows_by(self, dst, src, t, op):
        return self.nc.vector.tensor_tensor(self.grid(dst), self.grid(src), self.over_j(t), op)

    def cols_by(self, dst, src, t, op):
        return self.nc.vector.tensor_tensor(self.grid(dst), self.grid(src), self.over_i(t), op)

    def row_sums(self, src, op=ALU.add):
        return self.nc.vector.tensor_reduce(self.red[:, :, :], self.grid(src), AX.X, op)

    def col_sums(self, src, op=ALU.add):
        return self.nc.vector.tensor_reduce(self.red[:, :, :], self.turned(src), AX.X, op)

    def first(self, k):
        return (lambda: self.row_sums(self.z, ALU.max),
                lambda: self.rows_by(self.tmp, self.z, self.red, ALU.subtract),
                lambda: self.row_sums(self.mat),
                lambda: self.rows_by(self.logm, self.tmp, self.lra, ALU.subtract),
                lambda: self.col_sums(self.logm, ALU.max),
                lambda: self.cols_by(self.tmp, self.logm, self.red, ALU.subtract),
                lambda: self.col_sums(self.mat),
                lambda: self.cols_by(self.logm, self.tmp, self.lcb, ALU.subtract))[k - 1]()

    def iteration(self, k):
        return (lambda: self.cols_by(self.tmp, self.mat, self.cb, ALU.mult),
                lambda: self.row_sums(self.tmp),
                lambda: self.nc.vector.reciprocal(self.ra[:, :, :], self.red[:, :, :]),
                lambda: self.rows_by(self.tmp, self.mat, self.ra, ALU.mult),
                lambda: self.col_sums(self.tmp),
                lambda: self.nc.vector.reciprocal(self.cb[:, :, :], self.red[:, :, :]))[k - 1]()

    def log(self, k):
        src, dst, func = ((self.tmp, self.mat, ACT.Exp), (self.red, self.lra, ACT.Ln), (self.tmp, self.mat, ACT.Exp),
                          (self.red, self.lcb, ACT.Ln), (self.logm, self.mat, ACT.Exp))[k - 1] if k <= FIRST_LOGS else (
                         (self.ra, self.lra, ACT.Ln), (self.cb, self.lcb, ACT.Ln), (self.logm, self.mat, ACT.Exp))[(k - FIRST_LOGS - 1) % BLOCK_LOGS]
        return self.nc.scalar.activation(dst[:, :, :], src[:, :, :], func)


def log_after(k):
    if k <= FIRST_LOGS:
        return (2, 3, 6, 7, 8)[k - 1]
    n, i = divmod(k - FIRST_LOGS - 1, BLOCK_LOGS)
    return BASES[n + 1] - (2, 2, 0)[i]


def sinkhorn_step(chain, k):
    if k <= FIRST:
        return chain.first(k)
    n = max(i for i, base in enumerate(BASES[:-1]) if k > base)
    if k == BASES[n] + 1:
        return chain.nc.vector.memset(chain.cb[:, :, :], 1.0)
    if k == BASES[n + 1] - 1:
        return chain.rows_by(chain.logm, chain.logm, chain.lra, ALU.add)
    if k == BASES[n + 1]:
        return chain.cols_by(chain.logm, chain.logm, chain.lcb, ALU.add)
    return chain.iteration((k - BASES[n] - 2) % 6 + 1)


def autocorrelation_phase(nc, x1, ctx_in, ident, dft, w24, base, wb, facts, early, rows):
    with ExitStack() as ctx:
        def sb(name, shape, dt=F32):
            return ctx.enter_context(nc.sbuf_tensor("c_" + name, shape, dt))

        def sem(name):
            return ctx.enter_context(nc.semaphore("c_" + name))

        idf = sb("b_idf", [P, P])
        mats = sb("mats", [P, N_DFT, P])
        fwd_hi = sb("fwd_hi", [P, 4, P], F32R)
        fwd_lo = sb("fwd_lo", [P, 4, P], F32R)
        w24_sb = sb("w24_sb", [P, KD, NLOG])
        base_sb = sb("base_sb", [P, NLOG])
        wb_sb = sb("wb_sb", [P, 2, C])
        xin = sb("xin", [P, D])
        xn = sb("xn", [P, D])
        xn_hi = sb("xn_hi", [P, D], F32R)
        xn_lo = sb("xn_lo", [P, D], F32R)
        xres = sb("b_xres", [P, D])
        cin = sb("cin", [P, D])
        c_hi = [sb(f"c_hi{i}", [P, D], F32R) for i in range(2)]
        c_lo = [sb(f"c_lo{i}", [P, D], F32R) for i in range(2)]
        spec = [[sb(f"spec{i}{n}", [P, D]) for n in range(4)] for i in range(2)]
        row = [sb(f"row{i}", [P, ROW]) for i in range(2)]
        tq = [sb(f"tq{i}", [P, D]) for i in range(2)]
        tw = [sb(f"tw{i}", [P, D]) for i in range(4)]
        pause = sb("pause", [P, 4])
        top = sb("top", [P, KD, 8])
        ntop = sb("ntop", [P, KD])
        corr = sb("corr", [P, KD, T])
        rest = sb("rest", [P, KD, T])
        ninth = sb("ninth", [P, KD])
        ex = sb("ex", [P, KD, T])
        wgt = sb("wgt", [P, KD, T])
        wsum = sb("wsum", [P, KD])
        wrec = sb("wrec", [P, KD])
        wT = sb("wT", [P, D])
        x2 = sb("x2", [P, D])
        x3T = sb("x3T", [P, KD, T])
        xp = sb("xp", [P, C])
        xpT = sb("xpT", [P, 2, T])
        st2 = sb("st2", [P, 2, 6])
        mv2 = sb("mv2", [P, 2])
        ve2 = sb("ve2", [P, 1])
        rstd2 = sb("rstd2", [P, 1])
        st3 = sb("st3", [P, 2, 6])
        mv3 = sb("mv3", [P, 2])
        ve3 = sb("ve3", [P, 1])
        rstd3 = sb("rstd3", [P, 1])
        nb2 = sb("nb2", [P, 2])
        nb3 = sb("nb3", [P, 2])
        ms = sb("ms", [P, 3])
        rs = sb("rs", [P, 1])
        consts = sb("consts", [P, 4])
        mhalf, one, rms_eps, minus = (consts[:, i:i + 1] for i in range(4))
        lg = sb("lg", [P, NLOG])
        hx = sb("hx", [P, 2])
        hd = sb("hd", [P, 2, NS])
        he = sb("he", [P, 2, NS])
        hs = sb("hs", [P, 2])
        hr = sb("hr", [P, 2])
        hp = sb("hp", [P, NS])

        pair = [ctx.enter_context(nc.psum_tensor(f"pair{i}", [P, 2, HALF], F32)) for i in range(4)]
        p_a, p_b, p_c, p_d = pair
        flat = [p[:, :, :].rearrange("p a n -> p (a n)") for p in pair]
        f_a, f_b, f_c, f_d = flat
        logits = p_d[:, 0, 0:NLOG]
        y_ps_at = p_d[:, 0, C:2 * C]
        xpT_at = p_d[:, 1, 0:2 * T]

        const_in = sem("const_in"); fwd_in = sem("fwd_in"); fwd_hi_done = sem("fwd_hi_done"); fwd_lo_done = sem("fwd_lo_done")
        consts_set = sem("consts_set")
        x_in = sem("x_in"); xres_in = sem("xres_in"); cin_in = sem("cin_in")
        row_out = [sem(f"row_out{i}") for i in range(2)]
        n2_step = sem("n2_step"); rstd2_done = sem("rstd2_done"); nb2_step = sem("nb2_step"); xn_done = sem("xn_done")
        xnh_done = sem("xnh_done"); xnl_done = sem("xnl_done")
        chi_done = sem("chi_done"); clo_done = sem("clo_done")
        k_ps = sem("k_ps"); k_done = sem("k_done"); v_ps = sem("v_ps"); v_done = sem("v_done")
        q_ps = sem("q_ps"); tq_done = sem("tq_done"); corr_ps = sem("corr_ps"); corr_done = sem("corr_done")
        max_done = sem("max_done"); ntop_done = sem("ntop_done"); rest_done = sem("rest_done")
        ninth_done = sem("ninth_done"); exp_done = sem("exp_done"); pick_done = sem("pick_done")
        wrec_done = sem("wrec_done"); w_done = sem("w_done")
        wT_ps = sem("wT_ps"); wT_done = sem("wT_done"); ws_ps = sem("ws_ps"); tw_done = sem("tw_done")
        out_ps = sem("out_ps"); x2_done = sem("x2_done"); n3_step = sem("n3_step"); rstd3_done = sem("rstd3_done")
        x3_done = sem("x3_done"); x3T_ps = sem("x3T_ps"); x3T_done = sem("x3T_done"); lg_ps = sem("lg_ps")
        pool_step = sem("pool_step"); rs_done = sem("rs_done"); h_step = sem("h_step"); he_done = sem("he_done")
        xp_step = sem("xp_step"); xpT_ps = sem("xpT_ps"); xpT_done = sem("xpT_done"); y_ps = sem("y_ps")
        y_done = sem("y_done")
        N3, PS, HS, XS = 4, 7, 8, 4

        shares = {EARLY + 1: (2, 0, 1, 0, 3), EARLY + 2: (0, 0, 1, 0, 1),
                  **{b: (0, 0, 14, 0, 16) if b == EARLY + 3 else (5, 8, 12, 0, 5) for b in range(EARLY + 3, RESTART)},
                  RESTART: (3, 8, 20, 2, 5)}
        shares.update({b: (5, 8, 12, 0, 5) for b in range(RESTART + 1, B - 1)})
        shares.update({B - 1: (8, 0, 14, 0, 20), B: (8, 0, 8, 0, 20), B + 1: (1000, 0, 0, 0, 0)})
        early_end = BASES[2] - 2 - 6 * EARLY_LEFT
        early_steps, k = {}, 0
        for b, share in shares.items():
            ends = []
            for part, steps in enumerate(share):
                end = BASES[1] - 2 if b < RESTART or (b == RESTART and part < 3) else early_end
                if b == RESTART and part == 2:
                    assert k + steps >= end
                if b == RESTART and part == 3:
                    assert k == BASES[1] - 2
                k = min(k + steps, end)
                ends.append(k)
            early_steps[b] = ends
        assert k == early_end
        early_logs = {EARLY + 1: ((1,), (2,)), EARLY + 2: ((3,), (4,)), EARLY + 3: ((5,), ()), RESTART: ((), (6, 7, 8))}

        block = ctx.enter_context(nc.Block())

        def iterations(engine, body):
            body(-1, 1, near=True, far=False, last=False, tail=False, ahead=True)
            body(0, 0, near=True, far=True, last=False, tail=False, ahead=True)
            body(1, 1, near=True, far=True, last=True, tail=False, ahead=True)
            body(2, 0, near=True, far=True, last=True, tail=True, ahead=True)
            with engine.Fori(0, (EARLY - 2) // 2) as u:
                body(2 * u + 3, 1, near=True, far=True, last=True, tail=True, ahead=True)
                body(2 * u + 4, 0, near=True, far=True, last=True, tail=True, ahead=True)
            for b in range(EARLY + 1, B - 2):
                body(b, b % 2, near=True, far=True, last=True, tail=True, ahead=True)
            body(B - 2, 0, near=True, far=True, last=True, tail=True, ahead=False)
            body(B - 1, 1, near=False, far=True, last=True, tail=True, ahead=False)
            body(B, 0, near=False, far=False, last=True, tail=True, ahead=False)
            body(B + 1, 1, near=False, far=False, last=False, tail=True, ahead=False)

        def later(b, first):
            return not isinstance(b, int) or b > first

        def turns(n, par):
            return n // 2 if isinstance(n, int) else (n - par) // 2

        facts_v = facts[:, :, :].rearrange("p (u s) n -> p u s n", s=2)

        def fact(n, par, at, width):
            return facts_v[:, turns(n, par), par, at:at + width]

        @block.sync
        def _(sp):
            sp.dma_start(xin[:], x1[0]).then_inc(x_in, 16)
            sp.dma_start(mats[:, 0:INV_OUT, :], dft[:, 0:INV_OUT, :]).then_inc(fwd_in, 16)
            sp.dma_start(cin[:], ctx_in[0]).then_inc(cin_in, 16)
            sp.dma_start(mats[:, INV_OUT:N_DFT, :], dft[:, INV_OUT:N_DFT, :]).then_inc(const_in, 16)
            sp.dma_start(idf[:], ident).then_inc(const_in, 16)
            sp.dma_start(w24_sb[:], w24).then_inc(const_in, 16)
            sp.dma_start(base_sb[:], base).then_inc(const_in, 16)
            sp.dma_start(wb_sb[:], wb.rearrange("(k p) n -> p k n", k=2)).then_inc(const_in, 16)

            def body(b, par, near, far, last, tail, ahead):
                if tail:
                    sp.wait_ge(y_done, b - 1)
                    sp.dma_start(rows[b - 2], row[par][:]).then_inc(row_out[par], 16)
                if ahead:
                    sp.wait_ge(chi_done, b + 2)
                    sp.wait_ge(clo_done, b + 2)
                    sp.dma_start(cin[:], ctx_in[b + 2]).then_inc(cin_in, 16)
                    sp.wait_ge(xn_done, b + 2)
                    sp.dma_start(xin[:], x1[b + 2]).then_inc(x_in, 16)
                if far:
                    if near or last:
                        if later(b, 0):
                            sp.wait_ge(x2_done, 2 * b)
                    sp.dma_start(xres[:], x1[b]).then_inc(xres_in, 16)

            iterations(sp, body)
            for i in range(2):
                sp.wait_ge(row_out[i], 8 * B)

        @block.tensor
        def _(pe):
            def split3(dst, i, hi, lo):
                for n in range(2):
                    cols = slice(n * HALF, (n + 1) * HALF)
                    nc.tensor.matmul(dst[:, n, :], fwd_hi[:, i, :], hi[:, cols], start=True, stop=False)
                    nc.tensor.matmul(dst[:, n, :], fwd_hi[:, i, :], lo[:, cols], start=False, stop=False)
                    r = nc.tensor.matmul(dst[:, n, :], fwd_lo[:, i, :], hi[:, cols], start=False, stop=True)
                return r

            def spectrum(dst, i, src):
                for n in range(2):
                    r = nc.tensor.matmul(dst[:, n, :], mats[:, i, :], src[:, n * HALF:(n + 1) * HALF], start=True, stop=True)
                return r

            def out_half(n):
                for i in range(4):
                    r = nc.tensor.matmul(p_b[:, n, :], mats[:, INV_OUT + i, :], tw[i][:, n * HALF:(n + 1) * HALF],
                                         start=i == 0, stop=i == 3)
                r.then_inc(out_ps, 1)

            def body(b, par, near, far, last, tail, ahead):
                c = b + 1
                if near:
                    pe.wait_ge(xnh_done, c + 1)
                    pe.wait_ge(xnl_done, c + 1)
                    if not far:
                        pe.wait_ge(fwd_hi_done, 1)
                        pe.wait_ge(fwd_lo_done, 1)
                    if far:
                        pe.wait_ge(v_done, 2 * b + 1)
                    split3(p_a, FWD_A, xn_hi, xn_lo).then_inc(q_ps, 1)
                if tail:
                    pe.wait_ge(xp_step, XS * (b - 1))
                    pe.wait_ge(x3T_done, 2 * (b - 1))
                    for i in range(2):
                        r = nc.tensor.transpose(xpT_at[:, i * T:(i + 1) * T], xp[:, i * P:(i + 1) * P], idf[:])
                    r.then_inc(xpT_ps, 1)
                if near:
                    pe.wait_ge(chi_done, c + 1)
                    pe.wait_ge(clo_done, c + 1)
                    if last:
                        pe.wait_ge(x2_done, 2 * b)
                    split3(p_b, 0, c_hi[1 - par], c_lo[1 - par]).then_inc(k_ps, 1)
                if tail:
                    pe.wait_ge(xpT_done, b - 1)
                    for i in range(2):
                        r = nc.tensor.matmul(y_ps_at, xpT[:, i, :], wb_sb[:, i, :], start=i == 0, stop=i == 1)
                    r.then_inc(y_ps, 1)
                    pe.wait_ge(y_done, b - 1)
                if far:
                    pe.wait_ge(w_done, b + 1)
                    for i in range(KD):
                        r = nc.tensor.transpose(f_d[:, i * T:(i + 1) * T], wgt[:, i, :], idf[:])
                    r.then_inc(wT_ps, 1)
                if near:
                    if far:
                        pe.wait_ge(v_done, 2 * b + 2)
                    split3(p_c, 1, c_hi[1 - par], c_lo[1 - par]).then_inc(k_ps, 1)
                if far:
                    pe.wait_ge(wT_done, 2 * b + 2)
                    if near:
                        pe.wait_ge(k_done, 2 * c + 1)
                    else:
                        pe.wait_ge(x2_done, 2 * b)
                        pe.wait_ge(v_done, 2 * b + 2)
                    spectrum(p_b, FWD_A, wT).then_inc(ws_ps, 1)
                    if near:
                        pe.wait_ge(k_done, 2 * c + 2)
                    spectrum(p_c, FWD_ODD, wT).then_inc(ws_ps, 1)
                if near:
                    if not far:
                        pe.wait_ge(const_in, 80)
                    for n in range(2):
                        pe.wait_ge(tq_done, 2 * c + 2)
                        for i in range(4 * n, 4 * n + 4):
                            for t in range(2):
                                r = nc.tensor.matmul(f_a[:, i * T:(i + 1) * T], tq[t][:, i * P:(i + 1) * P], mats[:, INV_CORR + t, :],
                                                     start=t == 0, stop=t == 1)
                        r.then_inc(corr_ps, 1)
                if last:
                    pe.wait_ge(x3_done, b)
                    for i in range(KD):
                        r = nc.tensor.transpose(f_d[:, i * T:(i + 1) * T], row[1 - par][:, i * P:(i + 1) * P], idf[:])
                        if i % 4 == 3:
                            r.then_inc(x3T_ps, 1)
                if far:
                    pe.wait_ge(tw_done, 4 * b + 4)
                    out_half(0)
                if last:
                    pe.wait_ge(x3T_done, 2 * b)
                    for i in range(KD):
                        r = nc.tensor.matmul(logits, x3T[:, i, :], w24_sb[:, i, :], start=i == 0, stop=i == KD - 1)
                    r.then_inc(lg_ps, 1)
                if far:
                    out_half(1)
                if near:
                    pe.wait_ge(corr_done, 2 * c + 2)
                    split3(p_a, 2, c_hi[1 - par], c_lo[1 - par]).then_inc(v_ps, 1)
                    split3(p_c, 3, c_hi[1 - par], c_lo[1 - par]).then_inc(v_ps, 1)

            pe.wait_ge(fwd_in, 16)
            iterations(pe, body)

        @block.scalar
        def _(act):
            act.wait_ge(fwd_in, 16)
            nc.scalar.activation(fwd_hi[:, :, :], mats[:, 0:4, :], ACT.Copy).then_inc(fwd_hi_done, 1)

            def split_context(n, par):
                act.wait_ge(cin_in, 16 * (n + 1))
                if later(n, 1):
                    act.wait_ge(v_ps, 2 * (n - 1))
                nc.scalar.activation(c_hi[par][:], cin[:], ACT.Copy).then_inc(chi_done, 1)

            def normalise(n):
                act.wait_ge(nb2_step, 2 * (n + 1))
                if later(n, 0):
                    act.wait_ge(xnl_done, n)
                nc.scalar.activation(xn[:], xin[:], ACT.Identity, bias=nb2[:, 1:2], scale=rstd2[:]).then_inc(xn_done, 1)
                act.wait_ge(xn_done, n + 1)
                if later(n, 0):
                    act.wait_ge(q_ps, n)
                nc.scalar.activation(xn_hi[:], xn[:], ACT.Copy).then_inc(xnh_done, 1)

            def early_log(b, part):
                if isinstance(b, int):
                    for k in early_logs.get(b, ((), ()))[part]:
                        act.wait_ge(early.step, log_after(k))
                        early.log(k).then_inc(early.logs, 1)

            split_context(0, 0)
            normalise(0)

            def body(b, par, near, far, last, tail, ahead):
                c = b + 1

                def key_spectrum(i, src):
                    act.wait_ge(k_ps, 2 * c + i + 1)
                    if last:
                        act.wait_ge(tw_done, 4 * b)
                    nc.scalar.activation(spec[1 - par][i][:], src, ACT.Copy).then_inc(k_done, 1)

                if tail:
                    act.wait_ge(xpT_ps, b - 1)
                    nc.scalar.activation(xpT[:, :, :], xpT_at, ACT.Copy).then_inc(xpT_done, 1)
                if near:
                    key_spectrum(0, f_b)
                if tail:
                    act.wait_ge(y_ps, b - 1)
                    nc.scalar.activation(row[par][:, D:D + C], y_ps_at, ACT.Copy).then_inc(y_done, 1)
                if far:
                    act.wait_ge(wT_ps, b + 1)
                    for n in range(2):
                        nc.scalar.activation(wT[:, n * HALF:(n + 1) * HALF], p_d[:, n, :], ACT.Copy).then_inc(wT_done, 1)
                if near:
                    key_spectrum(1, f_c)
                if last:
                    act.wait_ge(pool_step, PS * (b - 1) + 2)
                    if tail and later(b, 2):
                        act.wait_ge(row_out[1 - par], 16 * turns(b - 1, 1 - par))
                    nc.scalar.activation(row[1 - par][:, 0:D], x2[:], ACT.Identity, bias=nb3[:, 1:2],
                                         scale=rstd3[:]).then_inc(x3_done, 1)
                if ahead:
                    split_context(b + 2, par)
                early_log(b, 0)
                if near:
                    if far:
                        act.wait_ge(pick_done, 8 * c)
                    for n in range(2):
                        act.wait_ge(corr_ps, 2 * c + n + 1)
                        nc.scalar.activation(corr[:, 4 * n:4 * n + 4, :], p_a[:, n, :], ACT.Copy).then_inc(corr_done, 1)
                if last:
                    for n in range(2):
                        act.wait_ge(x3T_ps, 2 * (b - 1) + n + 1)
                        nc.scalar.activation(x3T[:, 4 * n:4 * n + 4, :], p_d[:, n, :], ACT.Copy).then_inc(x3T_done, 1)
                if ahead:
                    normalise(b + 2)
                if near:
                    act.wait_ge(ntop_done, c + 1)
                    for i in range(KD):
                        nc.scalar.activation(ex[:, i, :], corr[:, i, :], ACT.Exp,
                                             bias=ntop[:, i:i + 1]).then_inc(exp_done, 1)
                if last:
                    act.wait_ge(h_step, HS * (b - 1) + 3)
                    nc.scalar.activation(he[:, :, :], hd[:, :, :], ACT.Exp).then_inc(he_done, 1)
                early_log(b, 1)
                if near:
                    for i, src in ((2, f_a), (3, f_c)):
                        act.wait_ge(v_ps, 2 * c + i - 1)
                        nc.scalar.activation(spec[1 - par][i][:], src, ACT.Copy).then_inc(v_done, 1)

            iterations(act, body)

        @block.vector
        def _(dve):
            dve.wait_ge(fwd_hi_done, 1)
            nc.vector.tensor_tensor(fwd_lo[:, :, :], mats[:, 0:4, :], fwd_hi[:, :, :].bitcast(F32),
                                    ALU.subtract).then_inc(fwd_lo_done, 1)

            def norm2_stats(n):
                dve.wait_ge(x_in, 16 * (n + 1))
                for i in range(2):
                    nc.vector.bn_stats(st2[:, i, :], xin[:, i * HALF:(i + 1) * HALF]).then_inc(n2_step, 1)
                dve.wait_ge(n2_step, 4 * n + 2)
                nc.vector.memset(pause[:, 2:3], 0.0)
                nc.vector.bn_aggr(mv2[:], st2[:, :, :]).then_inc(n2_step, 1)
                dve.wait_ge(n2_step, 4 * n + 3)
                nc.vector.tensor_scalar(ve2[:], mv2[:, 1:2], LN_EPS, None, ALU.add).then_inc(n2_step, 1)

            norm2_stats(0)
            issued = [0]

            def sink(to, most=1000):
                for k in range(issued[0] + 1, min(to, issued[0] + most) + 1):
                    if k > 1:
                        dve.wait_ge(early.step, k - 1)
                    if k in (3, 4, 7, 8):
                        dve.wait_ge(early.logs, {3: 1, 4: 2, 7: 3, 8: 4}[k])
                    for n in range(len(BLOCK_ITERS)):
                        if k == BASES[n] + 2:
                            dve.wait_ge(early.logs, FIRST_LOGS + n * BLOCK_LOGS)
                        if k == BASES[n + 1] - 1:
                            dve.wait_ge(early.logs, FIRST_LOGS + n * BLOCK_LOGS + 2)
                    sinkhorn_step(early, k).then_inc(early.step, 1)
                    issued[0] = k

            def beside(b, part):
                if isinstance(b, int) and b > EARLY + 2 and b in early_steps:
                    if issued[0] + 1 not in (BASES[1] - 1, BASES[1], BASES[2] - 1, BASES[2]):
                        sink(early_steps[b][part], 1)

            def up_to(b, part):
                if isinstance(b, int) and b in early_steps:
                    sink(early_steps[b][part])

            def body(b, par, near, far, last, tail, ahead):
                c = b + 1
                m = b - 1

                def products():
                    for i, src in enumerate((f_b, f_b, f_c, f_c)):
                        if i % 2 == 0:
                            dve.wait_ge(ws_ps, 2 * b + i // 2 + 1)
                            if i == 0:
                                dve.wait_ge(v_done, 2 * b + 2)
                                if last:
                                    dve.wait_ge(out_ps, 2 * b)
                        nc.vector.tensor_tensor(tw[i][:], src, spec[par][i][:], ALU.mult).then_inc(tw_done, 1)

                def h_steps(first, to):
                    pp = lg[:, NS * NS:NLOG].rearrange("p (a n) -> p a n", a=2)
                    for k in range(first, to + 1):
                        if k == 1:
                            dve.wait_ge(lg_ps, b)
                            dve.wait_ge(rs_done, b)
                            ins = nc.vector.scalar_tensor_tensor(lg[:], logits, rs[:], base_sb[:], ALU.mult, ALU.add)
                        else:
                            dve.wait_ge(h_step, HS * m + k - 1)
                        if k == 2:
                            ins = nc.vector.tensor_reduce(hx[:], pp, AX.X, ALU.max)
                        if k == 3:
                            ins = nc.vector.tensor_tensor(hd[:, :, :], pp, hx[:].rearrange("p (a o) -> p a o", o=1).to_broadcast([P, 2, NS]), ALU.subtract)
                        if k == 4:
                            ins = nc.vector.tensor_scalar(fact(m, 1 - par, 0, NS * NS), lg[:, 0:NS * NS], 1.0 / TAU, None, ALU.mult)
                        if k == 5:
                            dve.wait_ge(he_done, b)
                            ins = nc.vector.tensor_reduce(hs[:], he[:, :, :], AX.X, ALU.add)
                        if k == 6:
                            ins = nc.vector.reciprocal(hr[:], hs[:])
                        if k == 7:
                            ins = nc.vector.tensor_scalar(fact(m, 1 - par, AT_POST, NS), he[:, 1, :], hr[:, 1:2], None, ALU.mult)
                        if k == 8:
                            ins = nc.vector.tensor_scalar(hp[:], he[:, 0, :], hr[:, 0:1], None, ALU.mult)
                        ins.then_inc(h_step, 1)
                        beside(b, 2 if k <= 4 else 4)

                def branch_in(n):
                    x = row[1 - par][:, n * C:(n + 1) * C]
                    if n == 0:
                        dve.wait_ge(h_step, HS * m + HS)
                        if later(b, 1):
                            dve.wait_ge(xpT_ps, b - 1)
                        ins = nc.vector.tensor_scalar(xp[:], x, hp[:, 0:1], None, ALU.mult)
                    else:
                        dve.wait_ge(xp_step, XS * m + n)
                        ins = nc.vector.scalar_tensor_tensor(xp[:], x, hp[:, n:n + 1], xp[:], ALU.mult, ALU.add)
                    ins.then_inc(xp_step, 1)
                    beside(b, 4)

                up_to(b, 0)
                if near:
                    dve.wait_ge(q_ps, c + 1)
                    if far:
                        dve.wait_ge(corr_ps, 2 * c)
                    for i in range(2):
                        dve.wait_ge(k_done, 2 * c + i + 1)
                        nc.vector.tensor_tensor(tq[i][:], f_a, spec[1 - par][i][:], ALU.mult).then_inc(tq_done, 1)
                        if i == 0:
                            up_to(b, 1)
                if far:
                    products()
                if ahead:
                    norm2_stats(b + 2)
                if near:
                    for i in range(KD):
                        if i % 4 == 0:
                            dve.wait_ge(corr_done, 2 * c + i // 4 + 1)
                            nc.vector.memset(pause[:, i // 4:i // 4 + 1], 0.0)
                        nc.vector.max(top[:, i, :], corr[:, i, :]).then_inc(max_done, 1)
                        beside(b, 2)
                    dve.wait_ge(max_done, 8 * c + 8)
                    nc.vector.tensor_scalar(ntop[:], top[:, :, 0], -1.0, None, ALU.mult).then_inc(ntop_done, 1)
                    for i in range(KD):
                        nc.vector.match_replace(rest[:, i, :], top[:, i, :], corr[:, i, :], NEG).then_inc(rest_done, 1)
                        beside(b, 2)
                if near:
                    dve.wait_ge(rest_done, 8 * c + 8)
                    nc.vector.tensor_reduce(ninth[:], rest[:, :, :], AX.X, ALU.max).then_inc(ninth_done, 1)
                if last:
                    h_steps(1, 2)
                if last:
                    h_steps(3, 4)
                up_to(b, 2)
                if near:
                    dve.wait_ge(ninth_done, c + 1)
                    if far:
                        dve.wait_ge(wT_ps, b + 1)
                    for i in range(KD):
                        dve.wait_ge(exp_done, 8 * c + i + 1)
                        nc.vector.scalar_tensor_tensor(wgt[:, i, :], corr[:, i, :], ninth[:, i:i + 1], ex[:, i, :],
                                                       ALU.is_ge, ALU.mult, accum_out=wsum[:, i:i + 1]).then_inc(pick_done, 1)
                if near:
                    dve.wait_ge(pick_done, 8 * c + 8)
                    nc.vector.reciprocal(wrec[:], wsum[:]).then_inc(wrec_done, 1)
                up_to(b, 3)
                if last:
                    h_steps(5, 8)
                    branch_in(0)
                if far:
                    dve.wait_ge(xres_in, 16 * (b + 1))
                    if last:
                        dve.wait_ge(x3_done, b)
                for n in range(2):
                    if far:
                        dve.wait_ge(out_ps, 2 * b + n + 1)
                        cols = slice(n * HALF, (n + 1) * HALF)
                        nc.vector.tensor_tensor(x2[:, cols], p_b[:, n, :], xres[:, cols], ALU.add).then_inc(x2_done, 1)
                        beside(b, 4)
                    if last and n == 0:
                        branch_in(1)
                        branch_in(2)
                        branch_in(3)
                if far:
                    for n in range(2):
                        dve.wait_ge(x2_done, 2 * b + n + 1)
                        nc.vector.bn_stats(st3[:, n, :], x2[:, n * HALF:(n + 1) * HALF]).then_inc(n3_step, 1)
                        beside(b, 4)
                    dve.wait_ge(n3_step, N3 * b + 2)
                    if last:
                        dve.wait_ge(pool_step, PS * b)
                    nc.vector.memset(pause[:, 3:4], 0.0)
                    nc.vector.bn_aggr(mv3[:], st3[:, :, :]).then_inc(n3_step, 1)
                    dve.wait_ge(n3_step, N3 * b + 3)
                    nc.vector.tensor_scalar(ve3[:], mv3[:, 1:2], LN_EPS, None, ALU.add).then_inc(n3_step, 1)
                up_to(b, 4)

            iterations(dve, body)

        @block.gpsimd
        def _(pool):
            for at, value in ((mhalf, -0.5), (one, 1.0), (rms_eps, RMS_EPS), (minus, -1.0)):
                nc.gpsimd.memset(at, value).then_inc(consts_set, 1)
            pool.wait_ge(consts_set, 4)
            TT = nc.gpsimd.tensor_tensor

            def split_context(n, par):
                pool.wait_ge(chi_done, n + 1)
                if later(n, 1):
                    pool.wait_ge(v_ps, 2 * (n - 1))
                TT(c_lo[par][:], cin[:], c_hi[par][:].bitcast(F32), ALU.subtract).then_inc(clo_done, 1)

            def norm2(n):
                pool.wait_ge(n2_step, 4 * n + 4)
                TT(rstd2[:], ve2[:], mhalf, ALU.pow).then_inc(rstd2_done, 1)
                pool.wait_ge(rstd2_done, n + 1)
                TT(nb2[:, 0:1], mv2[:, 0:1], rstd2[:], ALU.mult).then_inc(nb2_step, 1)
                pool.wait_ge(nb2_step, 2 * n + 1)
                TT(nb2[:, 1:2], nb2[:, 0:1], minus, ALU.mult).then_inc(nb2_step, 1)

            def split_normalised(n):
                pool.wait_ge(xnh_done, n + 1)
                if later(n, 0):
                    pool.wait_ge(q_ps, n)
                TT(xn_lo[:], xn[:], xn_hi[:].bitcast(F32), ALU.subtract).then_inc(xnl_done, 1)

            norm2(0)
            split_context(0, 0)
            split_normalised(0)

            def body(b, par, near, far, last, tail, ahead):
                c = b + 1
                if ahead:
                    split_context(b + 2, par)
                    norm2(b + 2)
                    split_normalised(b + 2)
                if near:
                    pool.wait_ge(wrec_done, c + 1)
                    TT(wgt[:, :, :], wgt[:, :, :], wrec[:].rearrange("p (k o) -> p k o", o=1).to_broadcast([P, KD, T]),
                       ALU.mult).then_inc(w_done, 1)
                if far:
                    def step(k, ins):
                        ins.then_inc(pool_step, 1)
                        pool.wait_ge(pool_step, PS * b + k)

                    pool.wait_ge(n3_step, N3 * b + 4)
                    TT(rstd3[:], ve3[:], mhalf, ALU.pow).then_inc(rstd3_done, 1)
                    pool.wait_ge(rstd3_done, b + 1)
                    step(1, TT(nb3[:, 0:1], mv3[:, 0:1], rstd3[:], ALU.mult))
                    step(2, TT(nb3[:, 1:2], nb3[:, 0:1], minus, ALU.mult))
                    step(3, TT(fact(b, par, AT_SD, 1), ve3[:], rstd3[:], ALU.mult))
                    step(4, TT(fact(b, par, AT_MEAN, 1), mv3[:, 0:1], one, ALU.mult))
                    step(5, TT(ms[:, 0:1], mv3[:, 1:2], rstd3[:], ALU.mult))
                    step(6, TT(ms[:, 1:2], ms[:, 0:1], rstd3[:], ALU.mult))
                    step(7, TT(ms[:, 2:3], ms[:, 1:2], rms_eps, ALU.add))
                    if last:
                        pool.wait_ge(h_step, HS * (b - 1) + 1)
                    TT(rs[:], ms[:, 2:3], mhalf, ALU.pow).then_inc(rs_done, 1)

            iterations(pool, body)


def mixing_phase(nc, rows, facts, early, gate, ident, out):
    with ExitStack() as ctx:
        def sb(name, shape, dt=F32):
            return ctx.enter_context(nc.sbuf_tensor("m_" + name, shape, dt))

        def sem(name):
            return ctx.enter_context(nc.semaphore("m_" + name))

        PE_SEQS = 10
        HB = (B - EARLY) // 2
        N2 = NS * NS
        NC = N2 + NS + 1
        late_h = sb("late_h", [P, B - EARLY, N2])
        chains = [Chain(nc, ctx, f"m_late{h}", facts[:, EARLY + h * HB:EARLY + (h + 1) * HB, 0:N2],
                        late_h[:, h * HB:(h + 1) * HB, :]) for h in range(2)]
        coef = sb("coef", [P, B, NC])
        gt = sb("gt", [P, 4])
        ones = sb("ones", [P, NC])

        gate_in = sem("gate_in"); g_exp = sem("g_exp")
        coef_step = sem("coef_step"); ones_set = sem("ones_set"); id_in = sem("id_in")
        mean_done = sem("mean_done"); diag_done = sem("diag_done"); pe_done = sem("pe_done")
        EARLY_COEFS, LATE_COEFS = 6, 9
        ident_sb = sb("ident_sb", [P, P])

        PRODUCTS = NS * (NS + 1)

        class Mixer:
            def __init__(self, name, first, to, steps):
                self.first, self.count, self.steps = first, to - first, steps
                self.ot = [sb(f"ot_{name}{i}", [P, D]) for i in range(2)]
                self.stored = [sem(f"stored_{name}{i}") for i in range(2)]
                self.mixed = sem(f"mixed_{name}")

        late_row = [sb(f"late_row{n}", [P, ROW]) for n in range(B - EARLY)]
        late_in = sem("late_in")

        by_pe, by_dve = Mixer("pe", 0, PE_SEQS, 1), Mixer("dve", PE_SEQS, B - 1, PRODUCTS)
        pool_ot, pool_part = sb("pool_ot", [P, D]), sb("pool_part", [P, D])
        pool_step = sem("pool_step"); pool_stored = sem("pool_stored")
        by_pe.xr = [sb(f"xr{i}", [P, ROW]) for i in range(2)]
        by_pe.row_in = [sem(f"row_in{i}") for i in range(2)]
        now = [sb(f"now{i}", [P, NC]) for i in range(2)]
        now_done = sem("now_done")
        mean = [sb(f"mean{i}", [P, 1]) for i in range(2)]
        diag = [sb(f"diag{i}", [P, PRODUCTS, P]) for i in range(2)]
        p_out = [ctx.enter_context(nc.psum_tensor(f"p_out{i}", [P, D], F32)) for i in range(2)]

        block = ctx.enter_context(nc.Block())

        UNROLL = 4

        def turn(n, i):
            return 16 * (n // 2) if isinstance(n, int) else 8 * (n - i)

        def in_turn(engine, body, count):
            body(0, 0, True)
            body(1, 1, True)
            with engine.Fori(1, count // 2) as u:
                for i in range(2):
                    body(2 * u + i, i, False)
            if count % 2:
                body(count - 1, 0, False)

        @block.sync
        def _(sp):
            sp.dma_start(gt[:, 0:1], gate).then_inc(gate_in, 16)
            sp.dma_start(ident_sb[:], ident).then_inc(id_in, 16)

            def bring(m, n, i):
                sp.dma_start(m.xr[i][:], rows[m.first + n]).then_inc(m.row_in[i], 16)

            def keep(m, n, i):
                sp.wait_ge(m.mixed, m.steps * (n + 1))
                sp.wait_ge(gate_in, 16)
                sp.dma_start(out[m.first + n], m.ot[i][:]).then_inc(m.stored[i], 16)

            for n in range(2):
                bring(by_pe, n, n)
            for n in range(B - EARLY):
                sp.dma_start(late_row[n][:], rows[EARLY + n]).then_inc(late_in, 16)
            with sp.Fori(0, EARLY // 2 - 1) as u:
                for i in range(2):
                    keep(by_pe, 2 * u + i, i)
                    bring(by_pe, 2 * u + i + 2, i)
            for i in range(2):
                keep(by_pe, EARLY - 2 + i, i)
            for t in range(max(by_dve.count, by_pe.count - EARLY)):
                for m, n in ((by_dve, t), (by_pe, EARLY + t)):
                    if n < m.count:
                        keep(m, n, n % 2)
            sp.wait_ge(pool_step, PRODUCTS + NS)
            sp.wait_ge(gate_in, 16)
            sp.dma_start(out[B - 1], pool_ot[:]).then_inc(pool_stored, 16)
            sp.wait_ge(pool_stored, 16)
            mixers = (by_pe, by_dve)
            for m in mixers:
                for i in range(2):
                    sp.wait_ge(m.stored[i], 16 * ((m.count + 1 - i) // 2))

        @block.tensor
        def _(pe):
            m = by_pe

            def mix(n, i, first, late=False):
                if late:
                    pe.wait_ge(late_in, 16 * (B - EARLY))
                else:
                    pe.wait_ge(m.row_in[i], turn(n, i) + 16)
                x = late_row[n - EARLY] if late else m.xr[i]
                if not first:
                    pe.wait_ge(m.mixed, n - 1)
                for to in range(NS):
                    pe.wait_ge(diag_done, 2 * (NS * n + to + 1))
                    for j in range(NS + 1):
                        at = (NS + 1) * to + j
                        r = nc.tensor.matmul(p_out[i][:, to * C:(to + 1) * C], diag[i][:, at, :], x[:, j * C:(j + 1) * C],
                                             start=j == 0, stop=j == NS)
                r.then_inc(pe_done, 1)

            in_turn(pe, mix, EARLY)
            for n in range(EARLY, by_pe.count):
                mix(n, n % 2, False, late=True)

        @block.scalar
        def _(act):
            act.wait_ge(gate_in, 16)
            nc.scalar.activation(gt[:, 1:2], gt[:, 0:1], ACT.Exp, scale=-1.0).then_inc(g_exp, 1)

            def logs(first, to):
                for k in range(first, to + 1):
                    for chain in chains:
                        act.wait_ge(chain.step, log_after(k))
                        chain.log(k).then_inc(chain.logs, 1)

            m = by_pe

            LOGS_AT = (2, EARLY)

            def out_of_psum(n, i, first):
                act.wait_ge(pe_done, n + 1)
                act.wait_ge(mean_done, n + 1)
                if not first:
                    act.wait_ge(m.stored[i], turn(n, i))
                nc.scalar.activation(m.ot[i][:], p_out[i][:], ACT.Identity, bias=mean[i][:]).then_inc(m.mixed, 1)

            logs(1, FIRST_LOGS)
            for k in range(FIRST_LOGS + BLOCK_LOGS + 1, FIRST_LOGS + 2 * BLOCK_LOGS + 1):
                act.wait_ge(early.step, log_after(k))
                early.log(k).then_inc(early.logs, 1)
            for n in range(by_pe.count):
                if n == LOGS_AT[0]:
                    logs(FIRST_LOGS + 1, FIRST_LOGS + BLOCK_LOGS)
                if n == LOGS_AT[1]:
                    logs(FIRST_LOGS + BLOCK_LOGS + 1, FIRST_LOGS + 2 * BLOCK_LOGS)
                out_of_psum(n, n % 2, n < 2)

        @block.vector
        def _(dve):
            links = [0]

            def link(ins):
                links[0] += 1
                ins.then_inc(coef_step, 1)
                dve.wait_ge(coef_step, links[0])

            def coefficients(h, first, to):
                link(nc.vector.tensor_scalar(coef[:, first:to, 0:N2], h[:, :, :], gt[:, 3:4], None, ALU.mult))
                of_self = coef[:, first:to, 0:N2:NS + 1]
                sd = facts[:, first:to, AT_SD:AT_SD + 1].to_broadcast([P, to - first, NS])
                link(nc.vector.scalar_tensor_tensor(of_self, of_self, gt[:, 0:1], sd, ALU.add, ALU.add))
                link(nc.vector.tensor_copy(coef[:, first:to, N2:NC], facts[:, first:to, N2:NC]))

            def both(k, compute):
                for chain in chains:
                    if not isinstance(k, int) or k > 1:
                        dve.wait_ge(chain.step, k - 1)
                    compute(chain).then_inc(chain.step, 1)

            def logs_done(k):
                for chain in chains:
                    dve.wait_ge(chain.logs, k)

            issued = [BASES[2] - 2 - 6 * EARLY_LEFT]

            def early_iterations(steps):
                for k in range(issued[0] + 1, min(issued[0] + steps, BASES[2] - 2) + 1):
                    dve.wait_ge(early.step, k - 1)
                    sinkhorn_step(early, k).then_inc(early.step, 1)
                    issued[0] = k

            for k in range(1, FIRST + 1):
                if k in (3, 4, 7, 8):
                    early_iterations(4)
                    logs_done({3: 1, 4: 2, 7: 3, 8: 4}[k])
                both(k, lambda chain: chain.first(k))

            def iteration(base, steps=0):
                for k in range(1, 7):
                    both(base + k, lambda chain: chain.iteration(k))
                    early_iterations(steps)

            for n, size in enumerate(BLOCK_ITERS):
                base = BASES[n] + 1
                both(base, lambda chain: nc.vector.memset(chain.cb[:, :, :], 1.0))
                if n == 0:
                    early_iterations(4)
                logs_done(FIRST_LOGS + n * BLOCK_LOGS)
                straight = size % UNROLL + (2 * UNROLL if n == 0 else 0)
                for i in range(straight):
                    if n == 0 and i == straight - 4:
                        assert issued[0] == BASES[2] - 2
                    if n == 0 and i == straight - 2:
                        dve.wait_ge(early.logs, FIRST_LOGS + BLOCK_LOGS + 2)
                        early.rows_by(early.logm, early.logm, early.lra, ALU.add).then_inc(early.step, 1)
                        dve.wait_ge(early.step, BASES[2] - 1)
                        early.cols_by(early.logm, early.logm, early.lcb, ALU.add).then_inc(early.step, 1)
                    iteration(base + 6 * i, 1 if n == 0 else 0)
                if n == 0:
                    dve.wait_ge(g_exp, 1)
                    link(nc.vector.tensor_scalar(gt[:, 2:3], gt[:, 1:2], 1.0, None, ALU.add))
                    link(nc.vector.reciprocal(gt[:, 3:4], gt[:, 2:3]))
                    link(nc.vector.tensor_scalar(gt[:, 0:1], gt[:, 3:4], -1.0, 1.0, ALU.mult, ALU.add))
                    dve.wait_ge(early.logs, FIRST_LOGS + 2 * BLOCK_LOGS)
                    coefficients(early.mat, 0, EARLY)
                base += 6 * straight
                with dve.Fori(0, (size - straight) // UNROLL) as t:
                    for i in range(UNROLL):
                        iteration(base + 6 * UNROLL * t + 6 * i)
                logs_done(FIRST_LOGS + n * BLOCK_LOGS + 2)
                both(BASES[n + 1] - 1, lambda chain: chain.rows_by(chain.logm, chain.logm, chain.lra, ALU.add))
                both(BASES[n + 1], lambda chain: chain.cols_by(chain.logm, chain.logm, chain.lcb, ALU.add))
            logs_done(FIRST_LOGS + len(BLOCK_ITERS) * BLOCK_LOGS)
            coefficients(late_h, EARLY, B)

            m = by_dve

            def mix(n, i, first):
                nc.vector.tensor_copy(now[i][:], coef[:, m.first + n, :]).then_inc(now_done, 1)
                dve.wait_ge(late_in, 16 * (B - EARLY))
                if not first:
                    dve.wait_ge(m.stored[i], turn(n, i))
                dve.wait_ge(now_done, n + 1)
                w, x, o = now[i], late_row[m.first + n - EARLY], m.ot[i]
                for j in range(NS + 1):
                    for to in range(NS):
                        dst = o[:, to * C:(to + 1) * C]
                        if j == 0:
                            r = nc.vector.tensor_scalar(dst, x[:, 0:C], w[:, NS * to:NS * to + 1], w[:, NC - 1:NC], ALU.mult, ALU.add)
                        else:
                            at = NS * to + j if j < NS else N2 + to
                            dve.wait_ge(m.mixed, PRODUCTS * n + 4 * (j - 1) + to + 1)
                            r = nc.vector.scalar_tensor_tensor(dst, x[:, j * C:(j + 1) * C], w[:, at:at + 1], dst, ALU.mult, ALU.add)
                        r.then_inc(m.mixed, 1)

            for n in range(by_dve.count):
                mix(n, n % 2, n < 2)

        @block.gpsimd
        def _(pool):
            nc.gpsimd.memset(ones[:], 1.0).then_inc(ones_set, 1)
            pool.wait_ge(ones_set, 1)
            pool.wait_ge(id_in, 16)

            def diagonals(n, i, first):
                if not first:
                    pool.wait_ge(by_pe.mixed, n - 1)
                at = coef[:, by_pe.first + n, :]
                for to in range(NS):
                    own = at[:, to * NS:(to + 1) * NS]
                    nc.gpsimd.tensor_tensor(diag[i][:, (NS + 1) * to:(NS + 1) * to + NS, :],
                                            ident_sb[:, :].rearrange("p (o t) -> p o t", o=1).to_broadcast([P, NS, P]),
                                            own.rearrange("p (k o) -> p k o", o=1).to_broadcast([P, NS, P]), ALU.mult).then_inc(diag_done, 1)
                    nc.gpsimd.tensor_tensor(diag[i][:, (NS + 1) * to + NS, :], ident_sb[:, :],
                                            at[:, N2 + to:N2 + to + 1].to_broadcast([P, P]), ALU.mult).then_inc(diag_done, 1)
                nc.gpsimd.tensor_tensor(mean[i][:], at[:, PRODUCTS:NC], ones[:, 0:1], ALU.mult).then_inc(mean_done, 1)

            STREAMS_AFTER = {1: (0, 1), 2: (2,), 3: (3, 4)}
            pool.wait_ge(coef_step, EARLY_COEFS)
            in_turn(pool, diagonals, EARLY)
            pool.wait_ge(coef_step, LATE_COEFS)
            pool.wait_ge(late_in, 16 * (B - EARLY))
            w, x = coef[:, B - 1, :], late_row[B - 1 - EARLY]
            done = [0]

            def step(ins):
                ins.then_inc(pool_step, 1)
                done[0] += 1

            def add_stream(j):
                if j > 0:
                    pool.wait_ge(pool_step, done[0])
                for to in range(NS):
                    at = NS * to + j if j < NS else N2 + to
                    cols = slice(to * C, (to + 1) * C)
                    if j == 0:
                        step(nc.gpsimd.tensor_scalar(pool_ot[:, cols], x[:, 0:C], w[:, at:at + 1], w[:, NC - 1:NC], ALU.mult, ALU.add))
                    else:
                        step(nc.gpsimd.tensor_scalar(pool_part[:, cols], x[:, j * C:(j + 1) * C], w[:, at:at + 1], 1.0, ALU.mult, ALU.mult))
                if j > 0:
                    pool.wait_ge(pool_step, done[0])
                    step(nc.gpsimd.tensor_tensor(pool_ot[:], pool_ot[:], pool_part[:], ALU.add))

            for n in range(EARLY, by_pe.count):
                diagonals(n, n % 2, False)
                for j in STREAMS_AFTER.get(n - EARLY, ()):
                    add_stream(j)


def dft_matrices():
    t = np.arange(T, dtype=np.float64)
    f = np.arange(T // 2, dtype=np.float64)
    H = T // 2
    even = 2 * np.pi * np.outer(t, f) / T
    odd = 2 * np.pi * np.outer(t, f + 0.5) / T
    a = np.concatenate([np.cos(even), -np.sin(even)], 1)
    a[:, H] = (-1.0) ** t
    b = np.concatenate([a[:, H:], a[:, :H]], 1)
    b[:, 0] = t == T - 1
    o = np.concatenate([np.cos(odd), -np.sin(odd)], 1)
    ov = o.copy()
    ov[T - 1] -= o.sum(0)
    ovb = np.concatenate([ov[:, H:], ov[:, :H]], 1)
    c1 = 2 / T * np.concatenate([np.cos(even).T, np.cos(even).T], 0)
    c1[0] = 1 / T
    c1[H] = (-1.0) ** t / T
    c2 = 2 / T * np.concatenate([np.sin(even).T, -np.sin(even).T], 0)
    o1 = -c2 / 2
    o1[0] = 0.5
    o2 = np.concatenate([np.cos(odd).T, np.cos(odd).T], 0) / T
    o3 = np.concatenate([-np.sin(odd).T, np.sin(odd).T], 0) / T
    return np.stack([a, b, ov, ovb, o, c1 / 2, o1, o2, o3, c1, c2], 1).astype(np.float32)


def build(nc, x, ctx, wq, wk, wv, wo, w24, base, wb, gate, ident, causal, rope, dft, out):
    x1 = nc.dram_tensor("x1", [B, T, D], F32).ap()
    rows = nc.dram_tensor("rows", [B, T, ROW], F32).ap()
    attention_phase(nc, x, wq, wk, wv, wo, ident, causal, rope, x1)
    with ExitStack() as kept:
        facts = kept.enter_context(nc.sbuf_tensor("facts", [P, B, FACTS], F32))
        early_h = kept.enter_context(nc.sbuf_tensor("early_h", [P, EARLY, NS * NS], F32))
        early = Chain(nc, kept, "early", facts[:, 0:EARLY, 0:NS * NS], early_h)
        autocorrelation_phase(nc, x1, ctx, ident, dft, w24, base, wb, facts, early, rows)
        mixing_phase(nc, rows, facts, early, gate, ident, out)


def rope_tables():
    inv = (1.0 / 500000.0 ** (np.arange(0, HD, 2, dtype=np.float32) / np.float32(HD))).astype(np.float32)
    f = (np.arange(T, dtype=np.float32)[:, None] * inv[None, :]).astype(np.float64)
    c, s = np.cos(f), np.sin(f)
    cc, ss = np.concatenate([c, c], 1), np.concatenate([-s, s], 1)
    scale = 1.0 / np.sqrt(HD)
    return np.stack([cc * scale, ss * scale, cc, ss], 1).astype(np.float32)


def constants():
    eye = np.eye(P, dtype=np.float32)
    causal = np.where(np.arange(T)[None, :] > np.arange(T)[:, None], -1e30, 0.0)
    return {
        "ident": eye,
        "causal": causal.astype(np.float32),
        "rope": rope_tables(),
        "dft": dft_matrices(),
    }


_ORDER = ["x", "ctx", "wq", "wk", "wv", "wo", "w24", "base", "wb", "gate", "ident", "causal", "rope", "dft"]


def laid_out(inputs):
    w = np.concatenate([np.asarray(inputs["L0_ffn_W_" + n]) for n in ("res", "pre", "post")], 0)
    base = np.concatenate([np.asarray(inputs["L0_ffn_H_" + n + "_base"]).reshape(-1) for n in ("res", "pre", "post")])
    return {
        "x": inputs["x"], "ctx": inputs["ctx_4096"],
        "wq": inputs["L0_attn_Wq"], "wk": inputs["L0_attn_Wk"], "wv": inputs["L0_attn_Wv"], "wo": inputs["L0_attn_Wo"],
        "w24": w.T.reshape(KD, P, NLOG).transpose(1, 0, 2),
        "base": np.broadcast_to(base, (P, NLOG)),
        "wb": inputs["L0_ffn_W_branch"],
        "gate": np.broadcast_to(np.asarray(inputs["L0_ffn_gate"]), (P, 1)),
        **constants(),
    }


def kernel(**inputs):
    import concourse.bacc as bacc
    from concourse.bass_utils import run_bass_kernel_spmd

    nc = bacc.Bacc("TRN2", target_bir_lowering=False, num_devices=1)
    laid = laid_out(inputs)
    arrays, args = {}, []
    for name in _ORDER:
        a = np.ascontiguousarray(laid[name])
        arrays["in_" + name] = a
        args.append(nc.dram_tensor("in_" + name, a.shape, mybir.dt.from_np(a.dtype), kind="ExternalInput").ap())
    out = nc.dram_tensor("out", (B, T, D), F32, kind="ExternalOutput").ap()
    build(nc, *args, out)
    r = run_bass_kernel_spmd(nc, [arrays], core_ids=[0])
    return r.results[0]["out"]
```
